# Optimizing a Trainium2 kernel written in Bass

```python
import numpy as np
import jax
import jax.numpy as jnp

def _softmax(x, axis=-1):
    return jax.nn.softmax(x, axis=axis)

def _gelu(x):
    return jax.nn.gelu(x, approximate=True)

def _silu(x):
    return jax.nn.silu(x)

def _sigmoid(x):
    return jax.nn.sigmoid(x)

def _layernorm(x, axis=-1, eps=1e-05):
    m = jnp.mean(x, axis=axis, keepdims=True)
    v = jnp.var(x, axis=axis, keepdims=True)
    return (x - m) / jnp.sqrt(v + eps)

def _scatter_add(tgt, idx, src, axis=0):
    return tgt.at[idx].add(src)

def _segment_sum(src, seg, n):
    return jax.ops.segment_sum(src, seg, n)
kernel_name = 'mk_seq_preln_d2_jaxref_r8_4d0f9f'

def setup_inputs(seed: int=0):
    np.random.seed(seed)
    _w = jnp.asarray

    def _L0_attn_setup():
        import jax, jax.numpy as jnp
        import numpy as np
        import math
        NEMD = 128
        HEAD_NUM = 16
        HEAD_DIM = NEMD // HEAD_NUM
        key = jax.random.key(seed)
        k_x, k_wq, k_bq, k_wp, k_bp = jax.random.split(key, 5)
        B, T = (4, 256)
        X = jax.random.normal(k_x, (B, T, NEMD), dtype=jnp.float32)
        s1 = 1.0 / math.sqrt(NEMD)
        W_qkv = jax.random.uniform(k_wq, (NEMD, 3 * NEMD), minval=-s1, maxval=s1, dtype=jnp.float32)
        b_qkv = jax.random.uniform(k_bq, (3 * NEMD,), minval=-s1, maxval=s1, dtype=jnp.float32)
        W_proj = jax.random.uniform(k_wp, (NEMD, NEMD), minval=-s1, maxval=s1, dtype=jnp.float32)
        b_proj = jax.random.uniform(k_bp, (NEMD,), minval=-s1, maxval=s1, dtype=jnp.float32)
        return {'X': X, 'W_qkv': W_qkv, 'b_qkv': b_qkv, 'W_proj': W_proj, 'b_proj': b_proj}
    _L0_attn_in = _L0_attn_setup()

    def _L0_ffn_setup():
        import jax, jax.numpy as jnp
        import numpy as np
        B, T, D = (1, 256, 128)
        E, DFF = (8, 512)

        def _gating(logits):
            S, num_e = logits.shape
            gates = jax.nn.softmax(logits.astype(jnp.float32), axis=1)
            idx1 = jnp.argmax(gates, axis=1)
            mask1 = jax.nn.one_hot(idx1, num_e, dtype=jnp.int32)
            logits_ex1 = jnp.where(mask1.astype(bool), -jnp.inf, logits)
            idx2 = jnp.argmax(logits_ex1, axis=1)
            mask2 = jax.nn.one_hot(idx2, num_e, dtype=jnp.int32)
            loc1 = jnp.cumsum(mask1, axis=0) - 1
            loc2 = jnp.cumsum(mask2, axis=0) - 1 + jnp.sum(mask1, axis=0, keepdims=True)
            loc1_s = jnp.sum(loc1 * mask1, axis=1)
            loc2_s = jnp.sum(loc2 * mask2, axis=1)
            g1 = jnp.sum(gates * mask1, axis=1)
            g2 = jnp.sum(gates * mask2, axis=1)
            denom = jnp.maximum(g1 + g2, jnp.finfo(jnp.float32).eps)
            g1, g2 = (g1 / denom, g2 / denom)
            cap = S
            loc1_sc = jax.nn.one_hot(loc1_s, cap, dtype=jnp.float32)
            loc2_sc = jax.nn.one_hot(loc2_s, cap, dtype=jnp.float32)
            combine = (g1[:, None] * mask1)[:, :, None] * loc1_sc[:, None, :] + (g2[:, None] * mask2)[:, :, None] * loc2_sc[:, None, :]
            dispatch_mask = combine != 0
            return (combine.astype(logits.dtype), dispatch_mask)
        key = jax.random.key(seed)
        k1, k2, k3, k4 = jax.random.split(key, 4)
        x = jax.random.normal(k1, (B, T, D), dtype=jnp.float32)
        Wg = jax.random.normal(k2, (D, E), dtype=jnp.float32) * (1.0 / np.sqrt(D))
        w1 = jax.random.normal(k3, (D, DFF), dtype=jnp.float32) * (1.0 / np.sqrt(D))
        w2 = jax.random.normal(k4, (DFF, D), dtype=jnp.float32) * (1.0 / np.sqrt(DFF))
        return {'x': x, 'Wg': Wg, 'w1': w1, 'w2': w2}
    _L0_ffn_in = _L0_ffn_setup()

    def _L1_attn_setup():
        import jax, jax.numpy as jnp
        import numpy as np
        B, T, D, H, K, V, F = (4, 512, 128, 8, 128, 128, 512)
        EPS = 1e-05

        def layernorm(x, w, b):
            m = jnp.mean(x, -1, keepdims=True)
            v = jnp.var(x, -1, keepdims=True)
            return (x - m) * jax.lax.rsqrt(v + EPS) * w + b

        def l2norm(x):
            return x * jax.lax.rsqrt(jnp.sum(x * x, -1, keepdims=True) + 1e-06)

        def gdn_recurrence(q, k, v, alpha, beta):
            qT = jnp.moveaxis(q, 1, 0)
            kT = jnp.moveaxis(k, 1, 0)
            vT = jnp.moveaxis(v, 1, 0)
            aT = jnp.moveaxis(alpha, 1, 0)
            bT = jnp.moveaxis(beta, 1, 0)

            def step(S, inp):
                q_t, k_t, v_t, a_t, b_t = inp
                kS = jnp.einsum('bhk,bhkv->bhv', k_t, S)
                bk = (b_t[..., None] * k_t)[..., :, None]
                S = a_t[..., None, None] * (S - bk * kS[..., None, :]) + bk * v_t[..., None, :]
                o = jnp.einsum('bhk,bhkv->bhv', q_t, S)
                return (S, o)
            S0 = jnp.zeros((q.shape[0], H, K, V), q.dtype)
            _, oT = jax.lax.scan(step, S0, (qT, kT, vT, aT, bT))
            return jnp.moveaxis(oT, 0, 1)
        key = jax.random.key(seed)
        ks = jax.random.split(key, 12)
        s = 0.02
        return {'x': jax.random.normal(ks[0], (B, T, D), jnp.float32), 'Wq': jax.random.normal(ks[1], (D, H * K), jnp.float32) * s, 'Wk': jax.random.normal(ks[2], (D, H * K), jnp.float32) * s, 'Wv': jax.random.normal(ks[3], (D, H * V), jnp.float32) * s, 'Wb': jax.random.normal(ks[4], (D, H), jnp.float32) * s, 'Wa': jax.random.normal(ks[5], (D, H), jnp.float32) * s, 'Wo': jax.random.normal(ks[6], (H * V, D), jnp.float32) * s, 'ln1_w': jnp.ones((D,), jnp.float32), 'ln1_b': jnp.zeros((D,), jnp.float32), 'ln2_w': jnp.ones((D,), jnp.float32), 'ln2_b': jnp.zeros((D,), jnp.float32), 'W1': jax.random.normal(ks[7], (D, F), jnp.float32) * s, 'b1': jnp.zeros((F,), jnp.float32), 'W2': jax.random.normal(ks[8], (F, D), jnp.float32) * s, 'b2': jnp.zeros((D,), jnp.float32)}
    _L1_attn_in = _L1_attn_setup()

    def _L1_ffn_setup():
        import jax, jax.numpy as jnp
        import numpy as np
        D_MODEL = 128
        D_FF = 512
        N_EXPERTS = 8
        TOP_K = 2
        LN_EPS = 1e-06

        def _moe(x, router_w, w1, b1, w2, b2, gamma, beta):
            B, S, D = x.shape
            x_flat = x.reshape(-1, D)
            N = x_flat.shape[0]
            logits = x_flat @ router_w
            gate_vals, gate_idx = jax.lax.top_k(logits, TOP_K)
            gate_w = jax.nn.softmax(gate_vals, axis=-1)
            gates = jnp.zeros_like(logits).at[jnp.arange(N)[:, None], gate_idx].set(gate_w)
            h = jax.nn.gelu(jnp.einsum('nd,edf->enf', x_flat, w1) + b1[:, None, :], approximate=False)
            out = jnp.einsum('enf,efd->end', h, w2) + b2[:, None, :]
            res = x_flat[None, :, :] + out
            mu = jnp.mean(res, axis=-1, keepdims=True)
            var = jnp.mean(jnp.square(res - mu), axis=-1, keepdims=True)
            normed = (res - mu) * jax.lax.rsqrt(var + LN_EPS)
            expert_out = normed * gamma[:, None, :] + beta[:, None, :]
            y = jnp.einsum('end,ne->nd', expert_out, gates)
            return y.reshape(B, S, D)
        key = jax.random.key(seed)
        ks = jax.random.split(key, 8)
        x = jax.random.normal(ks[0], (2, 256, D_MODEL), dtype=jnp.float32)
        router_w = jax.random.normal(ks[1], (D_MODEL, N_EXPERTS), dtype=jnp.float32) * 0.02
        w1 = jax.random.normal(ks[2], (N_EXPERTS, D_MODEL, D_FF), dtype=jnp.float32) * 0.02
        b1 = jnp.zeros((N_EXPERTS, D_FF), dtype=jnp.float32)
        w2 = jax.random.normal(ks[3], (N_EXPERTS, D_FF, D_MODEL), dtype=jnp.float32) * 0.02
        b2 = jnp.zeros((N_EXPERTS, D_MODEL), dtype=jnp.float32)
        gamma = jnp.ones((N_EXPERTS, D_MODEL), dtype=jnp.float32)
        beta = jnp.zeros((N_EXPERTS, D_MODEL), dtype=jnp.float32)
        return {'x': x, 'router_w': router_w, 'w1': w1, 'b1': b1, 'w2': w2, 'b2': b2, 'gamma': gamma, 'beta': beta}
    _L1_ffn_in = _L1_ffn_setup()
    _d = {'L0_attn_X': _L0_attn_in['X'], 'L0_attn_W_qkv': _L0_attn_in['W_qkv'], 'L0_attn_b_qkv': _L0_attn_in['b_qkv'], 'L0_attn_W_proj': _L0_attn_in['W_proj'], 'L0_attn_b_proj': _L0_attn_in['b_proj'], 'L0_ffn_Wg': _L0_ffn_in['Wg'], 'L0_ffn_w1': _L0_ffn_in['w1'], 'L0_ffn_w2': _L0_ffn_in['w2'], 'L1_attn_Wq': _L1_attn_in['Wq'], 'L1_attn_Wk': _L1_attn_in['Wk'], 'L1_attn_Wv': _L1_attn_in['Wv'], 'L1_attn_Wb': _L1_attn_in['Wb'], 'L1_attn_Wa': _L1_attn_in['Wa'], 'L1_attn_Wo': _L1_attn_in['Wo'], 'L1_attn_ln1_w': _L1_attn_in['ln1_w'], 'L1_attn_ln1_b': _L1_attn_in['ln1_b'], 'L1_attn_ln2_w': _L1_attn_in['ln2_w'], 'L1_attn_ln2_b': _L1_attn_in['ln2_b'], 'L1_attn_W1': _L1_attn_in['W1'], 'L1_attn_b1': _L1_attn_in['b1'], 'L1_attn_W2': _L1_attn_in['W2'], 'L1_attn_b2': _L1_attn_in['b2'], 'L1_ffn_router_w': _L1_ffn_in['router_w'], 'L1_ffn_w1': _L1_ffn_in['w1'], 'L1_ffn_b1': _L1_ffn_in['b1'], 'L1_ffn_w2': _L1_ffn_in['w2'], 'L1_ffn_b2': _L1_ffn_in['b2'], 'L1_ffn_gamma': _L1_ffn_in['gamma'], 'L1_ffn_beta': _L1_ffn_in['beta']}
    _x0 = _d['L0_attn_X']
    _d['L0_attn_X'] = jax.random.normal(jax.random.fold_in(jax.random.key(seed), 1), (2, 1024, 128), dtype=_x0.dtype)
    del _x0
    return _d

def reference(L0_attn_X, L0_attn_W_qkv, L0_attn_b_qkv, L0_attn_W_proj, L0_attn_b_proj, L0_ffn_Wg, L0_ffn_w1, L0_ffn_w2, L1_attn_Wq, L1_attn_Wk, L1_attn_Wv, L1_attn_Wb, L1_attn_Wa, L1_attn_Wo, L1_attn_ln1_w, L1_attn_ln1_b, L1_attn_ln2_w, L1_attn_ln2_b, L1_attn_W1, L1_attn_b1, L1_attn_W2, L1_attn_b2, L1_ffn_router_w, L1_ffn_w1, L1_ffn_b1, L1_ffn_w2, L1_ffn_b2, L1_ffn_gamma, L1_ffn_beta):

    def _L0_attn_ref(X, W_qkv, b_qkv, W_proj, b_proj):
        import jax, jax.numpy as jnp
        import numpy as np
        import math
        NEMD = 128
        HEAD_NUM = 16
        HEAD_DIM = NEMD // HEAD_NUM
        B, T, C = X.shape
        qkv = X @ W_qkv + b_qkv
        q, k, v = jnp.split(qkv, 3, axis=-1)

        def to_heads(t):
            return t.reshape(B, T, HEAD_NUM, HEAD_DIM).transpose(0, 2, 1, 3)
        q, k, v = (to_heads(q), to_heads(k), to_heads(v))
        scale = 1.0 / math.sqrt(HEAD_DIM)
        scores = jnp.einsum('bhqd,bhkd->bhqk', q, k) * scale
        attn = jax.nn.softmax(scores, axis=-1)
        out = jnp.einsum('bhqk,bhkd->bhqd', attn, v)
        out = out.transpose(0, 2, 1, 3).reshape(B, T, C)
        return out @ W_proj + b_proj

    def _L0_ffn_ref(x, Wg, w1, w2):
        import jax, jax.numpy as jnp
        import numpy as np
        B, T, D = (1, 256, 128)
        E, DFF = (8, 512)

        def _gating(logits):
            S, num_e = logits.shape
            gates = jax.nn.softmax(logits.astype(jnp.float32), axis=1)
            idx1 = jnp.argmax(gates, axis=1)
            mask1 = jax.nn.one_hot(idx1, num_e, dtype=jnp.int32)
            logits_ex1 = jnp.where(mask1.astype(bool), -jnp.inf, logits)
            idx2 = jnp.argmax(logits_ex1, axis=1)
            mask2 = jax.nn.one_hot(idx2, num_e, dtype=jnp.int32)
            loc1 = jnp.cumsum(mask1, axis=0) - 1
            loc2 = jnp.cumsum(mask2, axis=0) - 1 + jnp.sum(mask1, axis=0, keepdims=True)
            loc1_s = jnp.sum(loc1 * mask1, axis=1)
            loc2_s = jnp.sum(loc2 * mask2, axis=1)
            g1 = jnp.sum(gates * mask1, axis=1)
            g2 = jnp.sum(gates * mask2, axis=1)
            denom = jnp.maximum(g1 + g2, jnp.finfo(jnp.float32).eps)
            g1, g2 = (g1 / denom, g2 / denom)
            cap = S
            loc1_sc = jax.nn.one_hot(loc1_s, cap, dtype=jnp.float32)
            loc2_sc = jax.nn.one_hot(loc2_s, cap, dtype=jnp.float32)
            combine = (g1[:, None] * mask1)[:, :, None] * loc1_sc[:, None, :] + (g2[:, None] * mask2)[:, :, None] * loc2_sc[:, None, :]
            dispatch_mask = combine != 0
            return (combine.astype(logits.dtype), dispatch_mask)
        d_model = x.shape[2]
        xs = x.reshape(-1, d_model)
        logits = xs @ Wg
        combine, dispatch_mask = _gating(logits)
        dispatched = jnp.einsum('sec,sm->ecm', dispatch_mask.astype(jnp.float32), xs)
        expert_out = jax.nn.relu(dispatched @ w1) @ w2
        out = jnp.einsum('sec,ecm->sm', combine, expert_out)
        return out.reshape(x.shape)

    def _L1_attn_ref(x, Wq, Wk, Wv, Wb, Wa, Wo, ln1_w, ln1_b, ln2_w, ln2_b, W1, b1, W2, b2):
        import jax, jax.numpy as jnp
        import numpy as np
        B, T, D, H, K, V, F = (4, 512, 128, 8, 128, 128, 512)
        EPS = 1e-05

        def layernorm(x, w, b):
            m = jnp.mean(x, -1, keepdims=True)
            v = jnp.var(x, -1, keepdims=True)
            return (x - m) * jax.lax.rsqrt(v + EPS) * w + b

        def l2norm(x):
            return x * jax.lax.rsqrt(jnp.sum(x * x, -1, keepdims=True) + 1e-06)

        def gdn_recurrence(q, k, v, alpha, beta):
            qT = jnp.moveaxis(q, 1, 0)
            kT = jnp.moveaxis(k, 1, 0)
            vT = jnp.moveaxis(v, 1, 0)
            aT = jnp.moveaxis(alpha, 1, 0)
            bT = jnp.moveaxis(beta, 1, 0)

            def step(S, inp):
                q_t, k_t, v_t, a_t, b_t = inp
                kS = jnp.einsum('bhk,bhkv->bhv', k_t, S)
                bk = (b_t[..., None] * k_t)[..., :, None]
                S = a_t[..., None, None] * (S - bk * kS[..., None, :]) + bk * v_t[..., None, :]
                o = jnp.einsum('bhk,bhkv->bhv', q_t, S)
                return (S, o)
            S0 = jnp.zeros((q.shape[0], H, K, V), q.dtype)
            _, oT = jax.lax.scan(step, S0, (qT, kT, vT, aT, bT))
            return jnp.moveaxis(oT, 0, 1)
        b, t, _ = x.shape
        n = layernorm(x, ln1_w, ln1_b)
        q = l2norm(jax.nn.silu(n @ Wq).reshape(b, t, H, K))
        k = l2norm(jax.nn.silu(n @ Wk).reshape(b, t, H, K))
        v = jax.nn.silu(n @ Wv).reshape(b, t, H, V)
        beta = jax.nn.sigmoid(n @ Wb)
        alpha = jax.nn.sigmoid(n @ Wa)
        o = gdn_recurrence(q, k, v, alpha, beta).reshape(b, t, H * V) @ Wo
        x = x + o
        h = layernorm(x, ln2_w, ln2_b)
        x = x + (jax.nn.gelu(h @ W1 + b1, approximate=False) @ W2 + b2)
        return x

    def _L1_ffn_ref(x, router_w, w1, b1, w2, b2, gamma, beta):
        import jax, jax.numpy as jnp
        import numpy as np
        D_MODEL = 128
        D_FF = 512
        N_EXPERTS = 8
        TOP_K = 2
        LN_EPS = 1e-06

        def _moe(x, router_w, w1, b1, w2, b2, gamma, beta):
            B, S, D = x.shape
            x_flat = x.reshape(-1, D)
            N = x_flat.shape[0]
            logits = x_flat @ router_w
            gate_vals, gate_idx = jax.lax.top_k(logits, TOP_K)
            gate_w = jax.nn.softmax(gate_vals, axis=-1)
            gates = jnp.zeros_like(logits).at[jnp.arange(N)[:, None], gate_idx].set(gate_w)
            h = jax.nn.gelu(jnp.einsum('nd,edf->enf', x_flat, w1) + b1[:, None, :], approximate=False)
            out = jnp.einsum('enf,efd->end', h, w2) + b2[:, None, :]
            res = x_flat[None, :, :] + out
            mu = jnp.mean(res, axis=-1, keepdims=True)
            var = jnp.mean(jnp.square(res - mu), axis=-1, keepdims=True)
            normed = (res - mu) * jax.lax.rsqrt(var + LN_EPS)
            expert_out = normed * gamma[:, None, :] + beta[:, None, :]
            y = jnp.einsum('end,ne->nd', expert_out, gates)
            return y.reshape(B, S, D)
        return _moe(x, router_w, w1, b1, w2, b2, gamma, beta)
    x = L0_attn_X
    x = x + _L0_attn_ref(_layernorm(x, axis=-1), L0_attn_W_qkv, L0_attn_b_qkv, L0_attn_W_proj, L0_attn_b_proj)
    x = x + _L0_ffn_ref(_layernorm(x, axis=-1), L0_ffn_Wg, L0_ffn_w1, L0_ffn_w2)
    x = x + _L1_attn_ref(_layernorm(x, axis=-1), L1_attn_Wq, L1_attn_Wk, L1_attn_Wv, L1_attn_Wb, L1_attn_Wa, L1_attn_Wo, L1_attn_ln1_w, L1_attn_ln1_b, L1_attn_ln2_w, L1_attn_ln2_b, L1_attn_W1, L1_attn_b1, L1_attn_W2, L1_attn_b2)
    x = x + _L1_ffn_ref(_layernorm(x, axis=-1), L1_ffn_router_w, L1_ffn_w1, L1_ffn_b1, L1_ffn_w2, L1_ffn_b2, L1_ffn_gamma, L1_ffn_beta)
    return x

_drawn_inputs = setup_inputs


def setup_inputs(seed=0):
    import zlib

    import numpy as np

    out = dict(_drawn_inputs(seed))
    spreads = {'L1_attn_ln1_w': (1.0, 0.6),
     'L1_attn_ln1_b': (0.0, 0.8),
     'L1_attn_ln2_w': (1.0, 0.6),
     'L1_attn_ln2_b': (0.0, 0.8),
     'L1_attn_b1': (0.0, 0.625),
     'L1_attn_b2': (0.0, 0.1),
     'L1_ffn_b1': (0.0, 0.8),
     'L1_ffn_b2': (0.0, 0.358),
     'L1_ffn_gamma': (1.0, 0.2),
     'L1_ffn_beta': (0.0, 0.385)}
    factors = {'L0_attn_W_qkv': 3.394,
     'L0_ffn_Wg': 8.0,
     'L1_attn_Wq': 8.0,
     'L1_attn_Wk': 8.0,
     'L1_attn_Wv': 8.0,
     'L1_attn_Wb': 8.0,
     'L1_attn_Wa': 8.0,
     'L1_attn_Wo': 8.0,
     'L1_ffn_w1': 4.802,
     'L1_ffn_w2': 4.263}
    for name, (base, spread) in spreads.items():
        noise = np.random.default_rng([zlib.crc32(name.encode()), seed]).standard_normal(out[name].shape)
        drawn = base * np.exp(spread * noise) if base else spread * noise
        out[name] = jnp.asarray(drawn.astype(out[name].dtype))
    for name, factor in factors.items():
        out[name] = (out[name] * factor).astype(out[name].dtype)
    return out
```

```python
from contextlib import ExitStack

import numpy as np

import concourse.bass as bass
from concourse import mybir

F32 = mybir.dt.float32
BF16 = mybir.dt.bfloat16
ALU = mybir.AluOpType
ACT = mybir.ActivationFunctionType
AX_X = mybir.AxisListType.X

P = 128
D = 128
BATCH, SEQ = 2, 1024
TILES = BATCH * SEQ // P
SEQ_TILES = SEQ // P
BLOCKS = 4
BLK = 512
FFN = 512
EXPERTS = 8

HEADS0, HDIM0 = 16, 8
SCALE0 = float(HDIM0) ** -0.5
PARTS = 3
PAIRS = [(a, b) for a in range(PARTS) for b in range(PARTS)]
MAX_ROW = len(PAIRS) * HDIM0
STACK = 96

HEADS1 = 8
GROUP = 4
LEVELS = [2, 4, 8, 16, 32, 64]
NEG = -1.0e30


def shape_constants():
    i = np.arange(P)
    ident = np.eye(P, dtype=np.float32)
    upper = (i[:, None] <= i[None, :]).astype(np.float32)
    below = np.where(i[:, None] <= i[None, :], 0.0, NEG).astype(np.float32)
    pair = ((i[:, None] // 2 == i[None, :] // 2) & (i[:, None] > i[None, :])).astype(np.float32)
    masks = []
    for s in LEVELS:
        odd = (i.reshape(-1, 2, s)[:, 1, :]).reshape(-1)
        masks.append(((i[:, None] // s + 1) == (odd[None, :] // s)).astype(np.float32))
    iota = np.tile(np.arange(EXPERTS, dtype=np.float32), (P, 1))
    return {
        "ident": ident, "upper": upper, "below": below, "pair": pair,
        "levels": np.concatenate(masks, axis=1), "iota": iota,
    }


class Core:

    def __init__(self, nc, ctx):
        self.nc, self.ctx = nc, ctx
        self.x = self.sb("x", [P, TILES, D])
        self.n = self.sb("n", [P, TILES, D])
        self.nT = self.sb("nT", [D, TILES * P])
        self.ident = self.sb("ident", [P, P])
        self.iota = self.sb("iota", [P, EXPERTS])
        self.norm_sems = [self.sem(f"norm_{s}") for s in (
            "stats_done", "moments_done", "shifted_done", "rstd_done", "normed", "turned_done", "kept")]
        self.norms = self.turned_norms = 0
        self.half = self.sb("half", [P, TILES])
        self.moved = self.sem("moved")
        self.chain, self.linked = self.sem("chain"), 0

    def link(self, dve, ins):
        self.linked += 1
        ins.then_inc(self.chain, 1)
        dve.wait_ge(self.chain, self.linked)

    def sb(self, name, shape, dt=F32, ctx=None):
        return (ctx or self.ctx).enter_context(self.nc.sbuf_tensor(name, shape, dt))

    def ps(self, name, shape, dt=F32, ctx=None):
        return (ctx or self.ctx).enter_context(self.nc.psum_tensor(name, shape, dt))

    def sem(self, name):
        return self.ctx.enter_context(self.nc.semaphore(name))


def layer_norm(k, tag, src, eps, tokens_out, turned_out=None, weight=None, bias=None):
    nc = k.nc
    with ExitStack() as ctx:
        stats = k.sb(f"{tag}_stats", [P, TILES, 6], ctx=ctx)
        moments = k.sb(f"{tag}_moments", [P, TILES, 2], ctx=ctx)
        shifted = k.sb(f"{tag}_shifted", [P, TILES], ctx=ctx)
        rstd = k.sb(f"{tag}_rstd", [P, TILES], ctx=ctx)
        turned = k.ps(f"{tag}_turned", [P, BLOCKS, BLK], ctx=ctx)
        stats_done, moments_done, shifted_done, rstd_done, normed, turned_done, kept = k.norm_sems
        n, m = k.norms, k.turned_norms
        k.norms, k.turned_norms = n + 1, m + (turned_out is not None)
        block = ctx.enter_context(nc.Block())

        @block.vector
        def _(dve):
            with dve.Fori(0, TILES) as i:
                nc.vector.bn_stats(stats[:, i, :], src[:, i, :]).then_inc(stats_done, 1)
            for i in range(TILES):
                dve.wait_ge(stats_done, n * TILES + i + 1)
                nc.vector.bn_aggr(moments[:, i, :], stats[:, i, :]).then_inc(moments_done, 1)
            dve.wait_ge(moments_done, (n + 1) * TILES)
            nc.vector.tensor_scalar(shifted[:], moments[:, :, 1], eps, None, ALU.add).then_inc(shifted_done, 1)
            dve.wait_ge(rstd_done, n + 1)
            with dve.Fori(0, TILES) as i:
                nc.vector.tensor_scalar(tokens_out[:, i, :], src[:, i, :], moments[:, i, 0:1], rstd[:, bass.ds(i, 1)],
                                        ALU.subtract, ALU.mult).then_inc(normed, 1)
            dve.wait_ge(normed, (n + 1) * TILES)

        @block.gpsimd
        def _(pool):
            pool.wait_ge(shifted_done, n + 1)
            nc.gpsimd.tensor_tensor(rstd[:], shifted[:], k.half[:], ALU.pow).then_inc(rstd_done, 1)

        if turned_out is None:
            return

        @block.tensor
        def _(pe):
            for t in range(TILES):
                pe.wait_ge(normed, n * TILES + t + 1)
                mm = nc.tensor.transpose(turned[:, t // 4, (t % 4) * P:(t % 4 + 1) * P], tokens_out[:, t, :], k.ident[:])
                if t % 4 == 3:
                    mm.then_inc(turned_done, 1)

        @block.scalar
        def _(act):
            with act.Fori(0, BLOCKS) as blk:
                act.wait_ge(turned_done, m * BLOCKS + blk + 1)
                nc.scalar.activation(
                    turned_out[:, bass.ds(blk * BLK, BLK)], turned[:, blk, :], ACT.Identity,
                    bias=0.0 if bias is None else bias[:], scale=1.0 if weight is None else weight[:],
                ).then_inc(kept, 1)
            act.wait_ge(kept, (m + 1) * BLOCKS)


def start(k, a):
    nc = k.nc
    loaded, half_set = k.moved, k.sem("start_half_set")
    with nc.Block() as block:
        @block.sync
        def _(sp):
            sp.dma_start(k.x[:], a["L0_attn_X"].rearrange("b (t p) d -> p (b t) d", p=P)).then_inc(loaded, 16)
            sp.dma_start(k.ident[:], a["ident"]).then_inc(loaded, 16)
            sp.dma_start(k.iota[:], a["iota"]).then_inc(loaded, 16)
            sp.wait_ge(loaded, 48)

        @block.gpsimd
        def _(pool):
            nc.gpsimd.memset(k.half[:], -0.5).then_inc(half_set, 1)
            pool.wait_ge(half_set, 1)


def attention(k, a):
    nc = k.nc
    KB = SEQ_TILES
    PAIRS_BH = BATCH * HEADS0
    VW = 32
    parts_dram = nc.dram_tensor("parts_dram", [2, PARTS, D, BATCH * SEQ], BF16)
    max_dram = nc.dram_tensor("max_dram", [PAIRS_BH, PARTS * KB, P], BF16)

    with ExitStack() as outer:
        stack = {w: k.sb(f"{w}_stack", [STACK, PAIRS_BH, SEQ], BF16, outer) for w in "qk"}
        v_all = k.sb("v_all", [P, PAIRS_BH, KB, HDIM0], ctx=outer)
        identb = k.sb("identb", [P, P], BF16, outer)

        with ExitStack() as ctx:
            w_qkv = k.sb("w_qkv", [D, 3 * D], ctx=ctx)
            b_col = k.sb("b_col", [D, 2], ctx=ctx)
            b_v = k.sb("b_v", [P, D], ctx=ctx)
            full = k.sb("full", [D, 2, BLK], ctx=ctx)
            rest = k.sb("rest", [D, 2, BLK], ctx=ctx)
            cut = k.sb("cut", [D, 2, PARTS, BLK], BF16, ctx)
            by_feature = k.ps("by_feature", [D, 2, BLK], ctx=ctx)
            v_psum = k.ps("v_psum", [P, 2, BLK], ctx=ctx)
            w_in, rows_set, projected, biased = (k.sem(f"qkv_{s}") for s in ("w_in", "rows_set", "projected", "biased"))
            cut1, rest1, cut2, rest2 = (k.sem(f"qkv_{s}") for s in ("cut1", "rest1", "cut2", "rest2"))
            saved = [k.sem(f"qkv_saved{i}") for i in range(2)]
            v_done, v_kept, stacked, identb_set = (k.sem(f"qkv_{s}") for s in ("v_done", "v_kept", "stacked", "identb_set"))
            block = ctx.enter_context(nc.Block())

            @block.sync
            def _(sp):
                sp.dma_start(w_qkv[:], a["L0_attn_W_qkv"]).then_inc(w_in, 16)
                sp.dma_start(b_col[:], a["L0_attn_b_qkv"].rearrange("(w d) -> d w", d=D)[:, 0:2],
                             allow_slow_non_contiguous=True).then_inc(w_in, 16)
                sp.dma_start(b_v[:], a["L0_attn_b_qkv"][2 * D:3 * D].partition_broadcast(P)).then_inc(w_in, 16)
                for step in range(2 * BLOCKS):
                    n = step % BLOCKS
                    sp.wait_ge(rest2, step + 1)
                    sp.dma_start(parts_dram[step // BLOCKS, :, :, n * BLK:(n + 1) * BLK].rearrange("s d t -> d s t"),
                                 cut[:, step % 2, :, :]).then_inc(saved[step % 2], 16)
                for par in range(2):
                    sp.wait_ge(saved[par], 16 * BLOCKS)
                for s, (pq, pk) in enumerate(PAIRS):
                    for w, part in (("q", pq), ("k", pk)):
                        if (s + 1) * HDIM0 > 64:
                            sp.wait_ge(rows_set, 2)
                        for b in range(BATCH):
                            sp.dma_start(
                                stack[w][s * HDIM0:(s + 1) * HDIM0, b * HEADS0:(b + 1) * HEADS0, :],
                                parts_dram["qk".index(w), part, :, b * SEQ:(b + 1) * SEQ].rearrange(
                                    "(h d) t -> d h t", d=HDIM0)).then_inc(stacked, 16)
                sp.wait_ge(stacked, 16 * 4 * len(PAIRS))

            @block.gpsimd
            def _(pool):
                nc.gpsimd.memset(stack["q"][64:STACK], 0.0).then_inc(rows_set, 1)
                nc.gpsimd.memset(stack["k"][64:STACK], 1.0).then_inc(rows_set, 1)
                pool.wait_ge(rows_set, 2)
                nc.gpsimd.tensor_copy(identb[:], k.ident[:]).then_inc(identb_set, 1)
                pool.wait_ge(identb_set, 1)

            @block.tensor
            def _(pe):
                pe.wait_ge(w_in, 48)
                for w in range(2):
                    for n in range(BLOCKS):
                        step = w * BLOCKS + n
                        if step >= 2:
                            pe.wait_ge(biased, step - 1)
                        nc.tensor.matmul(by_feature[:, step % 2, :], w_qkv[:, w * D:(w + 1) * D],
                                         k.nT[:, n * BLK:(n + 1) * BLK], start=True, stop=True).then_inc(projected, 1)
                for t in range(TILES):
                    if t % 4 == 0 and t >= 8:
                        pe.wait_ge(v_kept, t // 4 - 1)
                    mm = nc.tensor.matmul(v_psum[:, (t // 4) % 2, (t % 4) * D:(t % 4 + 1) * D],
                                          k.nT[:, t * P:(t + 1) * P], w_qkv[:, 2 * D:3 * D], start=True, stop=True)
                    if t % 4 == 3:
                        mm.then_inc(v_done, 1)

            @block.scalar
            def _(act):
                act.wait_ge(w_in, 48)
                for step in range(2 * BLOCKS):
                    act.wait_ge(projected, step + 1)
                    if step >= 2:
                        act.wait_ge(rest1, step - 1)
                    nc.scalar.activation(full[:, step % 2, :], by_feature[:, step % 2, :], ACT.Identity,
                                         bias=b_col[:, step // BLOCKS:step // BLOCKS + 1]).then_inc(biased, 1)

            @block.vector
            def _(dve):
                for step in range(2 * BLOCKS):
                    par = step % 2
                    dve.wait_ge(biased, step + 1)
                    if step >= 2:
                        dve.wait_ge(saved[par], 16 * (step // 2))
                    nc.vector.tensor_copy(cut[:, par, 0, :], full[:, par, :]).then_inc(cut1, 1)
                    dve.wait_ge(cut1, step + 1)
                    nc.vector.tensor_tensor(rest[:, par, :], full[:, par, :], cut[:, par, 0, :], ALU.subtract).then_inc(rest1, 1)
                    dve.wait_ge(rest1, step + 1)
                    nc.vector.tensor_copy(cut[:, par, 1, :], rest[:, par, :]).then_inc(cut2, 1)
                    dve.wait_ge(cut2, step + 1)
                    nc.vector.tensor_tensor(cut[:, par, 2, :], rest[:, par, :], cut[:, par, 1, :], ALU.subtract).then_inc(rest2, 1)
                for n in range(BLOCKS):
                    dve.wait_ge(v_done, n + 1)
                    dve.wait_ge(w_in, 48)
                    b, kb = n // 2, 4 * (n % 2)
                    for t in range(4):
                        last = nc.vector.tensor_tensor(
                            v_all[:, b * HEADS0:(b + 1) * HEADS0, kb + t, :],
                            v_psum[:, n % 2, t * D:(t + 1) * D].rearrange("p (h d) -> p h d", h=HEADS0),
                            b_v[:].rearrange("p (h d) -> p h d", h=HEADS0), ALU.add)
                    last.then_inc(v_kept, 1)
                dve.wait_ge(v_kept, BLOCKS)

        heads = k.sb("heads", [P, KB, PAIRS_BH, HDIM0], ctx=outer)
        with ExitStack() as ctx:
            v_head = k.sb("v_head", [P, 2, KB, VW], ctx=ctx)
            row_min = k.sb("row_min", [P, 2, KB, 2], ctx=ctx)
            neg_max = k.sb("neg_max", [P, 2, KB], ctx=ctx)
            zeros = k.sb("zeros", [P, KB * HDIM0], ctx=ctx)
            max_rest = k.sb("max_rest", [P, 2, KB], ctx=ctx)
            max_cut = k.sb("max_cut", [P, 2, PARTS, KB], BF16, ctx)
            max_rows = k.sb("max_rows", [PARTS * KB, 2, P], BF16, ctx)
            probs = k.sb("probs", [P, 2, SEQ], ctx=ctx)
            sums = k.sb("sums", [P, 2, 2 * P], ctx=ctx)
            recip = k.sb("recip", [P, 2, 2, 4], ctx=ctx)
            first = k.ps("first", [P, 2, BLK], ctx=ctx)
            scores = k.ps("scores", [P, 2, SEQ], ctx=ctx)
            summed = k.ps("summed", [P, BLK], ctx=ctx)
            turn = k.ps("turn", [P, BLK], ctx=ctx)
            turn_b = turn[:].bitcast(BF16)
            turn_q = turn[:, 0:2 * P].rearrange("p (half c w) -> p half c w", half=2, c=4)
            (first_ready, first_read, joined, m1, r1, m2, r2, m3, rows_turned, rows_kept, rows_out, rows_in, v_zeroed, v_ready,
             scores_ready, probs_ready, probs_used, sums_kept, sums_turned, recip_done, head_done) = (
                k.sem(f"att_{s}") for s in (
                    "first_ready", "first_read", "joined", "m1", "r1", "m2", "r2", "m3", "rows_turned", "rows_kept",
                    "rows_out", "rows_in", "v_zeroed", "v_ready", "scores_ready", "probs_ready", "probs_used",
                    "sums_kept", "sums_turned", "recip_done", "head_done"))
            block = ctx.enter_context(nc.Block())
            LOOPS = PAIRS_BH // 2

            def over_heads(eng, step):
                step(0, True)
                with eng.Fori(1, LOOPS - 1) as r:
                    step(r, True)
                step(LOOPS - 1, False)

            @block.tensor
            def _(pe):
                def find_max(j, t):
                    for half in range(2):
                        n = 2 * (KB * j + t) + half
                        if not (isinstance(n, int) and n < 2):
                            pe.wait_ge(first_read, n - 1)
                        nc.tensor.matmul(first[:, half, :], stack["q"][:, j, t * P:(t + 1) * P],
                                         stack["k"][:, j, half * BLK:(half + 1) * BLK],
                                         start=True, stop=True).then_inc(first_ready, 1)

                def turn_max(j, par):
                    pe.wait_ge(m3, j + 1)
                    if not (isinstance(j, int) and j < 3):
                        pe.wait_ge(head_done, j - 2)
                    if not (isinstance(j, int) and j < 1):
                        pe.wait_ge(rows_kept, j)
                    nc.tensor.transpose(turn_b[0:PARTS * KB, 0:P], max_cut[:, par].rearrange("p s t -> p (s t)"),
                                        identb[:]).then_inc(rows_turned, 1)

                def scores_of(i, kb):
                    n = KB * i + kb
                    if not (isinstance(n, int) and n < 2):
                        pe.wait_ge(probs_ready, n - 1)
                    for half in range(2):
                        mm = nc.tensor.matmul(scores[:, kb % 2, half * BLK:(half + 1) * BLK],
                                              stack["k"][:, i, kb * P:(kb + 1) * P],
                                              stack["q"][:, i, half * BLK:(half + 1) * BLK], start=True, stop=True)
                    mm.then_inc(scores_ready, 1)

                def sum_values(i, par, kb):
                    if kb == 0:
                        pe.wait_ge(v_ready, i + 1)
                        if not (isinstance(i, int) and i < 1):
                            pe.wait_ge(sums_kept, i)
                    pe.wait_ge(probs_ready, KB * i + kb + 1)
                    for c in range(4):
                        mm = nc.tensor.matmul(summed[VW * c:VW * (c + 1), 0:2 * P], v_head[:, par, kb, :],
                                              probs[:, kb % 2, c * 2 * P:(c + 1) * 2 * P],
                                              start=(kb == 0), stop=(kb == KB - 1))
                    mm.then_inc(probs_used, 1)

                def turn_sums(i, par, rows):
                    pe.wait_ge(sums_kept, i + 1)
                    pe.wait_ge(rows_kept, rows)
                    if not (isinstance(i, int) and i < 1):
                        pe.wait_ge(head_done, i)
                    for half in range(2):
                        mm = nc.tensor.transpose(turn[:, half * P:(half + 1) * P], sums[:, par, half * P:(half + 1) * P],
                                                 k.ident[:])
                    mm.then_inc(sums_turned, 1)

                def step(r, ahead):
                    for par in range(2):
                        i = 2 * r + par
                        pe.wait_ge(rows_in, 16 * i + 16)
                        for kb in range(KB):
                            if ahead:
                                find_max(i + 2, kb)
                            scores_of(i, kb)
                            if kb >= 1:
                                sum_values(i, par, kb - 1)
                            if kb == 1 and (ahead or par == 0):
                                turn_max(i + 1, 1 - par)
                            if kb == 3 and not (isinstance(i, int) and i == 0):
                                turn_sums(i - 1, 1 - par, i + 2 if (ahead or par == 0) else PAIRS_BH)
                        sum_values(i, par, KB - 1)

                for j in range(2):
                    for t in range(KB):
                        find_max(j, t)
                turn_max(0, 0)
                over_heads(pe, step)
                turn_sums(PAIRS_BH - 1, 1, PAIRS_BH)

            @block.vector
            def _(dve):
                def find_max(j, par, t):
                    if t == 0 and not (isinstance(j, int) and j < 2):
                        dve.wait_ge(joined, j - 1)
                    for half in range(2):
                        dve.wait_ge(first_ready, 2 * (KB * j + t) + half + 1)
                        nc.vector.tensor_reduce(row_min[:, par, t, half:half + 1], first[:, half, :], AX_X, ALU.max,
                                                negate=True).then_inc(first_read, 1)

                def join(j, par):
                    dve.wait_ge(first_read, 2 * KB * (j + 1))
                    if not (isinstance(j, int) and j < 2):
                        dve.wait_ge(m3, j - 1)
                    nc.vector.tensor_reduce(neg_max[:, par, :], row_min[:, par], AX_X, ALU.min).then_inc(joined, 1)

                def keep_rows(j, par):
                    dve.wait_ge(rows_turned, j + 1)
                    if not (isinstance(j, int) and j < 2):
                        dve.wait_ge(rows_out, 16 * j - 16)
                    nc.vector.tensor_copy(max_rows[:, par, :], turn_b[0:PARTS * KB, 0:P]).then_inc(rows_kept, 1)

                def divide(i, par):
                    dve.wait_ge(sums_turned, i + 1)
                    if not (isinstance(i, int) and i < 2):
                        dve.wait_ge(head_done, i - 1)
                    nc.vector.reciprocal(recip[:, par], turn_q[:, :, :, HDIM0]).then_inc(recip_done, 1)
                    dve.wait_ge(recip_done, i + 1)
                    nc.vector.tensor_tensor(
                        heads[:, :, i, :].rearrange("p (c half) d -> p half c d", half=2), turn_q[:, :, :, 0:HDIM0],
                        recip[:, par].unsqueeze(3).broadcast_to([P, 2, 4, HDIM0]), ALU.mult).then_inc(head_done, 1)

                def step(r, ahead):
                    for par in range(2):
                        i = 2 * r + par
                        for kb in range(KB):
                            if ahead:
                                find_max(i + 2, par, kb)
                            if kb == 2 and (ahead or par == 0):
                                keep_rows(i + 1, 1 - par)
                            if kb == 5 and not (isinstance(i, int) and i == 0):
                                divide(i - 1, 1 - par)
                        if ahead:
                            join(i + 2, par)

                for j in range(2):
                    for t in range(KB):
                        find_max(j, j, t)
                    join(j, j)
                keep_rows(0, 0)
                over_heads(dve, step)
                divide(PAIRS_BH - 1, 1)
                dve.wait_ge(head_done, PAIRS_BH)

            @block.scalar
            def _(act):
                def keep_sums(i, par):
                    act.wait_ge(probs_used, KB * (i + 1))
                    if not (isinstance(i, int) and i < 2):
                        act.wait_ge(sums_turned, i - 1)
                    nc.scalar.copy(sums[:, par, :], summed[:, 0:2 * P]).then_inc(sums_kept, 1)

                def rows_to_dram(j, par):
                    act.wait_ge(rows_kept, j + 1)
                    act.dma_start(max_dram[j], max_rows[:, par, :]).then_inc(rows_out, 16)

                def rows_to_stack(j):
                    act.wait_ge(rows_out, 16 * j + 16)
                    if not (isinstance(j, int) and j < 1):
                        act.wait_ge(rows_in, 16 * j)
                    act.dma_start(stack["q"][MAX_ROW:MAX_ROW + PARTS, j, :],
                                  max_dram[j].rearrange("(s t) q -> s (t q)", s=PARTS)).then_inc(rows_in, 16)

                def step(r, ahead):
                    for par in range(2):
                        i = 2 * r + par
                        for kb in range(KB):
                            if kb == 3 and (ahead or par == 0):
                                rows_to_dram(i + 1, 1 - par)
                            if kb == 5 and (ahead or par == 0):
                                rows_to_stack(i + 1)
                            n = KB * i + kb
                            act.wait_ge(scores_ready, n + 1)
                            if not (isinstance(n, int) and n < 2):
                                act.wait_ge(probs_used, n - 1)
                            nc.scalar.activation(probs[:, kb % 2, :], scores[:, kb % 2, :], ACT.Exp,
                                                 scale=SCALE0).then_inc(probs_ready, 1)
                            if kb == 0 and not (isinstance(i, int) and i == 0):
                                keep_sums(i - 1, 1 - par)

                rows_to_dram(0, 0)
                rows_to_stack(0)
                over_heads(act, step)
                keep_sums(PAIRS_BH - 1, 1)

            @block.gpsimd
            def _(pool):
                def cut_max(j, par):
                    pool.wait_ge(joined, j + 1)
                    if not (isinstance(j, int) and j < 2):
                        pool.wait_ge(rows_turned, j - 1)
                    nc.gpsimd.tensor_tensor(max_cut[:, par, 0, :], neg_max[:, par, :], zeros[:, 0:KB], ALU.add).then_inc(m1, 1)
                    pool.wait_ge(m1, j + 1)
                    nc.gpsimd.tensor_tensor(max_rest[:, par, :], neg_max[:, par, :], max_cut[:, par, 0, :],
                                            ALU.subtract).then_inc(r1, 1)
                    pool.wait_ge(r1, j + 1)
                    nc.gpsimd.tensor_tensor(max_cut[:, par, 1, :], max_rest[:, par, :], zeros[:, 0:KB], ALU.add).then_inc(m2, 1)
                    pool.wait_ge(m2, j + 1)
                    nc.gpsimd.tensor_tensor(max_cut[:, par, 2, :], max_rest[:, par, :], max_cut[:, par, 1, :],
                                            ALU.subtract).then_inc(m3, 1)

                def take_values(i, par):
                    if not (isinstance(i, int) and i < 2):
                        pool.wait_ge(probs_used, KB * (i - 1))
                    nc.gpsimd.tensor_tensor(v_head[:, par, :, 0:HDIM0], v_all[:, i],
                                            zeros[:].rearrange("p (t d) -> p t d", t=KB), ALU.add).then_inc(v_ready, 1)

                def step(r, ahead):
                    for par in range(2):
                        i = 2 * r + par
                        take_values(i, par)
                        if ahead:
                            cut_max(i + 2, par)

                nc.gpsimd.memset(v_head[:], 0.0).then_inc(v_zeroed, 1)
                pool.wait_ge(v_zeroed, 1)
                nc.gpsimd.memset(v_head[:, :, :, HDIM0:HDIM0 + 1], 1.0).then_inc(v_zeroed, 1)
                nc.gpsimd.memset(zeros[:], 0.0).then_inc(v_zeroed, 1)
                pool.wait_ge(v_zeroed, 3)
                for j in range(2):
                    cut_max(j, j)
                over_heads(pool, step)

        with ExitStack() as ctx:
            w_proj = k.sb("w_proj", [D, D], ctx=ctx)
            b_proj = k.sb("b_proj", [P, D], ctx=ctx)
            heads_T = k.sb("heads_T", [P, TILES, P], ctx=ctx)
            turned = k.ps("proj_turned", [P, 4, BLK], ctx=ctx)
            out = k.ps("proj_out", [P, 4, BLK], ctx=ctx)
            w_in, turned_done, kept, out_done, bias_added, done = (
                k.sem(f"proj_{s}") for s in ("w_in", "turned_done", "kept", "out_done", "bias_added", "done"))
            block = ctx.enter_context(nc.Block())

            @block.sync
            def _(sp):
                sp.dma_start(w_proj[:], a["L0_attn_W_proj"]).then_inc(w_in, 16)
                sp.dma_start(b_proj[:], a["L0_attn_b_proj"].partition_broadcast(P)).then_inc(w_in, 16)

            @block.tensor
            def _(pe):
                for t in range(TILES):
                    b, kb = t // KB, t % KB
                    mm = nc.tensor.transpose(turned[:, t // 4, (t % 4) * P:(t % 4 + 1) * P],
                                             heads[:, kb, b * HEADS0:(b + 1) * HEADS0, :], k.ident[:])
                    if t % 4 == 3:
                        mm.then_inc(turned_done, 1)
                pe.wait_ge(w_in, 32)
                for t in range(TILES):
                    pe.wait_ge(kept, t // 4 + 1)
                    mm = nc.tensor.matmul(out[:, t // 4, (t % 4) * P:(t % 4 + 1) * P], heads_T[:, t, :], w_proj[:],
                                          start=True, stop=True)
                    if t % 4 == 3:
                        mm.then_inc(out_done, 1)

            @block.scalar
            def _(act):
                for n in range(BLOCKS):
                    act.wait_ge(turned_done, n + 1)
                    nc.scalar.copy(heads_T[:, 4 * n:4 * n + 4, :], turned[:, n, :].rearrange("p (t q) -> p t q", t=4)).then_inc(kept, 1)

            @block.vector
            def _(dve):
                dve.wait_ge(w_in, 32)
                nc.vector.tensor_tensor(k.x[:], k.x[:], b_proj[:].unsqueeze(1).broadcast_to([P, TILES, D]),
                                        ALU.add).then_inc(bias_added, 1)
                dve.wait_ge(bias_added, 1)
                for n in range(BLOCKS):
                    dve.wait_ge(out_done, n + 1)
                    nc.vector.tensor_tensor(k.x[:, 4 * n:4 * n + 4, :], out[:, n, :].rearrange("p (t d) -> p t d", t=4),
                                            k.x[:, 4 * n:4 * n + 4, :], ALU.add).then_inc(done, 1)
                dve.wait_ge(done, BLOCKS)


def feed_forward(k, tag, loads, loads_per, experts, func, has_bias, finish):
    nc = k.nc
    FC = FFN // P
    with ExitStack() as ctx:
        pars = min(experts, 2)
        w1 = k.sb(f"{tag}_w1", [D, pars, FFN], ctx=ctx)
        w2 = k.sb(f"{tag}_w2", [P, pars, FC, D], ctx=ctx)
        b1 = k.sb(f"{tag}_b1", [P, pars, FC], ctx=ctx)
        hidden = k.sb(f"{tag}_hidden", [P, 2, FC, BLK], ctx=ctx)
        up = k.ps(f"{tag}_up", [P, FC, BLK], ctx=ctx)
        down = k.ps(f"{tag}_down", [P, 2, BLK], ctx=ctx)
        loaded = [k.sem(f"{tag}_loaded{i}") for i in range(pars)]
        up_ready, hidden_ready, down_ready, down_read = (
            k.sem(f"{tag}_{s}") for s in ("up_ready", "hidden_ready", "down_ready", "down_read"))

        def weights_in(eng, r, par):
            eng.wait_ge(loaded[par], 16 * loads_per * (r + 1))

        parts = finish(ctx, down, down_ready, down_read, weights_in)
        block = ctx.enter_context(nc.Block())

        def over_experts(eng, body):
            for par in range(pars):
                body(0, par)
            if experts > 2:
                with eng.Fori(1, experts // 2) as r:
                    for par in range(2):
                        body(r, par)

        @block.sync
        def _(sp):
            def load(e, par):
                for dst, src in loads(e, par, w1[:, par], w2[:, par], b1[:, par]):
                    sp.dma_start(dst, src, allow_slow_non_contiguous=True).then_inc(loaded[par], 16)

            for par in range(pars):
                load(par, par)
            for e in range(2, experts):
                sp.wait_ge(down_ready, BLOCKS * (e - 1))
                parts["used"](sp, e - 2)
                load(e, e % 2)

        @block.tensor
        def _(pe):
            def body(r, par):
                weights_in(pe, r, par)
                for blk in range(BLOCKS):
                    m = (pars * r + par) * BLOCKS + blk
                    for f in range(FC):
                        if not (isinstance(m, int) and m == 0):
                            pe.wait_ge(hidden_ready, FC * (m - 1) + f + 1)
                        nc.tensor.matmul(up[:, f, :], w1[:, par, f * P:(f + 1) * P], k.nT[:, blk * BLK:(blk + 1) * BLK],
                                         start=True, stop=True).then_inc(up_ready, 1)
                    if not (isinstance(m, int) and m < 2):
                        pe.wait_ge(down_read, m - 1)
                    for f in range(FC):
                        pe.wait_ge(hidden_ready, FC * m + f + 1)
                        for t in range(4):
                            mm = nc.tensor.matmul(down[:, blk % 2, t * D:(t + 1) * D], hidden[:, blk % 2, f, t * P:(t + 1) * P],
                                                  w2[:, par, f, :], start=(f == 0 and t == 0), stop=(f == FC - 1),
                                                  skip_group_check=True)
                    mm.then_inc(down_ready, 1)

            over_experts(pe, body)

        @block.scalar
        def _(act):
            def body(r, par):
                weights_in(act, r, par)
                for blk in range(BLOCKS):
                    m = (pars * r + par) * BLOCKS + blk
                    if not (isinstance(m, int) and m < 2):
                        act.wait_ge(down_ready, m - 1)
                    for f in range(FC):
                        act.wait_ge(up_ready, FC * m + f + 1)
                        nc.scalar.activation(hidden[:, blk % 2, f, :], up[:, f, :], func,
                                             bias=b1[:, par, f:f + 1] if has_bias else 0.0).then_inc(hidden_ready, 1)

            over_experts(act, body)

        @block.vector
        def _(dve):
            parts["vector"](dve)

        @block.gpsimd
        def _(pool):
            if "gpsimd" in parts:
                parts["gpsimd"](pool)


def top_two(k, tag, ctx, logits):
    nc = k.nc
    W = [P, TILES, EXPERTS]
    b = {s: k.sb(f"{tag}_{s}", W, ctx=ctx) for s in ("at_top", "index", "hot1", "hot2", "others")}
    v = {s: k.sb(f"{tag}_{s}", [P, TILES], ctx=ctx) for s in ("top1", "top2", "index1", "index2")}

    def wide(x):
        return x[:].unsqueeze(2).broadcast_to(W)

    def steps(dve):
        iota = k.iota[:].unsqueeze(1).broadcast_to(W)
        source = logits
        for top, index, hot in (("top1", "index1", "hot1"), ("top2", "index2", "hot2")):
            k.link(dve, nc.vector.tensor_reduce(v[top][:], source[:], AX_X, ALU.max))
            k.link(dve, nc.vector.tensor_tensor(b["at_top"][:], source[:], wide(v[top]), ALU.is_lt))
            k.link(dve, nc.vector.scalar_tensor_tensor(b["index"][:], b["at_top"][:], 2.0 * EXPERTS, iota, ALU.mult, ALU.add))
            k.link(dve, nc.vector.tensor_reduce(v[index][:], b["index"][:], AX_X, ALU.min))
            k.link(dve, nc.vector.tensor_tensor(b[hot][:], iota, wide(v[index]), ALU.is_equal))
            if source is logits:
                k.link(dve, nc.vector.scalar_tensor_tensor(b["others"][:], b[hot][:], -3.0e38, logits[:], ALU.mult, ALU.add))
                source = b["others"]

    return b, v, steps


def feed_forward0(k, a):
    nc = k.nc
    with ExitStack() as ctx:
        gate_w = k.sb("f0_gate_w", [D, EXPERTS], ctx=ctx)
        logits = k.sb("f0_logits", [P, TILES, EXPERTS], ctx=ctx)
        shifted = k.sb("f0_shifted", [P, TILES, EXPERTS], ctx=ctx)
        expd = k.sb("f0_expd", [P, TILES, EXPERTS], ctx=ctx)
        picked = k.sb("f0_picked", [P, TILES, EXPERTS], ctx=ctx)
        total, total_r, g1, g2, both, denom, denom_r, coef1, coef2, coef = (
            k.sb(f"f0_{s}", [P, TILES], ctx=ctx)
            for s in ("total", "total_r", "g1", "g2", "both", "denom", "denom_r", "coef1", "coef2", "coef"))
        w_in, logits_done, shifted_done, expd_done = (
            k.sem(f"f0_{s}") for s in ("w_in", "logits_done", "shifted_done", "expd_done"))
        hot, top, steps = top_two(k, "f0", ctx, logits)
        with ExitStack() as inner:
            gates = k.ps("f0_gates", [P, TILES, EXPERTS], ctx=inner)
            block = inner.enter_context(nc.Block())

            @block.sync
            def _(sp):
                sp.dma_start(gate_w[:], a["L0_ffn_Wg"]).then_inc(w_in, 16)

            @block.tensor
            def _(pe):
                pe.wait_ge(w_in, 16)
                for t in range(TILES):
                    mm = nc.tensor.matmul(gates[:, t, :], k.nT[:, t * P:(t + 1) * P], gate_w[:], start=True, stop=True)
                mm.then_inc(logits_done, 1)

            @block.scalar
            def _(act):
                act.wait_ge(shifted_done, 1)
                nc.scalar.activation(expd[:], shifted[:], ACT.Exp).then_inc(expd_done, 1)

            @block.vector
            def _(dve):
                W = [P, TILES, EXPERTS]
                dve.wait_ge(logits_done, 1)
                k.link(dve, nc.vector.tensor_copy(logits[:], gates[:]))
                steps(dve)
                nc.vector.tensor_tensor(shifted[:], logits[:], top["top1"][:].unsqueeze(2).broadcast_to(W),
                                        ALU.subtract).then_inc(shifted_done, 1)
                dve.wait_ge(expd_done, 1)

                k.link(dve, nc.vector.tensor_reduce(total[:], expd[:], AX_X, ALU.add))
                k.link(dve, nc.vector.reciprocal(total_r[:], total[:]))
                for h, g in (("hot1", g1), ("hot2", g2)):
                    k.link(dve, nc.vector.tensor_tensor(picked[:], expd[:], hot[h][:], ALU.mult))
                    k.link(dve, nc.vector.tensor_reduce(g[:], picked[:], AX_X, ALU.add))
                    k.link(dve, nc.vector.tensor_tensor(g[:], g[:], total_r[:], ALU.mult))
                k.link(dve, nc.vector.tensor_tensor(both[:], g1[:], g2[:], ALU.add))
                k.link(dve, nc.vector.tensor_scalar(denom[:], both[:], float(np.finfo(np.float32).eps), None, ALU.max))
                k.link(dve, nc.vector.reciprocal(denom_r[:], denom[:]))
                k.link(dve, nc.vector.tensor_tensor(coef1[:], g1[:], denom_r[:], ALU.mult))
                k.link(dve, nc.vector.tensor_tensor(coef2[:], g2[:], denom_r[:], ALU.mult))
                k.link(dve, nc.vector.tensor_tensor(coef[:], coef1[:], coef2[:], ALU.add))

        def loads(e, par, w1, w2, b1):
            return [(w1, a["L0_ffn_w1"]), (w2, a["L0_ffn_w2"].rearrange("(f p) d -> p f d", p=P))]

        def finish(ctx, down, down_ready, down_read, weights_in):
            def vector(dve):
                for blk in range(BLOCKS):
                    dve.wait_ge(down_ready, blk + 1)
                    for t in range(4):
                        i = 4 * blk + t
                        mm = nc.vector.scalar_tensor_tensor(k.x[:, i, :], down[:, blk % 2, t * D:(t + 1) * D], coef[:, i:i + 1],
                                                            k.x[:, i, :], ALU.mult, ALU.add)
                    mm.then_inc(down_read, 1)
                dve.wait_ge(down_read, BLOCKS)

            return {"vector": vector}

        feed_forward(k, "f0", loads, 2, 1, ACT.Relu, False, finish)


def delta_layer(k, a):
    nc = k.nc
    H, B = HEADS1, BATCH
    CHUNKS = SEQ_TILES
    GATES = TILES * H
    UNITS = [(b, g) for b in range(B) for g in range(H // GROUP)]
    NU = len(UNITS)
    W = GROUP * P
    NLEV = len(LEVELS)
    HALF = P // 2

    with ExitStack() as outer:
        mixed = k.sb("mixed", [P, TILES, D], ctx=outer)
        normT = k.nT
        rows = {s: k.sb(f"d_{s}", [D, 1], ctx=outer) for s in ("ln1_w", "ln1_b", "ln2_w", "ln2_b")}
        rows_in = k.sem("d_rows_in")
        with nc.Block() as block:
            @block.sync
            def _(sp):
                for s, t in rows.items():
                    sp.dma_start(t[:], a[f"L1_attn_{s}"].rearrange("(d o) -> d o", o=1)).then_inc(rows_in, 16)
                sp.wait_ge(rows_in, 64)
        layer_norm(k, "ln3", k.n, 1e-5, mixed, normT, rows["ln1_w"], rows["ln1_b"])

        with ExitStack() as gated:
            names = ("log_a", "summed", "neg_summed", "beta", "neg_beta", "grown", "neg_beta_grown", "rest", "last")
            all_gates = k.sb("d_all_gates", [P, TILES, len(names), H], ctx=gated)
            gate = {s: all_gates[:, :, i, :] for i, s in enumerate(names)}
            upper = k.sb("d_upper", [P, P], ctx=gated)
            ones = k.sb("d_ones", [P, P], ctx=gated)

            with ExitStack() as ctx:
                w_ab = k.sb("d_w_ab", [D, 2, H], ctx=ctx)
                z = k.sb("d_z", [P, 2, TILES, H], ctx=ctx)
                size, soft, tmp = (k.sb(f"d_{s}", [P, 2, TILES, H], ctx=ctx) for s in ("size", "soft", "tmp"))
                logits = k.ps("d_logits", [P, 2, BLK], ctx=ctx)
                sums = k.ps("d_sums", [P, 2, BLK], ctx=ctx)
                w_in, z_done, size_done, exp_done, one_done, log_done, ones_set, log_a_done, sums_done, diff_done, done = (
                    k.sem(f"d_{s}") for s in ("w_in", "z_done", "size_done", "exp_done", "one_done", "log_done",
                                              "ones_set", "log_a_done", "sums_done", "diff_done", "gates_done"))
                block = ctx.enter_context(nc.Block())

                @block.sync
                def _(sp):
                    sp.dma_start(w_ab[:, 0, :], a["L1_attn_Wa"]).then_inc(w_in, 16)
                    sp.dma_start(w_ab[:, 1, :], a["L1_attn_Wb"]).then_inc(w_in, 16)
                    sp.dma_start(upper[:], a["upper"]).then_inc(w_in, 16)

                @block.gpsimd
                def _(pool):
                    nc.gpsimd.memset(ones[:], 1.0).then_inc(ones_set, 1)
                    pool.wait_ge(ones_set, 1)

                @block.tensor
                def _(pe):
                    pe.wait_ge(w_in, 48)
                    for t in range(TILES):
                        for w in range(2):
                            mm = nc.tensor.matmul(logits[:, w, t * H:(t + 1) * H], normT[:, t * P:(t + 1) * P], w_ab[:, w, :],
                                                  start=True, stop=True)
                    mm.then_inc(z_done, 1)
                    pe.wait_ge(log_a_done, 1)
                    pe.wait_ge(ones_set, 1)
                    log_a = gate["log_a"]
                    nc.tensor.matmul(sums[:, 0, 0:GATES].rearrange("p (t h) -> p t h", h=H), upper[:], log_a, start=True, stop=True)
                    nc.tensor.matmul(sums[:, 1, 0:GATES].rearrange("p (t h) -> p t h", h=H), ones[:], log_a, start=True, stop=True).then_inc(sums_done, 1)

                @block.scalar
                def _(act):
                    act.wait_ge(size_done, 1)
                    nc.scalar.activation(soft[:], size[:], ACT.Exp, scale=-1.0).then_inc(exp_done, 1)
                    act.wait_ge(one_done, 1)
                    nc.scalar.activation(tmp[:, 0], size[:, 0], ACT.Ln).then_inc(log_done, 1)
                    act.wait_ge(diff_done, 1)
                    nc.scalar.activation(gate["grown"], gate["summed"], ACT.Exp).then_inc(exp_done, 1)
                    nc.scalar.activation(gate["rest"], z[:, 0], ACT.Exp).then_inc(exp_done, 1)
                    nc.scalar.activation(gate["last"], size[:, 1], ACT.Exp).then_inc(exp_done, 1)

                @block.vector
                def _(dve):
                    dve.wait_ge(z_done, 1)
                    k.link(dve, nc.vector.tensor_copy(z[:].rearrange("p w t h -> p w (t h)"), logits[:, :, 0:GATES]))
                    k.link(dve, nc.vector.tensor_scalar(tmp[:], z[:], -1.0, None, ALU.mult))
                    nc.vector.tensor_tensor(size[:], z[:], tmp[:], ALU.max).then_inc(size_done, 1)
                    dve.wait_ge(exp_done, 1)
                    k.link(dve, nc.vector.tensor_scalar(size[:], soft[:], 1.0, None, ALU.add))
                    nc.vector.tensor_scalar(z[:, 0], z[:, 0], 0.0, None, ALU.min).then_inc(one_done, 1)
                    k.link(dve, nc.vector.reciprocal(tmp[:, 1], size[:, 1]))
                    k.link(dve, nc.vector.tensor_scalar(z[:, 1], z[:, 1], 0.0, None, ALU.is_ge))
                    k.link(dve, nc.vector.tensor_tensor(soft[:, 1], soft[:, 1], z[:, 1], ALU.max))
                    k.link(dve, nc.vector.tensor_tensor(gate["beta"], soft[:, 1], tmp[:, 1], ALU.mult))
                    k.link(dve, nc.vector.tensor_scalar(gate["neg_beta"], gate["beta"], -1.0, None, ALU.mult))
                    dve.wait_ge(log_done, 1)
                    nc.vector.tensor_tensor(gate["log_a"], z[:, 0], tmp[:, 0], ALU.subtract).then_inc(log_a_done, 1)
                    dve.wait_ge(sums_done, 1)
                    dve.wait_ge(log_a_done, 1)
                    k.link(dve, nc.vector.tensor_copy(gate["summed"], sums[:, 0, 0:GATES].rearrange("p (t h) -> p t h", h=H)))
                    k.link(dve, nc.vector.tensor_copy(size[:, 1].rearrange("p t h -> p (t h)"), sums[:, 1, 0:GATES]))
                    k.link(dve, nc.vector.tensor_scalar(gate["neg_summed"], gate["summed"], -1.0, None, ALU.mult))
                    nc.vector.tensor_tensor(z[:, 0], size[:, 1], gate["summed"], ALU.subtract).then_inc(diff_done, 1)
                    dve.wait_ge(exp_done, 4)
                    nc.vector.tensor_tensor(gate["neg_beta_grown"], gate["neg_beta"], gate["grown"], ALU.mult).then_inc(done, 1)
                    dve.wait_ge(done, 1)

            with ExitStack() as ctx:
                w_qkv = k.sb("g_w_qkv", [D, 3, H * P], ctx=ctx)
                w_o = k.sb("g_w_o", [P, H, D], ctx=ctx)
                level_masks = k.sb("g_level_masks", [P, NLEV, HALF], ctx=ctx)
                pair_mask = k.sb("g_pair_mask", [P, P], ctx=ctx)
                below = k.sb("g_below", [P, P], ctx=ctx)
                below_b = k.sb("g_below_b", [P, GROUP, P], BF16, ctx)
                identb = k.sb("g_identb", [P, P], BF16, ctx)
                state = k.sb("g_state", [P, NU, GROUP, P], ctx=ctx)
                chunk_T = k.sb("g_chunk_T", [D, B, P], ctx=ctx)
                chunk_gates = k.sb("g_chunk_gates", [P, B, len(names), H], ctx=ctx)

                def unit_buffer(s, width=W):
                    return k.sb(f"g_{s}", [P, NU, width], ctx=ctx)

                q, qg, kk, kt, v = (unit_buffer(s) for s in ("q", "qg", "k", "kt", "v"))
                kT, qT, qgT = (unit_buffer(s) for s in ("kT", "qT", "qgT"))
                decay, attend, coupling, solve_T, solve = (unit_buffer(s) for s in ("decay", "attend", "coupling", "solve_T", "solve"))
                update, out_T = unit_buffer("update"), unit_buffer("out_T")
                partial = unit_buffer("partial", GROUP * HALF)
                squares = k.sb("g_squares", [P, NU, 2 * GROUP], ctx=ctx)
                norms = k.sb("g_norms", [P, NU, 2 * GROUP], ctx=ctx)
                bank = k.ps("g_bank", [P, 2, NU, W], ctx=ctx)

                sem_names = (
                    "w_in", "consts_set", "state_set", "chunk_ready", "gates_ready", "q_proj", "k_proj", "v_proj", "q_silu", "k_silu", "v_silu",
                    "q_sq", "k_sq", "sq_done", "eps_done", "norm_done", "qg_done", "q_done", "k_done", "v_done", "la_done",
                    "kT_turned", "kT_kept", "qT_turned", "qT_kept", "qgT_turned", "qgT_kept", "decay_sum", "decay_done",
                    "kk_done", "kk_read", "kq_done", "attend_done", "coup_turned", "coup_done", "pair_done", "solve0_done",
                    "solve_turned", "solve_T0", "m_done", "m_read", "n_done", "n_read", "t_turned", "t_kept",
                    "ks_done", "v_ready", "u_done", "u_kept", "o_done", "o_kept", "ds_done", "state_done", "wo_done", "mixed_done")
                s_ = {n: k.sem(f"g_{n}") for n in sem_names}
                block = ctx.enter_context(nc.Block())

                def heads4(t):
                    return t.rearrange("p (h c) -> p h c", h=GROUP)

                def wide(col):
                    return col.unsqueeze(2).broadcast_to([P, GROUP, P])

                def odd(t, s):
                    return t.rearrange("p (n two s) -> p n two s", two=2, s=s)[:, :, 1, :]

                def cols(name, b, g):
                    return chunk_gates[:, b, names.index(name), g * GROUP:(g + 1) * GROUP]

                @block.sync
                def _(sp):
                    for i, w in enumerate(("Wq", "Wk", "Wv")):
                        sp.dma_start(w_qkv[:, i, :], a[f"L1_attn_{w}"]).then_inc(s_["w_in"], 16)
                    sp.dma_start(w_o[:], a["L1_attn_Wo"].rearrange("(h v) d -> v h d", v=P)).then_inc(s_["w_in"], 16)
                    sp.dma_start(level_masks[:], a["levels"].rearrange("p (l c) -> p l c", l=NLEV)).then_inc(s_["w_in"], 16)
                    sp.dma_start(pair_mask[:], a["pair"]).then_inc(s_["w_in"], 16)
                    sp.dma_start(below[:], a["below"]).then_inc(s_["w_in"], 16)

                WEIGHTS = 16 * 7

                @block.tensor
                def _(pe):
                    pe.wait_ge(s_["w_in"], WEIGHTS)
                    pe.wait_ge(s_["consts_set"], 2)

                    def X(u):
                        return bank[:, 0, u, :]

                    def Y(u):
                        return bank[:, 1, u, :]

                    def sl(t, u, h):
                        return t[:, u, h * P:(h + 1) * P]

                    def each_head(out, u, lhs, rhs, done, width=P, **kw):
                        for h in range(GROUP):
                            mm = nc.tensor.matmul(out(u)[:, h * width:(h + 1) * width], lhs(h), rhs(h), **({"start": True, "stop": True} | kw))
                        mm.then_inc(s_[done], 1)

                    def turn(out, u, src, done):
                        for h in range(GROUP):
                            mm = nc.tensor.transpose(out(u)[:, h * P:(h + 1) * P], sl(src, u, h), k.ident[:])
                        mm.then_inc(s_[done], 1)

                    def body(c):
                        first = isinstance(c, int)

                        def w(name, u, back=0):
                            if back and first:
                                return
                            pe.wait_ge(s_[name], NU * (c - back) + u + 1)

                        def w_level(name, lev, u):
                            pe.wait_ge(s_[name], NU * (NLEV * c + lev) + u + 1)

                        for u, (b, g) in enumerate(UNITS):
                            if g == 0:
                                pe.wait_ge(s_["chunk_ready"], B * c + b + 1)
                            w("state_done", u, 1)
                            nc.tensor.matmul(X(u), chunk_T[:, b, :], w_qkv[:, 0, g * W:(g + 1) * W], start=True, stop=True).then_inc(s_["q_proj"], 1)
                            if g == 0 and not first:
                                pe.wait_ge(s_["mixed_done"], B * (c - 1) + b + 1)
                            w("o_kept", u, 1)
                            nc.tensor.matmul(Y(u), chunk_T[:, b, :], w_qkv[:, 1, g * W:(g + 1) * W], start=True, stop=True).then_inc(s_["k_proj"], 1)
                        for u, (b, g) in enumerate(UNITS):
                            w("q_silu", u)
                            nc.tensor.matmul(X(u), chunk_T[:, b, :], w_qkv[:, 2, g * W:(g + 1) * W], start=True, stop=True).then_inc(s_["v_proj"], 1)
                        for u in range(NU):
                            w("k_done", u)
                            turn(Y, u, kk, "kT_turned")
                        for u in range(NU):
                            w("la_done", u)
                            w("v_silu", u)
                            nc.tensor.matmul(X(u), ones[:], out_T[:, u, :], start=True, stop=False)
                            nc.tensor.matmul(X(u), identb[:], below_b[:].rearrange("p h c -> p (h c)"), start=False, stop=True).then_inc(s_["decay_sum"], 1)
                        for u in range(NU):
                            w("q_done", u)
                            w("kT_kept", u)
                            turn(Y, u, q, "qT_turned")
                        for u in range(NU):
                            w("decay_done", u)
                            each_head(X, u, lambda h: sl(kT, u, h), lambda h: sl(kT, u, h), "kk_done")
                        for u in range(NU):
                            w("qT_kept", u)
                            each_head(Y, u, lambda h: sl(kT, u, h), lambda h: sl(qT, u, h), "kq_done")
                        for u in range(NU):
                            w("kk_read", u)
                            turn(X, u, update, "coup_turned")
                        for u in range(NU):
                            w("attend_done", u)
                            w("qg_done", u)
                            turn(Y, u, qg, "qgT_turned")
                        for u in range(NU):
                            w("pair_done", u)
                            w("coup_done", u)
                            turn(X, u, solve_T, "solve_turned")
                        for u in range(NU):
                            w("qgT_kept", u)
                            w("state_done", u, 1)
                            each_head(Y, u, lambda h: sl(kT, u, h), lambda h: state[:, u, h, :], "ks_done")
                        for lev, s in enumerate(LEVELS):
                            for u in range(NU):
                                if lev == 0:
                                    w("solve_T0", u)
                                else:
                                    w_level("n_read", lev - 1, u)
                                    pe.wait_ge(s_["t_kept"], NU * ((NLEV - 1) * c + lev - 1) + u + 1)
                                each_head(X, u, lambda h: sl(coupling, u, h), lambda h: odd(sl(solve, u, h), s), "m_done", HALF)
                            for u in range(NU):
                                w_level("m_read", lev, u)
                                if lev == 0:
                                    w("v_ready", u)
                                each_head(Y, u, lambda h: sl(solve_T, u, h), lambda h: partial[:, u, h * HALF:(h + 1) * HALF], "n_done", HALF)
                            if lev < NLEV - 1:
                                for u in range(NU):
                                    w_level("n_read", lev, u)
                                    turn(X, u, solve, "t_turned")
                        for u in range(NU):
                            w_level("n_read", NLEV - 1, u)
                            each_head(X, u, lambda h: sl(solve, u, h), lambda h: sl(v, u, h), "u_done")
                        for u in range(NU):
                            w("u_kept", u)
                            for h in range(GROUP):
                                nc.tensor.matmul(Y(u)[:, h * P:(h + 1) * P], state[:, u, h, :], sl(qgT, u, h), start=True, stop=False)
                                mm = nc.tensor.matmul(Y(u)[:, h * P:(h + 1) * P], sl(update, u, h), sl(attend, u, h), start=False, stop=True)
                            mm.then_inc(s_["o_done"], 1)
                        for u in range(NU):
                            each_head(X, u, lambda h: sl(kt, u, h), lambda h: sl(update, u, h), "ds_done")
                        for b in range(B):
                            u0 = b * (H // GROUP)
                            for u in range(u0, u0 + H // GROUP):
                                w("o_kept", u)
                                for h in range(GROUP):
                                    mm = nc.tensor.matmul(Y(u0)[:, 0:D], sl(out_T, u, h), w_o[:, (u - u0) * GROUP + h, :],
                                                          start=(u == u0 and h == 0), stop=(u > u0 and h == GROUP - 1))
                            mm.then_inc(s_["wo_done"], 1)

                    body(0)
                    with pe.Fori(1, CHUNKS) as c:
                        body(c)

                @block.scalar
                def _(act):
                    def body(c):
                        first = isinstance(c, int)

                        def w(name, u, back=0):
                            if back and first:
                                return
                            act.wait_ge(s_[name], NU * (c - back) + u + 1)

                        def keep(src, u, dst, ready, kept):
                            w(ready, u)
                            nc.scalar.copy(dst[:, u, :], bank[:, src, u, :]).then_inc(s_[kept], 1)

                        for u in range(NU):
                            w("q_proj", u)
                            w("qgT_turned", u, 1)
                            nc.scalar.activation(q[:, u, :], bank[:, 0, u, :], ACT.Silu).then_inc(s_["q_silu"], 1)
                            w("k_proj", u)
                            w("ds_done", u, 1)
                            nc.scalar.activation(kk[:, u, :], bank[:, 1, u, :], ACT.Silu).then_inc(s_["k_silu"], 1)
                        for u in range(NU):
                            w("v_proj", u)
                            nc.scalar.activation(v[:, u, :], bank[:, 0, u, :], ACT.Silu).then_inc(s_["v_silu"], 1)
                        for u in range(NU):
                            keep(1, u, kT, "kT_turned", "kT_kept")
                        for u, (b, g) in enumerate(UNITS):
                            w("decay_sum", u)
                            act.wait_ge(s_["gates_ready"], B * c + b + 1)
                            for h in range(GROUP):
                                last = nc.scalar.activation(
                                    decay[:, u, h * P:(h + 1) * P], bank[:, 0, u, h * P:(h + 1) * P], ACT.Exp,
                                    bias=cols("neg_summed", b, g)[:, h:h + 1])
                            last.then_inc(s_["decay_done"], 1)
                        for u in range(NU):
                            keep(1, u, qT, "qT_turned", "qT_kept")
                        for u in range(NU):
                            w("o_done", u, 1)
                            keep(1, u, qgT, "qgT_turned", "qgT_kept")
                        for u in range(NU):
                            keep(0, u, solve, "solve_turned", "solve_T0")
                        for lev in range(NLEV - 1):
                            for u in range(NU):
                                act.wait_ge(s_["t_turned"], NU * ((NLEV - 1) * c + lev) + u + 1)
                                nc.scalar.copy(solve_T[:, u, :], bank[:, 0, u, :]).then_inc(s_["t_kept"], 1)
                        for u in range(NU):
                            keep(0, u, update, "u_done", "u_kept")
                        for u in range(NU):
                            keep(1, u, out_T, "o_done", "o_kept")

                    body(0)
                    with act.Fori(1, CHUNKS) as c:
                        body(c)

                @block.vector
                def _(dve):
                    nc.vector.memset(state[:], 0.0).then_inc(s_["state_set"], 1)
                    dve.wait_ge(s_["w_in"], WEIGHTS)
                    dve.wait_ge(s_["state_set"], 1)

                    def body(c):
                        first = isinstance(c, int)

                        def w(name, u, back=0):
                            if back and first:
                                return
                            dve.wait_ge(s_[name], NU * (c - back) + u + 1)

                        for b in range(B):
                            last_unit = (b + 1) * (H // GROUP)
                            if not first:
                                dve.wait_ge(s_["v_proj"], NU * (c - 1) + last_unit)
                                dve.wait_ge(s_["decay_done"], NU * (c - 1) + last_unit)
                                dve.wait_ge(s_["v_done"], NU * (c - 1) + last_unit)
                                dve.wait_ge(s_["state_done"], NU * (c - 1) + last_unit)
                            nc.vector.tensor_scalar(chunk_T[:, b, :], normT[:, bass.ds((b * CHUNKS + c) * P, P)], 0.0, None,
                                                    ALU.add).then_inc(s_["chunk_ready"], 1)
                            nc.vector.tensor_scalar(chunk_gates[:, b], all_gates[:, b * CHUNKS + c], 0.0, None,
                                                    ALU.add).then_inc(s_["gates_ready"], 1)
                        for u in range(NU):
                            w("q_sq", u)
                            nc.vector.tensor_reduce(squares[:, u, 0:GROUP], heads4(solve[:, u, :]), AX_X, ALU.add)
                            w("k_sq", u)
                            nc.vector.tensor_reduce(squares[:, u, GROUP:], heads4(solve_T[:, u, :]), AX_X, ALU.add).then_inc(s_["sq_done"], 1)
                            w("sq_done", u)
                            nc.vector.tensor_scalar(norms[:, u, :], squares[:, u, :], 1e-6, None, ALU.add).then_inc(s_["eps_done"], 1)
                        for u in range(NU):
                            w("kk_done", u)
                            w("u_kept", u, 1)
                            w("decay_done", u)
                            nc.vector.tensor_tensor(update[:, u, :], bank[:, 0, u, :], decay[:, u, :], ALU.mult).then_inc(s_["kk_read"], 1)
                        for u in range(NU):
                            w("kq_done", u)
                            nc.vector.tensor_tensor(attend[:, u, :], bank[:, 1, u, :], decay[:, u, :], ALU.mult).then_inc(s_["attend_done"], 1)
                        for u, (b, g) in enumerate(UNITS):
                            w("coup_turned", u)
                            dve.wait_ge(s_["gates_ready"], B * c + b + 1)
                            nc.vector.tensor_tensor(heads4(coupling[:, u, :]), heads4(bank[:, 0, u, :]), wide(cols("neg_beta", b, g)),
                                                    ALU.mult).then_inc(s_["coup_done"], 1)
                        for u, (b, g) in enumerate(UNITS):
                            w("ks_done", u)
                            w("v_done", u)
                            for h in range(GROUP):
                                last = nc.vector.scalar_tensor_tensor(
                                    v[:, u, h * P:(h + 1) * P], bank[:, 1, u, h * P:(h + 1) * P],
                                    cols("neg_beta_grown", b, g)[:, h:h + 1],
                                    v[:, u, h * P:(h + 1) * P], ALU.mult, ALU.add)
                            last.then_inc(s_["v_ready"], 1)
                        for lev, s in enumerate(LEVELS):
                            for u in range(NU):
                                m = NU * (NLEV * c + lev) + u + 1
                                dve.wait_ge(s_["m_done"], m)
                                nc.vector.tensor_tensor(
                                    partial[:, u, :].rearrange("p (h c) -> p h c", h=GROUP),
                                    bank[:, 0, u, 0:GROUP * HALF].rearrange("p (h c) -> p h c", h=GROUP),
                                    level_masks[:, lev, :].unsqueeze(1).broadcast_to([P, GROUP, HALF]), ALU.mult).then_inc(s_["m_read"], 1)
                            for u in range(NU):
                                m = NU * (NLEV * c + lev) + u + 1
                                dve.wait_ge(s_["n_done"], m)
                                nc.vector.tensor_tensor(
                                    odd(solve[:, u, :], s), bank[:, 1, u, 0:GROUP * HALF].rearrange("p (n s) -> p n s", s=s),
                                    odd(solve[:, u, :], s), ALU.add).then_inc(s_["n_read"], 1)
                        for u, (b, g) in enumerate(UNITS):
                            w("ds_done", u)
                            for h in range(GROUP):
                                last = nc.vector.scalar_tensor_tensor(
                                    state[:, u, h, :], state[:, u, h, :],
                                    cols("last", b, g)[:, h:h + 1],
                                    bank[:, 0, u, h * P:(h + 1) * P], ALU.mult, ALU.add)
                            last.then_inc(s_["state_done"], 1)
                        for b in range(B):
                            dve.wait_ge(s_["wo_done"], B * c + b + 1)
                            nc.vector.tensor_tensor(mixed[:, b * CHUNKS + c, :], bank[:, 1, b * (H // GROUP), 0:D], k.n[:, b * CHUNKS + c, :],
                                                    ALU.add).then_inc(s_["mixed_done"], 1)

                    body(0)
                    with dve.Fori(1, CHUNKS) as c:
                        body(c)
                    dve.wait_ge(s_["mixed_done"], B * CHUNKS)

                @block.gpsimd
                def _(pool):
                    pool.wait_ge(s_["w_in"], WEIGHTS)
                    for h in range(GROUP):
                        last = nc.gpsimd.tensor_copy(below_b[:, h, :], below[:])
                    last.then_inc(s_["consts_set"], 1)
                    nc.gpsimd.tensor_copy(identb[:], k.ident[:]).then_inc(s_["consts_set"], 1)
                    pool.wait_ge(s_["consts_set"], 2)
                    TT = nc.gpsimd.tensor_tensor

                    def body(c):
                        first = isinstance(c, int)

                        def w(name, u, back=0):
                            if back and first:
                                return
                            pool.wait_ge(s_[name], NU * (c - back) + u + 1)

                        for u, (b, g) in enumerate(UNITS):
                            w("q_silu", u)
                            w("u_done", u, 1)
                            TT(solve[:, u, :], q[:, u, :], q[:, u, :], ALU.mult).then_inc(s_["q_sq"], 1)
                            w("k_silu", u)
                            TT(solve_T[:, u, :], kk[:, u, :], kk[:, u, :], ALU.mult).then_inc(s_["k_sq"], 1)
                        for u, (b, g) in enumerate(UNITS):
                            w("eps_done", u)
                            pool.wait_ge(s_["gates_ready"], B * c + b + 1)
                            TT(squares[:, u, :], norms[:, u, :], k.half[:, 0:2 * GROUP], ALU.pow).then_inc(s_["norm_done"], 1)
                            w("norm_done", u)
                            TT(heads4(kk[:, u, :]), heads4(kk[:, u, :]), wide(squares[:, u, GROUP:]), ALU.mult).then_inc(s_["k_done"], 1)
                            if not first:
                                pool.wait_ge(s_["wo_done"], B * (c - 1) + b + 1)
                            TT(heads4(out_T[:, u, :]), upper[:].unsqueeze(1).broadcast_to([P, GROUP, P]), wide(cols("log_a", b, g)),
                               ALU.mult).then_inc(s_["la_done"], 1)
                            TT(heads4(q[:, u, :]), heads4(q[:, u, :]), wide(squares[:, u, 0:GROUP]), ALU.mult).then_inc(s_["q_done"], 1)
                        for u, (b, g) in enumerate(UNITS):
                            w("k_done", u)
                            TT(heads4(kt[:, u, :]), heads4(kk[:, u, :]), wide(cols("rest", b, g)), ALU.mult)
                            w("q_done", u)
                            TT(heads4(qg[:, u, :]), heads4(q[:, u, :]), wide(cols("grown", b, g)), ALU.mult).then_inc(s_["qg_done"], 1)
                            w("v_silu", u)
                            TT(heads4(v[:, u, :]), heads4(v[:, u, :]), wide(cols("beta", b, g)), ALU.mult).then_inc(s_["v_done"], 1)
                        for u in range(NU):
                            w("coup_done", u)
                            TT(heads4(solve_T[:, u, :]), heads4(coupling[:, u, :]), pair_mask[:].unsqueeze(1).broadcast_to([P, GROUP, P]),
                               ALU.mult).then_inc(s_["solve0_done"], 1)
                            w("solve0_done", u)
                            TT(heads4(solve_T[:, u, :]), heads4(solve_T[:, u, :]), k.ident[:].unsqueeze(1).broadcast_to([P, GROUP, P]),
                               ALU.add).then_inc(s_["pair_done"], 1)

                    body(0)
                    with pool.Fori(1, CHUNKS) as c:
                        body(c)

        layer_norm(k, "ln4", mixed, 1e-5, k.n, k.nT, rows["ln2_w"], rows["ln2_b"])
        with ExitStack() as ctx:
            b2 = k.sb("f1_b2", [P, D], ctx=ctx)

            def loads(e, par, w1, w2, b1):
                return [(w1, a["L1_attn_W1"]), (w2, a["L1_attn_W2"].rearrange("(f p) d -> p f d", p=P)),
                        (b1, a["L1_attn_b1"].rearrange("(f p) -> p f", p=P)), (b2[:], a["L1_attn_b2"].partition_broadcast(P))]

            def finish(ctx, down, down_ready, down_read, weights_in):
                base_done, added = k.sem("f1_base_done"), k.sem("f1_added")

                def vector(dve):
                    weights_in(dve, 0, 0)
                    nc.vector.tensor_tensor(mixed[:], mixed[:], b2[:].unsqueeze(1).broadcast_to([P, TILES, D]), ALU.add).then_inc(base_done, 1)
                    dve.wait_ge(base_done, 1)
                    nc.vector.tensor_tensor(k.x[:], k.x[:], mixed[:], ALU.add).then_inc(base_done, 1)
                    dve.wait_ge(base_done, 2)
                    for blk in range(BLOCKS):
                        dve.wait_ge(down_ready, blk + 1)
                        nc.vector.tensor_tensor(k.x[:, 4 * blk:4 * blk + 4, :], down[:, blk % 2, :].rearrange("p (t d) -> p t d", t=4),
                                                k.x[:, 4 * blk:4 * blk + 4, :], ALU.add).then_inc(down_read, 1)
                    dve.wait_ge(down_read, BLOCKS)

                return {"vector": vector}

            feed_forward(k, "f1", loads, 4, 1, ACT.Gelu, True, finish)


def experts(k, a):
    nc = k.nc
    with ExitStack() as ctx:
        router = k.sb("moe_router", [D, EXPERTS], ctx=ctx)
        beta = k.sb("moe_beta", [EXPERTS, D], ctx=ctx)
        logits = k.sb("moe_logits", [P, TILES, EXPERTS], ctx=ctx)
        gate_of = k.sb("moe_gate_of", [P, EXPERTS, TILES], ctx=ctx)
        gates = k.sb("moe_gates", [P, TILES, EXPERTS], ctx=ctx)
        gates_T = k.sb("moe_gates_T", [EXPERTS, TILES, P], ctx=ctx)
        scaled = k.sb("moe_scaled", [P, TILES, EXPERTS], ctx=ctx)
        gap, expd, total, w_1, w_2 = (k.sb(f"moe_{s}", [P, TILES], ctx=ctx) for s in ("gap", "expd", "total", "w_1", "w_2"))
        w_in, logits_done, gap_done, expd_done, gates_done, turned_done, kept, beta_done = (
            k.sem(f"moe_{s}") for s in ("w_in", "logits_done", "gap_done", "expd_done", "gates_done", "turned_done",
                                        "kept", "beta_done"))
        hot, top, steps = top_two(k, "moe", ctx, logits)
        with ExitStack() as inner:
            route = k.ps("moe_route", [P, TILES, EXPERTS], ctx=inner)
            turned = k.ps("moe_turned", [EXPERTS, TILES, P], ctx=inner)
            offset = k.ps("moe_offset", [P, 2, BLK], ctx=inner)
            block = inner.enter_context(nc.Block())

            @block.sync
            def _(sp):
                sp.dma_start(router[:], a["L1_ffn_router_w"]).then_inc(w_in, 16)
                sp.dma_start(beta[:], a["L1_ffn_beta"]).then_inc(w_in, 16)

            @block.tensor
            def _(pe):
                pe.wait_ge(w_in, 32)
                for t in range(TILES):
                    mm = nc.tensor.matmul(route[:, t, :], k.nT[:, t * P:(t + 1) * P], router[:], start=True, stop=True)
                mm.then_inc(logits_done, 1)
                pe.wait_ge(gates_done, 1)
                for t in range(TILES):
                    mm = nc.tensor.transpose(turned[:, t, :], gates[:, t, :], k.ident[:])
                mm.then_inc(turned_done, 1)
                pe.wait_ge(kept, 1)
                for t in range(TILES):
                    if t % 4 == 0 and t >= 8:
                        pe.wait_ge(beta_done, t // 4 - 1)
                    mm = nc.tensor.matmul(offset[:, (t // 4) % 2, (t % 4) * D:(t % 4 + 1) * D], gates_T[:, t, :], beta[:],
                                          start=True, stop=True)
                    if t % 4 == 3:
                        mm.then_inc(turned_done, 1)

            @block.scalar
            def _(act):
                act.wait_ge(gap_done, 1)
                nc.scalar.activation(expd[:], gap[:], ACT.Exp).then_inc(expd_done, 1)
                act.wait_ge(turned_done, 1)
                nc.scalar.copy(gates_T[:], turned[:]).then_inc(kept, 1)

            @block.vector
            def _(dve):
                dve.wait_ge(logits_done, 1)
                k.link(dve, nc.vector.tensor_copy(logits[:], route[:]))
                steps(dve)
                nc.vector.tensor_tensor(gap[:], top["top2"][:], top["top1"][:], ALU.subtract).then_inc(gap_done, 1)
                dve.wait_ge(expd_done, 1)

                W = [P, TILES, EXPERTS]
                k.link(dve, nc.vector.tensor_scalar(total[:], expd[:], 1.0, None, ALU.add))
                k.link(dve, nc.vector.reciprocal(w_1[:], total[:]))
                k.link(dve, nc.vector.tensor_tensor(w_2[:], w_1[:], expd[:], ALU.mult))
                k.link(dve, nc.vector.tensor_tensor(scaled[:], hot["hot1"][:], w_1[:].unsqueeze(2).broadcast_to(W), ALU.mult))
                k.link(dve, nc.vector.tensor_tensor(gates[:], hot["hot2"][:], w_2[:].unsqueeze(2).broadcast_to(W), ALU.mult))
                k.link(dve, nc.vector.tensor_tensor(gates[:], gates[:], scaled[:], ALU.add))
                nc.vector.tensor_copy(gate_of[:], gates[:].rearrange("p t e -> p e t")).then_inc(gates_done, 1)
                for g in range(BLOCKS):
                    dve.wait_ge(turned_done, g + 2)
                    nc.vector.tensor_tensor(k.x[:, 4 * g:4 * g + 4, :], offset[:, g % 2, :].rearrange("p (t d) -> p t d", t=4),
                                            k.x[:, 4 * g:4 * g + 4, :], ALU.add).then_inc(beta_done, 1)
                dve.wait_ge(beta_done, BLOCKS)
                dve.wait_ge(gates_done, 1)

        b2 = k.sb("moe_b2", [P, 2, D], ctx=ctx)
        gamma = k.sb("moe_gamma", [P, 2, D], ctx=ctx)

        def loads(e, par, w1, w2, b1):
            return [(w1, a["L1_ffn_w1"][e]), (w2, a["L1_ffn_w2"][e].rearrange("(f p) d -> p f d", p=P)),
                    (b1, a["L1_ffn_b1"][e].rearrange("(f p) -> p f", p=P)),
                    (b2[:, par], a["L1_ffn_b2"][e].partition_broadcast(P)),
                    (gamma[:, par], a["L1_ffn_gamma"][e].partition_broadcast(P))]

        def finish(ctx, down, down_ready, down_read, weights_in):
            res = k.sb("moe_res", [P, 2, 4, D], ctx=ctx)
            stats = k.sb("moe_stats", [P, 2, 4, 6], ctx=ctx)
            moments = k.sb("moe_moments", [P, 2, 4, 2], ctx=ctx)
            shifted = k.sb("moe_shifted", [P, 2, 4], ctx=ctx)
            rstd = k.sb("moe_rstd", [P, 2, 4], ctx=ctx)
            gated = k.sb("moe_gated", [P, 2, 4], ctx=ctx)
            res_done, stats_done, moments_done, shifted_done, rstd_done, gated_done, normed, weighted, added = (
                k.sem(f"moe_{s}") for s in ("res_done", "stats_done", "moments_done", "shifted_done", "rstd_done",
                                            "gated_done", "normed", "weighted", "added"))
            ALL = EXPERTS * BLOCKS

            def over(eng, body):
                for par in range(2):
                    body(0, par)
                with eng.Fori(1, EXPERTS // 2) as r:
                    for par in range(2):
                        body(r, par)

            def vector(dve):
                def scale(e, m, blk, s):
                    dve.wait_ge(rstd_done, m + 1)
                    nc.vector.tensor_tensor(gated[:, s, :], rstd[:, s, :], gate_of[:, e, 4 * blk:4 * blk + 4],
                                            ALU.mult).then_inc(gated_done, 1)
                    dve.wait_ge(gated_done, m + 1)
                    for t in range(4):
                        last = nc.vector.tensor_scalar(res[:, s, t, :], res[:, s, t, :], moments[:, s, t, 0:1],
                                                       gated[:, s, t:t + 1], ALU.subtract, ALU.mult)
                    last.then_inc(normed, 1)

                def body(r, par):
                    e = 2 * r + par
                    weights_in(dve, r, par)
                    for blk in range(BLOCKS):
                        m, s = e * BLOCKS + blk, blk % 2
                        dve.wait_ge(down_ready, m + 1)
                        if not (isinstance(m, int) and m < 2):
                            dve.wait_ge(added, m - 1)
                        nc.vector.tensor_tensor(res[:, s], down[:, s, :].rearrange("p (t d) -> p t d", t=4),
                                                k.n[:, 4 * blk:4 * blk + 4, :], ALU.add).then_inc(down_read, 1)
                        dve.wait_ge(down_read, m + 1)
                        nc.vector.tensor_tensor(res[:, s], res[:, s], b2[:, par].unsqueeze(1).broadcast_to([P, 4, D]),
                                                ALU.add).then_inc(res_done, 1)
                        dve.wait_ge(res_done, m + 1)
                        for t in range(4):
                            last = nc.vector.bn_stats(stats[:, s, t, :], res[:, s, t, :])
                        last.then_inc(stats_done, 1)
                        dve.wait_ge(stats_done, m + 1)
                        if not (isinstance(m, int) and m == 0):
                            scale(e if blk else e - 1, m - 1, (blk - 1) % BLOCKS, 1 - s)
                        for t in range(4):
                            last = nc.vector.bn_aggr(moments[:, s, t, :], stats[:, s, t, :])
                        last.then_inc(moments_done, 1)
                        dve.wait_ge(moments_done, m + 1)
                        nc.vector.tensor_scalar(shifted[:, s, :], moments[:, s, :, 1], 1e-6, None, ALU.add).then_inc(shifted_done, 1)

                over(dve, body)
                scale(EXPERTS - 1, ALL - 1, BLOCKS - 1, 1)
                dve.wait_ge(normed, ALL)

            def gpsimd(pool):
                def add(par, m, blk, s):
                    pool.wait_ge(normed, m + 1)
                    nc.gpsimd.tensor_tensor(res[:, s], res[:, s], gamma[:, par].unsqueeze(1).broadcast_to([P, 4, D]),
                                            ALU.mult).then_inc(weighted, 1)
                    pool.wait_ge(weighted, m + 1)
                    nc.gpsimd.tensor_tensor(k.x[:, 4 * blk:4 * blk + 4, :], k.x[:, 4 * blk:4 * blk + 4, :], res[:, s],
                                            ALU.add).then_inc(added, 1)

                def body(r, par):
                    weights_in(pool, r, par)
                    for blk in range(BLOCKS):
                        m, s = (2 * r + par) * BLOCKS + blk, blk % 2
                        pool.wait_ge(shifted_done, m + 1)
                        nc.gpsimd.tensor_tensor(rstd[:, s, :], shifted[:, s, :], k.half[:, 0:4], ALU.pow).then_inc(rstd_done, 1)
                        if not (isinstance(m, int) and m == 0):
                            add(par if blk else 1 - par, m - 1, (blk - 1) % BLOCKS, 1 - s)

                over(pool, body)
                add(1, ALL - 1, BLOCKS - 1, 1)
                pool.wait_ge(added, ALL)

            def used(sp, e):
                sp.wait_ge(added, BLOCKS * (e + 1))

            return {"vector": vector, "gpsimd": gpsimd, "used": used}

        feed_forward(k, "moe", loads, 5, EXPERTS, ACT.Gelu, True, finish)


def store(k, out):
    with k.nc.Block() as block:
        @block.sync
        def _(sp):
            sp.dma_start(out.rearrange("b (t p) d -> p (b t) d", p=P), k.x[:]).then_inc(k.moved, 16)
            sp.wait_ge(k.moved, 64)


def build_program(nc, a, out):
    with ExitStack() as ctx:
        k = Core(nc, ctx)
        start(k, a)
        layer_norm(k, "ln0", k.x, 1e-5, k.n, k.nT)
        attention(k, a)
        layer_norm(k, "ln1", k.x, 1e-5, k.n, k.nT)
        feed_forward0(k, a)
        layer_norm(k, "ln2", k.x, 1e-5, k.n)
        delta_layer(k, a)
        layer_norm(k, "ln5", k.x, 1e-5, k.n, k.nT)
        experts(k, a)
        store(k, out)


_INPUTS = [
    "L0_attn_X", "L0_attn_W_qkv", "L0_attn_b_qkv", "L0_attn_W_proj", "L0_attn_b_proj", "L0_ffn_Wg", "L0_ffn_w1",
    "L0_ffn_w2", "L1_attn_Wq", "L1_attn_Wk", "L1_attn_Wv", "L1_attn_Wb", "L1_attn_Wa", "L1_attn_Wo", "L1_attn_ln1_w",
    "L1_attn_ln1_b", "L1_attn_ln2_w", "L1_attn_ln2_b", "L1_attn_W1", "L1_attn_b1", "L1_attn_W2", "L1_attn_b2",
    "L1_ffn_router_w", "L1_ffn_w1", "L1_ffn_b1", "L1_ffn_w2", "L1_ffn_b2", "L1_ffn_gamma", "L1_ffn_beta",
]


def kernel(**inputs):
    from concourse import bacc
    from concourse.bass_utils import run_bass_kernel_spmd

    nc = bacc.Bacc("TRN2", target_bir_lowering=False, num_devices=1)
    arrays = {name: np.ascontiguousarray(inputs[name]) for name in _INPUTS}
    arrays.update(shape_constants())
    a = {name: nc.dram_tensor(f"in_{name}", v.shape, mybir.dt.from_np(v.dtype), kind="ExternalInput").ap()
         for name, v in arrays.items()}
    out = nc.dram_tensor("out", arrays["L0_attn_X"].shape, F32, kind="ExternalOutput").ap()
    build_program(nc, a, out)
    result = run_bass_kernel_spmd(nc, [{f"in_{name}": v for name, v in arrays.items()}], core_ids=[0])
    return result.results[0]["out"]
```

```python
from contextlib import ExitStack

import numpy as np

import concourse.bass as bass
from concourse import mybir

F32 = mybir.dt.float32
BF16 = mybir.dt.bfloat16
ALU = mybir.AluOpType
ACT = mybir.ActivationFunctionType
AX_X = mybir.AxisListType.X

P = 128
D = 128
BATCH, SEQ = 2, 1024
TILES = BATCH * SEQ // P
SEQ_TILES = SEQ // P
BLOCKS = 4
BLK = 512
FFN = 512
EXPERTS = 8

HEADS0, HDIM0 = 16, 8
SCALE0 = float(HDIM0) ** -0.5
PARTS = 3
PAIRS = [(a, b) for a in range(PARTS) for b in range(PARTS)]
MAX_ROW = len(PAIRS) * HDIM0
STACK = 96

HEADS1 = 8
GROUP = 4
BASE = 16
LEVELS = [16, 32, 64]
NEG = -1.0e30


def shape_constants():
    i = np.arange(P)
    ident = np.eye(P, dtype=np.float32)
    upper = (i[:, None] <= i[None, :]).astype(np.float32)
    below = np.where(i[:, None] <= i[None, :], 0.0, NEG).astype(np.float32)
    block_of = (i[:, None] // BASE == np.arange(P // BASE)[None, :]).astype(np.float32)
    delta = (i[:, None] % BASE == np.arange(BASE)[None, :]).astype(np.float32)
    masks = []
    for s in LEVELS:
        odd = (i.reshape(-1, 2, s)[:, 1, :]).reshape(-1)
        masks.append(((i[:, None] // s + 1) == (odd[None, :] // s)).astype(np.float32))
    iota = np.tile(np.arange(EXPERTS, dtype=np.float32), (P, 1))
    return {
        "ident": ident, "upper": upper, "below": below, "block_of": block_of, "delta": delta,
        "levels": np.concatenate(masks, axis=1), "iota": iota,
    }


class Core:

    def __init__(self, nc, ctx):
        self.nc, self.ctx = nc, ctx
        self.x = self.sb("x", [P, TILES, D])
        self.n = self.sb("n", [P, TILES, D])
        self.nT = self.sb("nT", [D, TILES * P])
        self.ident = self.sb("ident", [P, P])
        self.iota = self.sb("iota", [P, EXPERTS])
        self.norm_sems = [self.sem(f"norm_{s}") for s in (
            "stats_done", "moments_done", "shifted_done", "rstd_done", "normed", "turned_done", "kept")]
        self.norms = self.turned_norms = 0
        self.half = self.sb("half", [P, TILES])
        self.moved = self.sem("moved")
        self.chain, self.linked = self.sem("chain"), 0

    def link(self, dve, ins):
        self.linked += 1
        ins.then_inc(self.chain, 1)
        dve.wait_ge(self.chain, self.linked)

    def sb(self, name, shape, dt=F32, ctx=None):
        return (ctx or self.ctx).enter_context(self.nc.sbuf_tensor(name, shape, dt))

    def ps(self, name, shape, dt=F32, ctx=None):
        return (ctx or self.ctx).enter_context(self.nc.psum_tensor(name, shape, dt))

    def sem(self, name):
        return self.ctx.enter_context(self.nc.semaphore(name))


def layer_norm(k, tag, src, eps, tokens_out, turned_out=None, weight=None, bias=None, prefetch=None):
    nc = k.nc
    with ExitStack() as ctx:
        stats = k.sb(f"{tag}_stats", [P, TILES, 6], ctx=ctx)
        moments = k.sb(f"{tag}_moments", [P, TILES, 2], ctx=ctx)
        shifted = k.sb(f"{tag}_shifted", [P, TILES], ctx=ctx)
        rstd = k.sb(f"{tag}_rstd", [P, TILES], ctx=ctx)
        turned = k.ps(f"{tag}_turned", [P, BLOCKS, BLK], ctx=ctx)
        stats_done, moments_done, shifted_done, rstd_done, normed, turned_done, kept = k.norm_sems
        n, m = k.norms, k.turned_norms
        k.norms, k.turned_norms = n + 1, m + (turned_out is not None)
        BT = TILES // BLOCKS
        block = ctx.enter_context(nc.Block())

        if prefetch:
            @block.sync
            def _(sp):
                prefetch(sp)

        @block.vector
        def _(dve):
            def measure(blk):
                for i in range(BT * blk, BT * (blk + 1)):
                    last = nc.vector.bn_stats(stats[:, i, :], src[:, i, :])
                last.then_inc(stats_done, 1)

            def gather(blk):
                dve.wait_ge(stats_done, n * BLOCKS + blk + 1)
                for i in range(BT * blk, BT * (blk + 1)):
                    last = nc.vector.bn_aggr(moments[:, i, :], stats[:, i, :])
                last.then_inc(moments_done, 1)
                dve.wait_ge(moments_done, n * BLOCKS + blk + 1)
                nc.vector.tensor_scalar(shifted[:, BT * blk:BT * (blk + 1)], moments[:, BT * blk:BT * (blk + 1), 1], eps, None,
                                        ALU.add).then_inc(shifted_done, 1)

            def normalise(blk):
                dve.wait_ge(rstd_done, n * BLOCKS + blk + 1)
                for i in range(BT * blk, BT * (blk + 1)):
                    last = nc.vector.tensor_scalar(tokens_out[:, i, :], src[:, i, :], moments[:, i, 0:1], rstd[:, i:i + 1],
                                                   ALU.subtract, ALU.mult)
                last.then_inc(normed, 1)

            measure(0)
            for blk in range(BLOCKS):
                gather(blk)
                if blk < BLOCKS - 1:
                    measure(blk + 1)
                if blk > 0:
                    normalise(blk - 1)
            normalise(BLOCKS - 1)
            dve.wait_ge(normed, (n + 1) * BLOCKS)

        @block.gpsimd
        def _(pool):
            for blk in range(BLOCKS):
                pool.wait_ge(shifted_done, n * BLOCKS + blk + 1)
                nc.gpsimd.tensor_tensor(rstd[:, BT * blk:BT * (blk + 1)], shifted[:, BT * blk:BT * (blk + 1)],
                                        k.half[:, 0:BT], ALU.pow).then_inc(rstd_done, 1)

        if turned_out is None:
            return

        @block.tensor
        def _(pe):
            for blk in range(BLOCKS):
                pe.wait_ge(normed, n * BLOCKS + blk + 1)
                for t in range(BT):
                    mm = nc.tensor.transpose(turned[:, blk, t * P:(t + 1) * P], tokens_out[:, BT * blk + t, :], k.ident[:])
                mm.then_inc(turned_done, 1)

        @block.scalar
        def _(act):
            for blk in range(BLOCKS):
                act.wait_ge(turned_done, m * BLOCKS + blk + 1)
                nc.scalar.activation(
                    turned_out[:, blk * BLK:(blk + 1) * BLK], turned[:, blk, :], ACT.Identity,
                    bias=0.0 if bias is None else bias[:], scale=1.0 if weight is None else weight[:],
                ).then_inc(kept, 1)
            act.wait_ge(kept, (m + 1) * BLOCKS)


def start(k, a):
    nc = k.nc
    loaded, half_set = k.moved, k.sem("start_half_set")
    with nc.Block() as block:
        @block.sync
        def _(sp):
            sp.dma_start(k.x[:], a["L0_attn_X"].rearrange("b (t p) d -> p (b t) d", p=P)).then_inc(loaded, 16)
            sp.dma_start(k.ident[:], a["ident"]).then_inc(loaded, 16)
            sp.dma_start(k.iota[:], a["iota"]).then_inc(loaded, 16)
            sp.wait_ge(loaded, 48)

        @block.gpsimd
        def _(pool):
            nc.gpsimd.memset(k.half[:], -0.5).then_inc(half_set, 1)
            pool.wait_ge(half_set, 1)


def attention(k, a):
    nc = k.nc
    KB = SEQ_TILES
    PAIRS_BH = BATCH * HEADS0
    VW = 32
    parts_dram = nc.dram_tensor("parts_dram", [2, PARTS, D, BATCH * SEQ], BF16)
    max_dram = nc.dram_tensor("max_dram", [PAIRS_BH, PARTS * KB, P], BF16)

    with ExitStack() as outer:
        stack = {w: k.sb(f"{w}_stack", [STACK, PAIRS_BH, SEQ], BF16, outer) for w in "qk"}
        v_all = k.sb("v_all", [P, PAIRS_BH, KB, HDIM0], ctx=outer)
        identb = k.sb("identb", [P, P], BF16, outer)

        with ExitStack() as ctx:
            w_qkv = k.sb("w_qkv", [D, 3 * D], ctx=ctx)
            b_col = k.sb("b_col", [D, 2], ctx=ctx)
            b_v = k.sb("b_v", [P, D], ctx=ctx)
            w_in = k.sem("qkv_w_in")

            def prefetch(sp):
                sp.dma_start(w_qkv[:], a["L0_attn_W_qkv"]).then_inc(w_in, 16)
                sp.dma_start(b_col[:], a["L0_attn_b_qkv"].rearrange("(w d) -> d w", d=D)[:, 0:2],
                             allow_slow_non_contiguous=True).then_inc(w_in, 16)
                sp.dma_start(b_v[:], a["L0_attn_b_qkv"][2 * D:3 * D].partition_broadcast(P)).then_inc(w_in, 16)

            layer_norm(k, "ln0", k.x, 1e-5, k.n, k.nT, prefetch=prefetch)
            full = k.sb("full", [D, 2, BLK], ctx=ctx)
            rest = k.sb("rest", [D, 2, BLK], ctx=ctx)
            cut = k.sb("cut", [D, 2, PARTS, BLK], BF16, ctx)
            by_feature = k.ps("by_feature", [D, 2, BLK], ctx=ctx)
            v_psum = k.ps("v_psum", [P, 2, BLK], ctx=ctx)
            rows_set, projected, biased = (k.sem(f"qkv_{s}") for s in ("rows_set", "projected", "biased"))
            cut1, rest1, cut2, rest2 = (k.sem(f"qkv_{s}") for s in ("cut1", "rest1", "cut2", "rest2"))
            saved = [k.sem(f"qkv_saved{i}") for i in range(2)]
            v_done, v_kept, stacked, identb_set = (k.sem(f"qkv_{s}") for s in ("v_done", "v_kept", "stacked", "identb_set"))
            block = ctx.enter_context(nc.Block())

            @block.sync
            def _(sp):
                for step in range(2 * BLOCKS):
                    n = step % BLOCKS
                    sp.wait_ge(rest2, step + 1)
                    sp.dma_start(parts_dram[step // BLOCKS, :, :, n * BLK:(n + 1) * BLK].rearrange("s d t -> d s t"),
                                 cut[:, step % 2, :, :]).then_inc(saved[step % 2], 16)
                for par in range(2):
                    sp.wait_ge(saved[par], 16 * BLOCKS)
                for s, (pq, pk) in enumerate(PAIRS):
                    for w, part in (("q", pq), ("k", pk)):
                        if (s + 1) * HDIM0 > 64:
                            sp.wait_ge(rows_set, 2)
                        for b in range(BATCH):
                            sp.dma_start(
                                stack[w][s * HDIM0:(s + 1) * HDIM0, b * HEADS0:(b + 1) * HEADS0, :],
                                parts_dram["qk".index(w), part, :, b * SEQ:(b + 1) * SEQ].rearrange(
                                    "(h d) t -> d h t", d=HDIM0)).then_inc(stacked, 16)
                sp.wait_ge(stacked, 16 * 4 * len(PAIRS))

            @block.gpsimd
            def _(pool):
                nc.gpsimd.memset(stack["q"][64:STACK], 0.0).then_inc(rows_set, 1)
                nc.gpsimd.memset(stack["k"][64:STACK], 1.0).then_inc(rows_set, 1)
                pool.wait_ge(rows_set, 2)
                nc.gpsimd.tensor_copy(identb[:], k.ident[:]).then_inc(identb_set, 1)
                pool.wait_ge(identb_set, 1)

            @block.tensor
            def _(pe):
                pe.wait_ge(w_in, 48)
                for w in range(2):
                    for n in range(BLOCKS):
                        step = w * BLOCKS + n
                        if step >= 2:
                            pe.wait_ge(biased, step - 1)
                        nc.tensor.matmul(by_feature[:, step % 2, :], w_qkv[:, w * D:(w + 1) * D],
                                         k.nT[:, n * BLK:(n + 1) * BLK], start=True, stop=True).then_inc(projected, 1)
                for t in range(TILES):
                    if t % 4 == 0 and t >= 8:
                        pe.wait_ge(v_kept, t // 4 - 1)
                    mm = nc.tensor.matmul(v_psum[:, (t // 4) % 2, (t % 4) * D:(t % 4 + 1) * D],
                                          k.nT[:, t * P:(t + 1) * P], w_qkv[:, 2 * D:3 * D], start=True, stop=True)
                    if t % 4 == 3:
                        mm.then_inc(v_done, 1)

            @block.scalar
            def _(act):
                act.wait_ge(w_in, 48)
                for step in range(2 * BLOCKS):
                    act.wait_ge(projected, step + 1)
                    if step >= 2:
                        act.wait_ge(rest1, step - 1)
                    nc.scalar.activation(full[:, step % 2, :], by_feature[:, step % 2, :], ACT.Identity,
                                         bias=b_col[:, step // BLOCKS:step // BLOCKS + 1]).then_inc(biased, 1)

            @block.vector
            def _(dve):
                for step in range(2 * BLOCKS):
                    par = step % 2
                    dve.wait_ge(biased, step + 1)
                    if step >= 2:
                        dve.wait_ge(saved[par], 16 * (step // 2))
                    nc.vector.tensor_copy(cut[:, par, 0, :], full[:, par, :]).then_inc(cut1, 1)
                    dve.wait_ge(cut1, step + 1)
                    nc.vector.tensor_tensor(rest[:, par, :], full[:, par, :], cut[:, par, 0, :], ALU.subtract).then_inc(rest1, 1)
                    dve.wait_ge(rest1, step + 1)
                    nc.vector.tensor_copy(cut[:, par, 1, :], rest[:, par, :]).then_inc(cut2, 1)
                    dve.wait_ge(cut2, step + 1)
                    nc.vector.tensor_tensor(cut[:, par, 2, :], rest[:, par, :], cut[:, par, 1, :], ALU.subtract).then_inc(rest2, 1)
                for n in range(BLOCKS):
                    dve.wait_ge(v_done, n + 1)
                    dve.wait_ge(w_in, 48)
                    b, kb = n // 2, 4 * (n % 2)
                    for t in range(4):
                        last = nc.vector.tensor_tensor(
                            v_all[:, b * HEADS0:(b + 1) * HEADS0, kb + t, :],
                            v_psum[:, n % 2, t * D:(t + 1) * D].rearrange("p (h d) -> p h d", h=HEADS0),
                            b_v[:].rearrange("p (h d) -> p h d", h=HEADS0), ALU.add)
                    last.then_inc(v_kept, 1)
                dve.wait_ge(v_kept, BLOCKS)

        heads = k.sb("heads", [P, KB, PAIRS_BH, HDIM0], ctx=outer)
        with ExitStack() as ctx:
            v_head = k.sb("v_head", [P, 2, KB, VW], ctx=ctx)
            row_min = k.sb("row_min", [P, 2, KB, 2], ctx=ctx)
            neg_max = k.sb("neg_max", [P, 2, KB], ctx=ctx)
            zeros = k.sb("zeros", [P, KB * HDIM0], ctx=ctx)
            max_rest = k.sb("max_rest", [P, 2, KB], ctx=ctx)
            max_cut = k.sb("max_cut", [P, 2, PARTS, KB], BF16, ctx)
            max_rows = k.sb("max_rows", [PARTS * KB, 2, P], BF16, ctx)
            probs = k.sb("probs", [P, 2, SEQ], ctx=ctx)
            sums = k.sb("sums", [P, 2, 2 * P], ctx=ctx)
            recip = k.sb("recip", [P, 2, 2, 4], ctx=ctx)
            first = k.ps("first", [P, 2, BLK], ctx=ctx)
            scores = k.ps("scores", [P, 2, SEQ], ctx=ctx)
            summed = k.ps("summed", [P, BLK], ctx=ctx)
            turn = k.ps("turn", [P, BLK], ctx=ctx)
            turn_b = turn[:].bitcast(BF16)
            turn_q = turn[:, 0:2 * P].rearrange("p (half c w) -> p half c w", half=2, c=4)
            (first_ready, first_read, joined, m1, r1, m2, r2, m3, rows_turned, rows_kept, rows_out, rows_in, v_zeroed, v_ready,
             scores_ready, probs_ready, probs_used, sums_kept, sums_turned, recip_done, head_done) = (
                k.sem(f"att_{s}") for s in (
                    "first_ready", "first_read", "joined", "m1", "r1", "m2", "r2", "m3", "rows_turned", "rows_kept",
                    "rows_out", "rows_in", "v_zeroed", "v_ready", "scores_ready", "probs_ready", "probs_used",
                    "sums_kept", "sums_turned", "recip_done", "head_done"))
            block = ctx.enter_context(nc.Block())
            LOOPS = PAIRS_BH // 2

            def over_heads(eng, step):
                step(0, True)
                with eng.Fori(1, LOOPS - 1) as r:
                    step(r, True)
                step(LOOPS - 1, False)

            @block.tensor
            def _(pe):
                def find_max(j, t):
                    for half in range(2):
                        n = 2 * (KB * j + t) + half
                        if not (isinstance(n, int) and n < 2):
                            pe.wait_ge(first_read, n - 1)
                        nc.tensor.matmul(first[:, half, :], stack["q"][:, j, t * P:(t + 1) * P],
                                         stack["k"][:, j, half * BLK:(half + 1) * BLK],
                                         start=True, stop=True).then_inc(first_ready, 1)

                def turn_max(j, par):
                    pe.wait_ge(m3, j + 1)
                    if not (isinstance(j, int) and j < 3):
                        pe.wait_ge(head_done, j - 2)
                    if not (isinstance(j, int) and j < 1):
                        pe.wait_ge(rows_kept, j)
                    nc.tensor.transpose(turn_b[0:PARTS * KB, 0:P], max_cut[:, par].rearrange("p s t -> p (s t)"),
                                        identb[:]).then_inc(rows_turned, 1)

                def scores_of(i, kb):
                    n = KB * i + kb
                    if not (isinstance(n, int) and n < 2):
                        pe.wait_ge(probs_ready, n - 1)
                    for half in range(2):
                        mm = nc.tensor.matmul(scores[:, kb % 2, half * BLK:(half + 1) * BLK],
                                              stack["k"][:, i, kb * P:(kb + 1) * P],
                                              stack["q"][:, i, half * BLK:(half + 1) * BLK], start=True, stop=True)
                    mm.then_inc(scores_ready, 1)

                def sum_values(i, par, kb):
                    if kb == 0:
                        pe.wait_ge(v_ready, i + 1)
                        if not (isinstance(i, int) and i < 1):
                            pe.wait_ge(sums_kept, i)
                    pe.wait_ge(probs_ready, KB * i + kb + 1)
                    for c in range(4):
                        mm = nc.tensor.matmul(summed[VW * c:VW * (c + 1), 0:2 * P], v_head[:, par, kb, :],
                                              probs[:, kb % 2, c * 2 * P:(c + 1) * 2 * P],
                                              start=(kb == 0), stop=(kb == KB - 1))
                    mm.then_inc(probs_used, 1)

                def turn_sums(i, par, rows):
                    pe.wait_ge(sums_kept, i + 1)
                    pe.wait_ge(rows_kept, rows)
                    if not (isinstance(i, int) and i < 1):
                        pe.wait_ge(head_done, i)
                    for half in range(2):
                        mm = nc.tensor.transpose(turn[:, half * P:(half + 1) * P], sums[:, par, half * P:(half + 1) * P],
                                                 k.ident[:])
                    mm.then_inc(sums_turned, 1)

                def step(r, ahead):
                    for par in range(2):
                        i = 2 * r + par
                        pe.wait_ge(rows_in, 16 * i + 16)
                        for kb in range(KB):
                            if ahead:
                                find_max(i + 2, kb)
                            scores_of(i, kb)
                            if kb >= 1:
                                sum_values(i, par, kb - 1)
                            if kb == 1 and (ahead or par == 0):
                                turn_max(i + 1, 1 - par)
                            if kb == 3 and not (isinstance(i, int) and i == 0):
                                turn_sums(i - 1, 1 - par, i + 2 if (ahead or par == 0) else PAIRS_BH)
                        sum_values(i, par, KB - 1)

                for j in range(2):
                    for t in range(KB):
                        find_max(j, t)
                turn_max(0, 0)
                over_heads(pe, step)
                turn_sums(PAIRS_BH - 1, 1, PAIRS_BH)

            @block.vector
            def _(dve):
                def find_max(j, par, t):
                    if t == 0 and not (isinstance(j, int) and j < 2):
                        dve.wait_ge(joined, j - 1)
                    for half in range(2):
                        dve.wait_ge(first_ready, 2 * (KB * j + t) + half + 1)
                        nc.vector.tensor_reduce(row_min[:, par, t, half:half + 1], first[:, half, :], AX_X, ALU.max,
                                                negate=True).then_inc(first_read, 1)

                def join(j, par):
                    dve.wait_ge(first_read, 2 * KB * (j + 1))
                    if not (isinstance(j, int) and j < 2):
                        dve.wait_ge(m3, j - 1)
                    nc.vector.tensor_reduce(neg_max[:, par, :], row_min[:, par], AX_X, ALU.min).then_inc(joined, 1)

                def keep_rows(j, par):
                    dve.wait_ge(rows_turned, j + 1)
                    if not (isinstance(j, int) and j < 2):
                        dve.wait_ge(rows_out, 16 * j - 16)
                    nc.vector.tensor_copy(max_rows[:, par, :], turn_b[0:PARTS * KB, 0:P]).then_inc(rows_kept, 1)

                def divide(i, par):
                    dve.wait_ge(sums_turned, i + 1)
                    if not (isinstance(i, int) and i < 2):
                        dve.wait_ge(head_done, i - 1)
                    nc.vector.reciprocal(recip[:, par], turn_q[:, :, :, HDIM0]).then_inc(recip_done, 1)
                    dve.wait_ge(recip_done, i + 1)
                    nc.vector.tensor_tensor(
                        heads[:, :, i, :].rearrange("p (c half) d -> p half c d", half=2), turn_q[:, :, :, 0:HDIM0],
                        recip[:, par].unsqueeze(3).broadcast_to([P, 2, 4, HDIM0]), ALU.mult).then_inc(head_done, 1)

                def step(r, ahead):
                    for par in range(2):
                        i = 2 * r + par
                        for kb in range(KB):
                            if ahead:
                                find_max(i + 2, par, kb)
                            if kb == 2 and (ahead or par == 0):
                                keep_rows(i + 1, 1 - par)
                            if kb == 5 and not (isinstance(i, int) and i == 0):
                                divide(i - 1, 1 - par)
                        if ahead:
                            join(i + 2, par)

                for j in range(2):
                    for t in range(KB):
                        find_max(j, j, t)
                    join(j, j)
                keep_rows(0, 0)
                over_heads(dve, step)
                divide(PAIRS_BH - 1, 1)
                dve.wait_ge(head_done, PAIRS_BH)

            @block.scalar
            def _(act):
                def keep_sums(i, par):
                    act.wait_ge(probs_used, KB * (i + 1))
                    if not (isinstance(i, int) and i < 2):
                        act.wait_ge(sums_turned, i - 1)
                    nc.scalar.copy(sums[:, par, :], summed[:, 0:2 * P]).then_inc(sums_kept, 1)

                def rows_to_dram(j, par):
                    act.wait_ge(rows_kept, j + 1)
                    act.dma_start(max_dram[j], max_rows[:, par, :]).then_inc(rows_out, 16)

                def rows_to_stack(j):
                    act.wait_ge(rows_out, 16 * j + 16)
                    if not (isinstance(j, int) and j < 1):
                        act.wait_ge(rows_in, 16 * j)
                    act.dma_start(stack["q"][MAX_ROW:MAX_ROW + PARTS, j, :],
                                  max_dram[j].rearrange("(s t) q -> s (t q)", s=PARTS)).then_inc(rows_in, 16)

                def step(r, ahead):
                    for par in range(2):
                        i = 2 * r + par
                        for kb in range(KB):
                            if kb == 3 and (ahead or par == 0):
                                rows_to_dram(i + 1, 1 - par)
                            if kb == 5 and (ahead or par == 0):
                                rows_to_stack(i + 1)
                            n = KB * i + kb
                            act.wait_ge(scores_ready, n + 1)
                            if not (isinstance(n, int) and n < 2):
                                act.wait_ge(probs_used, n - 1)
                            nc.scalar.activation(probs[:, kb % 2, :], scores[:, kb % 2, :], ACT.Exp,
                                                 scale=SCALE0).then_inc(probs_ready, 1)
                            if kb == 0 and not (isinstance(i, int) and i == 0):
                                keep_sums(i - 1, 1 - par)

                rows_to_dram(0, 0)
                rows_to_stack(0)
                over_heads(act, step)
                keep_sums(PAIRS_BH - 1, 1)

            @block.gpsimd
            def _(pool):
                def cut_max(j, par):
                    pool.wait_ge(joined, j + 1)
                    if not (isinstance(j, int) and j < 2):
                        pool.wait_ge(rows_turned, j - 1)
                    nc.gpsimd.tensor_tensor(max_cut[:, par, 0, :], neg_max[:, par, :], zeros[:, 0:KB], ALU.add).then_inc(m1, 1)
                    pool.wait_ge(m1, j + 1)
                    nc.gpsimd.tensor_tensor(max_rest[:, par, :], neg_max[:, par, :], max_cut[:, par, 0, :],
                                            ALU.subtract).then_inc(r1, 1)
                    pool.wait_ge(r1, j + 1)
                    nc.gpsimd.tensor_tensor(max_cut[:, par, 1, :], max_rest[:, par, :], zeros[:, 0:KB], ALU.add).then_inc(m2, 1)
                    pool.wait_ge(m2, j + 1)
                    nc.gpsimd.tensor_tensor(max_cut[:, par, 2, :], max_rest[:, par, :], max_cut[:, par, 1, :],
                                            ALU.subtract).then_inc(m3, 1)

                def take_values(i, par):
                    if not (isinstance(i, int) and i < 2):
                        pool.wait_ge(probs_used, KB * (i - 1))
                    nc.gpsimd.tensor_tensor(v_head[:, par, :, 0:HDIM0], v_all[:, i],
                                            zeros[:].rearrange("p (t d) -> p t d", t=KB), ALU.add).then_inc(v_ready, 1)

                def step(r, ahead):
                    for par in range(2):
                        i = 2 * r + par
                        take_values(i, par)
                        if ahead:
                            cut_max(i + 2, par)

                nc.gpsimd.memset(v_head[:], 0.0).then_inc(v_zeroed, 1)
                pool.wait_ge(v_zeroed, 1)
                nc.gpsimd.memset(v_head[:, :, :, HDIM0:HDIM0 + 1], 1.0).then_inc(v_zeroed, 1)
                nc.gpsimd.memset(zeros[:], 0.0).then_inc(v_zeroed, 1)
                pool.wait_ge(v_zeroed, 3)
                for j in range(2):
                    cut_max(j, j)
                over_heads(pool, step)

        with ExitStack() as ctx:
            w_proj = k.sb("w_proj", [D, D], ctx=ctx)
            b_proj = k.sb("b_proj", [P, D], ctx=ctx)
            heads_T = k.sb("heads_T", [P, TILES, P], ctx=ctx)
            turned = k.ps("proj_turned", [P, 4, BLK], ctx=ctx)
            out = k.ps("proj_out", [P, 4, BLK], ctx=ctx)
            w_in, turned_done, kept, out_done, bias_added, done = (
                k.sem(f"proj_{s}") for s in ("w_in", "turned_done", "kept", "out_done", "bias_added", "done"))
            block = ctx.enter_context(nc.Block())

            @block.sync
            def _(sp):
                sp.dma_start(w_proj[:], a["L0_attn_W_proj"]).then_inc(w_in, 16)
                sp.dma_start(b_proj[:], a["L0_attn_b_proj"].partition_broadcast(P)).then_inc(w_in, 16)

            @block.tensor
            def _(pe):
                for t in range(TILES):
                    b, kb = t // KB, t % KB
                    mm = nc.tensor.transpose(turned[:, t // 4, (t % 4) * P:(t % 4 + 1) * P],
                                             heads[:, kb, b * HEADS0:(b + 1) * HEADS0, :], k.ident[:])
                    if t % 4 == 3:
                        mm.then_inc(turned_done, 1)
                pe.wait_ge(w_in, 32)
                for t in range(TILES):
                    pe.wait_ge(kept, t // 4 + 1)
                    mm = nc.tensor.matmul(out[:, t // 4, (t % 4) * P:(t % 4 + 1) * P], heads_T[:, t, :], w_proj[:],
                                          start=True, stop=True)
                    if t % 4 == 3:
                        mm.then_inc(out_done, 1)

            @block.scalar
            def _(act):
                for n in range(BLOCKS):
                    act.wait_ge(turned_done, n + 1)
                    nc.scalar.copy(heads_T[:, 4 * n:4 * n + 4, :], turned[:, n, :].rearrange("p (t q) -> p t q", t=4)).then_inc(kept, 1)

            @block.vector
            def _(dve):
                dve.wait_ge(w_in, 32)
                nc.vector.tensor_tensor(k.x[:], k.x[:], b_proj[:].unsqueeze(1).broadcast_to([P, TILES, D]),
                                        ALU.add).then_inc(bias_added, 1)
                dve.wait_ge(bias_added, 1)
                for n in range(BLOCKS):
                    dve.wait_ge(out_done, n + 1)
                    nc.vector.tensor_tensor(k.x[:, 4 * n:4 * n + 4, :], out[:, n, :].rearrange("p (t d) -> p t d", t=4),
                                            k.x[:, 4 * n:4 * n + 4, :], ALU.add).then_inc(done, 1)
                dve.wait_ge(done, BLOCKS)


class HiddenWeights:

    def __init__(self, k, tag, ctx, loads, loads_per, experts):
        self.loads, self.loads_per, self.experts = loads, loads_per, experts
        self.pars = min(experts, 2)
        self.w1 = k.sb(f"{tag}_w1", [D, self.pars, FFN], ctx=ctx)
        self.w2 = k.sb(f"{tag}_w2", [P, self.pars, FFN // P, D], ctx=ctx)
        self.b1 = k.sb(f"{tag}_b1", [P, self.pars, FFN // P], ctx=ctx)
        self.loaded = [k.sem(f"{tag}_loaded{i}") for i in range(self.pars)]

    def load(self, sp, e):
        par = e % 2
        for dst, src in self.loads(e, par, self.w1[:, par], self.w2[:, par], self.b1[:, par]):
            sp.dma_start(dst, src, allow_slow_non_contiguous=True).then_inc(self.loaded[par], 16)

    def load_first(self, sp):
        for par in range(self.pars):
            self.load(sp, par)


def feed_forward(k, tag, weights, func, has_bias, finish):
    nc = k.nc
    FC = FFN // P
    experts, pars, loads_per = weights.experts, weights.pars, weights.loads_per
    w1, w2, b1, loaded = weights.w1, weights.w2, weights.b1, weights.loaded
    with ExitStack() as ctx:
        hidden = k.sb(f"{tag}_hidden", [P, 2, FC, BLK], ctx=ctx)
        up = k.ps(f"{tag}_up", [P, FC, BLK], ctx=ctx)
        down = k.ps(f"{tag}_down", [P, 2, BLK], ctx=ctx)
        up_ready, hidden_ready, down_ready, down_read = (
            k.sem(f"{tag}_{s}") for s in ("up_ready", "hidden_ready", "down_ready", "down_read"))

        def weights_in(eng, r, par):
            eng.wait_ge(loaded[par], 16 * loads_per * (r + 1))

        parts = finish(ctx, down, down_ready, down_read, weights_in)
        block = ctx.enter_context(nc.Block())

        def over_experts(eng, body):
            for par in range(pars):
                body(0, par)
            if experts > 2:
                with eng.Fori(1, experts // 2) as r:
                    for par in range(2):
                        body(r, par)

        @block.sync
        def _(sp):
            for e in range(2, experts):
                sp.wait_ge(down_ready, BLOCKS * (e - 1))
                parts["used"](sp, e - 2)
                weights.load(sp, e)

        @block.tensor
        def _(pe):
            def body(r, par):
                weights_in(pe, r, par)
                for blk in range(BLOCKS):
                    m = (pars * r + par) * BLOCKS + blk
                    for f in range(FC):
                        if not (isinstance(m, int) and m == 0):
                            pe.wait_ge(hidden_ready, FC * (m - 1) + f + 1)
                        nc.tensor.matmul(up[:, f, :], w1[:, par, f * P:(f + 1) * P], k.nT[:, blk * BLK:(blk + 1) * BLK],
                                         start=True, stop=True).then_inc(up_ready, 1)
                    if not (isinstance(m, int) and m < 2):
                        pe.wait_ge(down_read, m - 1)
                    for f in range(FC):
                        pe.wait_ge(hidden_ready, FC * m + f + 1)
                        for t in range(4):
                            mm = nc.tensor.matmul(down[:, blk % 2, t * D:(t + 1) * D], hidden[:, blk % 2, f, t * P:(t + 1) * P],
                                                  w2[:, par, f, :], start=(f == 0 and t == 0), stop=(f == FC - 1),
                                                  skip_group_check=True)
                    mm.then_inc(down_ready, 1)

            over_experts(pe, body)

        @block.scalar
        def _(act):
            def body(r, par):
                weights_in(act, r, par)
                for blk in range(BLOCKS):
                    m = (pars * r + par) * BLOCKS + blk
                    if not (isinstance(m, int) and m < 2):
                        act.wait_ge(down_ready, m - 1)
                    for f in range(FC):
                        act.wait_ge(up_ready, FC * m + f + 1)
                        nc.scalar.activation(hidden[:, blk % 2, f, :], up[:, f, :], func,
                                             bias=b1[:, par, f:f + 1] if has_bias else 0.0).then_inc(hidden_ready, 1)

            over_experts(act, body)

        @block.vector
        def _(dve):
            parts["vector"](dve)

        @block.gpsimd
        def _(pool):
            if "gpsimd" in parts:
                parts["gpsimd"](pool)


def top_two(k, tag, ctx, logits):
    nc = k.nc
    W = [P, TILES, EXPERTS]
    b = {s: k.sb(f"{tag}_{s}", W, ctx=ctx) for s in ("at_top", "index", "hot1", "hot2", "others")}
    v = {s: k.sb(f"{tag}_{s}", [P, TILES], ctx=ctx) for s in ("top1", "top2", "index1", "index2")}

    def wide(x):
        return x[:].unsqueeze(2).broadcast_to(W)

    def steps(dve):
        iota = k.iota[:].unsqueeze(1).broadcast_to(W)
        source = logits
        for top, index, hot in (("top1", "index1", "hot1"), ("top2", "index2", "hot2")):
            k.link(dve, nc.vector.tensor_reduce(v[top][:], source[:], AX_X, ALU.max))
            k.link(dve, nc.vector.tensor_tensor(b["at_top"][:], source[:], wide(v[top]), ALU.is_lt))
            k.link(dve, nc.vector.scalar_tensor_tensor(b["index"][:], b["at_top"][:], 2.0 * EXPERTS, iota, ALU.mult, ALU.add))
            k.link(dve, nc.vector.tensor_reduce(v[index][:], b["index"][:], AX_X, ALU.min))
            k.link(dve, nc.vector.tensor_tensor(b[hot][:], iota, wide(v[index]), ALU.is_equal))
            if source is logits:
                k.link(dve, nc.vector.scalar_tensor_tensor(b["others"][:], b[hot][:], -3.0e38, logits[:], ALU.mult, ALU.add))
                source = b["others"]

    return b, v, steps


def feed_forward0(k, a):
    nc = k.nc
    with ExitStack() as ctx:
        gate_w = k.sb("f0_gate_w", [D, EXPERTS], ctx=ctx)
        logits = k.sb("f0_logits", [P, TILES, EXPERTS], ctx=ctx)
        shifted = k.sb("f0_shifted", [P, TILES, EXPERTS], ctx=ctx)
        expd = k.sb("f0_expd", [P, TILES, EXPERTS], ctx=ctx)
        picked = k.sb("f0_picked", [P, TILES, EXPERTS], ctx=ctx)
        total, total_r, g1, g2, both, denom, denom_r, coef1, coef2, coef = (
            k.sb(f"f0_{s}", [P, TILES], ctx=ctx)
            for s in ("total", "total_r", "g1", "g2", "both", "denom", "denom_r", "coef1", "coef2", "coef"))
        w_in, logits_done, shifted_done, expd_done = (
            k.sem(f"f0_{s}") for s in ("w_in", "logits_done", "shifted_done", "expd_done"))
        hot, top, steps = top_two(k, "f0", ctx, logits)

        def loads(e, par, w1, w2, b1):
            return [(w1, a["L0_ffn_w1"]), (w2, a["L0_ffn_w2"].rearrange("(f p) d -> p f d", p=P))]

        weights = HiddenWeights(k, "f0", ctx, loads, 2, 1)

        def prefetch(sp):
            sp.dma_start(gate_w[:], a["L0_ffn_Wg"]).then_inc(w_in, 16)
            weights.load_first(sp)

        layer_norm(k, "ln1", k.x, 1e-5, k.n, k.nT, prefetch=prefetch)
        with ExitStack() as inner:
            gates = k.ps("f0_gates", [P, TILES, EXPERTS], ctx=inner)
            block = inner.enter_context(nc.Block())

            @block.tensor
            def _(pe):
                pe.wait_ge(w_in, 16)
                for t in range(TILES):
                    mm = nc.tensor.matmul(gates[:, t, :], k.nT[:, t * P:(t + 1) * P], gate_w[:], start=True, stop=True)
                mm.then_inc(logits_done, 1)

            @block.scalar
            def _(act):
                act.wait_ge(shifted_done, 1)
                nc.scalar.activation(expd[:], shifted[:], ACT.Exp).then_inc(expd_done, 1)

            @block.vector
            def _(dve):
                W = [P, TILES, EXPERTS]
                dve.wait_ge(logits_done, 1)
                k.link(dve, nc.vector.tensor_copy(logits[:], gates[:]))
                steps(dve)
                nc.vector.tensor_tensor(shifted[:], logits[:], top["top1"][:].unsqueeze(2).broadcast_to(W),
                                        ALU.subtract).then_inc(shifted_done, 1)
                dve.wait_ge(expd_done, 1)

                k.link(dve, nc.vector.tensor_reduce(total[:], expd[:], AX_X, ALU.add))
                k.link(dve, nc.vector.reciprocal(total_r[:], total[:]))
                for h, g in (("hot1", g1), ("hot2", g2)):
                    k.link(dve, nc.vector.tensor_tensor(picked[:], expd[:], hot[h][:], ALU.mult))
                    k.link(dve, nc.vector.tensor_reduce(g[:], picked[:], AX_X, ALU.add))
                    k.link(dve, nc.vector.tensor_tensor(g[:], g[:], total_r[:], ALU.mult))
                k.link(dve, nc.vector.tensor_tensor(both[:], g1[:], g2[:], ALU.add))
                k.link(dve, nc.vector.tensor_scalar(denom[:], both[:], float(np.finfo(np.float32).eps), None, ALU.max))
                k.link(dve, nc.vector.reciprocal(denom_r[:], denom[:]))
                k.link(dve, nc.vector.tensor_tensor(coef1[:], g1[:], denom_r[:], ALU.mult))
                k.link(dve, nc.vector.tensor_tensor(coef2[:], g2[:], denom_r[:], ALU.mult))
                k.link(dve, nc.vector.tensor_tensor(coef[:], coef1[:], coef2[:], ALU.add))

        def finish(ctx, down, down_ready, down_read, weights_in):
            def vector(dve):
                for blk in range(BLOCKS):
                    dve.wait_ge(down_ready, blk + 1)
                    for t in range(4):
                        i = 4 * blk + t
                        mm = nc.vector.scalar_tensor_tensor(k.x[:, i, :], down[:, blk % 2, t * D:(t + 1) * D], coef[:, i:i + 1],
                                                            k.x[:, i, :], ALU.mult, ALU.add)
                    mm.then_inc(down_read, 1)
                dve.wait_ge(down_read, BLOCKS)

            return {"vector": vector}

        feed_forward(k, "f0", weights, ACT.Relu, False, finish)


def delta_layer(k, a):
    nc = k.nc
    H, B = HEADS1, BATCH
    CHUNKS = SEQ_TILES
    GATES = TILES * H
    UNITS = [(b, g) for b in range(B) for g in range(H // GROUP)]
    NU = len(UNITS)
    W = GROUP * P
    NLEV = len(LEVELS)
    HALF = P // 2

    with ExitStack() as outer:
        mixed = k.sb("mixed", [P, TILES, D], ctx=outer)
        normT = k.nT
        rows = {s: k.sb(f"d_{s}", [D, 1], ctx=outer) for s in ("ln1_w", "ln1_b", "ln2_w", "ln2_b")}
        rows_in = k.sem("d_rows_in")
        with ExitStack() as gated:
            names = ("log_a", "summed", "neg_summed", "beta", "neg_beta", "grown", "neg_beta_grown", "rest", "last")
            all_gates = k.sb("d_all_gates", [P, TILES, len(names), H], ctx=gated)
            gate = {s: all_gates[:, :, i, :] for i, s in enumerate(names)}
            upper = k.sb("d_upper", [P, P], ctx=gated)
            ones = k.sb("d_ones", [P, P], ctx=gated)
            w_ab = k.sb("d_w_ab", [D, 2, H], ctx=gated)
            w_qkv = k.sb("g_w_qkv", [D, 3, H * P], ctx=gated)
            w_o = k.sb("g_w_o", [P, H, D], ctx=gated)
            level_masks = k.sb("g_level_masks", [P, NLEV, HALF], ctx=gated)
            block_of = k.sb("g_block_of", [P, P // BASE], ctx=gated)
            delta = k.sb("g_delta", [P, BASE], ctx=gated)
            below = k.sb("g_below", [P, P], ctx=gated)
            w_in, weights_in = k.sem("d_w_in"), k.sem("g_weights_in")

            def prefetch(sp):
                for s, t in rows.items():
                    sp.dma_start(t[:], a[f"L1_attn_{s}"].rearrange("(d o) -> d o", o=1)).then_inc(rows_in, 16)
                sp.dma_start(w_ab[:, 0, :], a["L1_attn_Wa"]).then_inc(w_in, 16)
                sp.dma_start(w_ab[:, 1, :], a["L1_attn_Wb"]).then_inc(w_in, 16)
                sp.dma_start(upper[:], a["upper"]).then_inc(w_in, 16)
                for i, w in enumerate(("Wq", "Wk", "Wv")):
                    sp.dma_start(w_qkv[:, i, :], a[f"L1_attn_{w}"]).then_inc(weights_in, 16)
                sp.dma_start(w_o[:], a["L1_attn_Wo"].rearrange("(h v) d -> v h d", v=P)).then_inc(weights_in, 16)
                sp.dma_start(level_masks[:], a["levels"].rearrange("p (l c) -> p l c", l=NLEV)).then_inc(weights_in, 16)
                sp.dma_start(block_of[:], a["block_of"]).then_inc(weights_in, 16)
                sp.dma_start(delta[:], a["delta"]).then_inc(weights_in, 16)
                sp.dma_start(below[:], a["below"]).then_inc(weights_in, 16)
                sp.wait_ge(rows_in, 64)

            layer_norm(k, "ln2", k.x, 1e-5, k.n, prefetch=prefetch)
            layer_norm(k, "ln3", k.n, 1e-5, mixed, normT, rows["ln1_w"], rows["ln1_b"])

            with ExitStack() as ctx:
                z = k.sb("d_z", [P, 2, TILES, H], ctx=ctx)
                size, soft, tmp = (k.sb(f"d_{s}", [P, 2, TILES, H], ctx=ctx) for s in ("size", "soft", "tmp"))
                logits = k.ps("d_logits", [P, TILES, 2 * H], ctx=ctx)
                sums = k.ps("d_sums", [P, 2, BLK], ctx=ctx)
                z_done, operands, taken, ones_set, log_a_done, sums_done, done = (
                    k.sem(f"d_{s}") for s in ("z_done", "operands", "taken", "ones_set", "log_a_done", "sums_done", "gates_done"))
                block = ctx.enter_context(nc.Block())

                @block.gpsimd
                def _(pool):
                    nc.gpsimd.memset(ones[:], 1.0).then_inc(ones_set, 1)
                    pool.wait_ge(ones_set, 1)

                @block.tensor
                def _(pe):
                    pe.wait_ge(w_in, 48)
                    for t in range(TILES):
                        mm = nc.tensor.matmul(logits[:, t, :], normT[:, t * P:(t + 1) * P], w_ab[:].rearrange("d w h -> d (w h)"),
                                              start=True, stop=True)
                    mm.then_inc(z_done, 1)
                    pe.wait_ge(log_a_done, 1)
                    pe.wait_ge(ones_set, 1)
                    log_a = gate["log_a"]
                    nc.tensor.matmul(sums[:, 0, 0:GATES].rearrange("p (t h) -> p t h", h=H), upper[:], log_a, start=True, stop=True)
                    nc.tensor.matmul(sums[:, 1, 0:GATES].rearrange("p (t h) -> p t h", h=H), ones[:], log_a, start=True, stop=True).then_inc(sums_done, 1)

                @block.scalar
                def _(act):
                    act.wait_ge(operands, 1)
                    nc.scalar.activation(soft[:], size[:], ACT.Exp, scale=-1.0).then_inc(taken, 1)
                    act.wait_ge(operands, 2)
                    nc.scalar.activation(tmp[:, 0], size[:, 0], ACT.Ln).then_inc(taken, 1)
                    act.wait_ge(operands, 3)
                    nc.scalar.activation(gate["grown"], gate["summed"], ACT.Exp).then_inc(taken, 1)
                    nc.scalar.activation(gate["rest"], z[:, 0], ACT.Exp).then_inc(taken, 1)
                    nc.scalar.activation(gate["last"], size[:, 1], ACT.Exp).then_inc(taken, 1)

                @block.vector
                def _(dve):
                    dve.wait_ge(z_done, 1)
                    k.link(dve, nc.vector.tensor_copy(z[:], logits[:].rearrange("p t (w h) -> p w t h", w=2)))
                    k.link(dve, nc.vector.tensor_scalar(tmp[:], z[:], -1.0, None, ALU.mult))
                    nc.vector.tensor_tensor(size[:], z[:], tmp[:], ALU.max).then_inc(operands, 1)
                    dve.wait_ge(taken, 1)
                    k.link(dve, nc.vector.tensor_scalar(size[:], soft[:], 1.0, None, ALU.add))
                    nc.vector.tensor_scalar(z[:, 0], z[:, 0], 0.0, None, ALU.min).then_inc(operands, 1)
                    k.link(dve, nc.vector.reciprocal(tmp[:, 1], size[:, 1]))
                    k.link(dve, nc.vector.tensor_scalar(z[:, 1], z[:, 1], 0.0, None, ALU.is_ge))
                    k.link(dve, nc.vector.tensor_tensor(soft[:, 1], soft[:, 1], z[:, 1], ALU.max))
                    k.link(dve, nc.vector.tensor_tensor(gate["beta"], soft[:, 1], tmp[:, 1], ALU.mult))
                    k.link(dve, nc.vector.tensor_scalar(gate["neg_beta"], gate["beta"], -1.0, None, ALU.mult))
                    dve.wait_ge(taken, 2)
                    nc.vector.tensor_tensor(gate["log_a"], z[:, 0], tmp[:, 0], ALU.subtract).then_inc(log_a_done, 1)
                    dve.wait_ge(sums_done, 1)
                    dve.wait_ge(log_a_done, 1)
                    k.link(dve, nc.vector.tensor_copy(gate["summed"], sums[:, 0, 0:GATES].rearrange("p (t h) -> p t h", h=H)))
                    k.link(dve, nc.vector.tensor_copy(size[:, 1].rearrange("p t h -> p (t h)"), sums[:, 1, 0:GATES]))
                    k.link(dve, nc.vector.tensor_scalar(gate["neg_summed"], gate["summed"], -1.0, None, ALU.mult))
                    nc.vector.tensor_tensor(z[:, 0], size[:, 1], gate["summed"], ALU.subtract).then_inc(operands, 1)
                    dve.wait_ge(taken, 5)
                    nc.vector.tensor_tensor(gate["neg_beta_grown"], gate["neg_beta"], gate["grown"], ALU.mult).then_inc(done, 1)
                    dve.wait_ge(done, 1)

            with ExitStack() as ctx:
                NG = H // GROUP
                NB = P // BASE
                blocks_dram = nc.dram_tensor("blocks_dram", [B, H, NB, BASE, BASE], F32)
                inverse = k.sb("g_inverse", [P, NB, BASE], ctx=ctx)
                rows_of = k.sb("g_rows_of", [P, NB, BASE * BASE], ctx=ctx)
                products = k.sb("g_products", [P, NB, BASE], ctx=ctx)
                below_b = k.sb("g_below_b", [P, GROUP, P], BF16, ctx)
                identb = k.sb("g_identb", [P, P], BF16, ctx)
                chunk_T = k.sb("g_chunk_T", [D, B, P], ctx=ctx)
                chunk_gates = k.sb("g_chunk_gates", [P, B, len(names), H], ctx=ctx)
                state, kt, v, kT, qT, qgT, decay = (k.sb(f"g_{s}", [P, B, NG, W], ctx=ctx)
                                                    for s in ("state", "kt", "v", "kT", "qT", "qgT", "decay"))
                q, qg, kk, q_sq, k_sq, spread = (k.sb(f"g_{s}", [P, NG, W], ctx=ctx)
                                                 for s in ("q", "qg", "k", "q_sq", "k_sq", "spread"))
                squares, shifted, inv_norm = (k.sb(f"g_{s}", [P, NG, 2 * GROUP], ctx=ctx) for s in ("squares", "shifted", "inv_norm"))
                raw, attend, coupling, solve_T, solve, update, out_T = (
                    k.sb(f"g_{s}", [P, NG, W], ctx=ctx)
                    for s in ("raw", "attend", "coupling", "solve_T", "solve", "update", "out_T"))
                partial = k.sb("g_partial", [P, NG, GROUP * HALF], ctx=ctx)
                front_bank = k.ps("g_front_bank", [P, 2, NG, W], ctx=ctx)
                back_bank = k.ps("g_back_bank", [P, 2, NG, W], ctx=ctx)

                sem_names = (
                    "consts_set",
                    "chunk_ready", "q_proj", "k_proj", "v_proj", "q_silu", "k_silu", "v_silu",
                    "squared", "squares_done", "shifted_done", "norm_done", "k_done", "q_done", "qg_done", "v_done",
                    "spread_done", "kT_turned", "kT_kept", "qT_turned", "qT_kept", "qgT_turned", "qgT_kept", "decay_sum", "decay_done",
                    "kk_done", "raw_done", "kq_done", "attend_done", "coup_turned", "coup_done", "blocks_out", "blocks_in",
                    "solved", "inverse_turned", "base_done",
                    "solve_turned", "solve_kept", "m_done", "m_read", "n_done", "n_read", "t_turned", "t_kept",
                    "ks_done", "v_ready", "u_done", "u_kept", "o_done", "o_kept", "ds_done", "state_done", "wo_done", "mixed_done")
                s_ = {n: k.sem(f"g_{n}") for n in sem_names}
                block = ctx.enter_context(nc.Block())
                WEIGHTS = 16 * 8

                SOLVE_STEPS = 2 * BASE

                def heads4(t):
                    return t.rearrange("p (h c) -> p h c", h=GROUP)

                def wide(col):
                    return col.unsqueeze(2).broadcast_to([P, GROUP, P])

                def spread4(mask):
                    return mask.unsqueeze(1).broadcast_to([P, GROUP, mask.shape[-1]])

                def odd(t, s):
                    return t.rearrange("p (n two s) -> p n two s", two=2, s=s)[:, :, 1, :]

                def columns(t, col, s):
                    return t[:, col:col + s] if len(t.shape) == 2 else t[:, col // s, :]

                def head(t, h):
                    return t[:, h * P:(h + 1) * P]

                def cols(name, b, g):
                    return chunk_gates[:, b, names.index(name), g * GROUP:(g + 1) * GROUP]

                def waiter(eng):
                    def w(name, c, b, g, back=0):
                        n = NG * (B * c + b - back) + g + 1
                        if not (isinstance(n, int) and n <= 0):
                            eng.wait_ge(s_[name], n)
                    return w

                def level_waiter(eng):
                    def w(name, c, b, g, lev, levels=NLEV):
                        eng.wait_ge(s_[name], NG * (levels * (B * c + b) + lev) + g + 1)
                    return w

                def over_items(eng, front, back):
                    front(0, 0)
                    back(0, 0, (0, 1))
                    back(0, 1, (1, 0))
                    with eng.Fori(1, CHUNKS - 1) as c:
                        back(c, 0, (c, 1))
                        back(c, 1, (c + 1, 0))
                    back(CHUNKS - 1, 0, (CHUNKS - 1, 1))
                    back(CHUNKS - 1, 1, None)

                @block.sync
                def _(sp):
                    def spread_blocks(c, b):
                        n = B * c + b + 1
                        waiter(sp)("coup_done", c, b, NG - 1)
                        for j in range(NB):
                            sp.dma_start(
                                blocks_dram[b, :, j].rearrange("h i k -> i h k"),
                                coupling[j * BASE:(j + 1) * BASE].rearrange("p g (h c) -> p (g h) c", h=GROUP)[:, :, j * BASE:(j + 1) * BASE],
                            ).then_inc(s_["blocks_out"], 16)
                        sp.wait_ge(s_["blocks_out"], 16 * NB * n)
                        sp.dma_start(rows_of[:].rearrange("p j x -> p (j x)"),
                                     blocks_dram[b].rearrange("h j i k -> h (j i k)").unsqueeze(1)
                                     .broadcast_to([H, BASE, NB * BASE * BASE])).then_inc(s_["blocks_in"], 16)

                    def back(c, b, ahead):
                        if ahead:
                            spread_blocks(*ahead)

                    over_items(sp, spread_blocks, back)

                @block.tensor
                def _(pe):
                    w, w_level = waiter(pe), level_waiter(pe)
                    pe.wait_ge(weights_in, WEIGHTS)
                    pe.wait_ge(s_["consts_set"], 2)

                    def each_head(out, lhs, rhs, done, width=P):
                        for h in range(GROUP):
                            mm = nc.tensor.matmul(out[:, h * width:(h + 1) * width], lhs(h), rhs(h), start=True, stop=True)
                        mm.then_inc(s_[done], 1)

                    def merge(out, lhs, rhs, s, done):
                        for h in range(GROUP):
                            if s < 32:
                                mm = nc.tensor.matmul(out[:, h * HALF:(h + 1) * HALF], head(lhs, h), rhs(h), start=True, stop=True)
                            else:
                                for even in range(0, P, 2 * s):
                                    col = even // 2
                                    mm = nc.tensor.matmul(
                                        out[even:even + s, h * HALF + col:h * HALF + col + s],
                                        lhs[:, h * P + even:h * P + even + s], columns(rhs(h), col, s),
                                        start=True, stop=True, tile_position=(0, even))
                        mm.then_inc(s_[done], 1)

                    def turn(out, src, done):
                        for h in range(GROUP):
                            mm = nc.tensor.transpose(head(out, h), head(src, h), k.ident[:])
                        mm.then_inc(s_[done], 1)

                    FX, FY = ([front_bank[:, i, g, :] for g in range(NG)] for i in range(2))
                    BX, BY = ([back_bank[:, i, g, :] for g in range(NG)] for i in range(2))

                    def project(i, bank, b, g, done):
                        nc.tensor.matmul(bank, chunk_T[:, b, :], w_qkv[:, i, g * W:(g + 1) * W],
                                         start=True, stop=True).then_inc(s_[done], 1)

                    def project_qk(c, b):
                        pe.wait_ge(s_["chunk_ready"], 2 * (B * c + b) + 1)
                        for g in range(NG):
                            w("qgT_kept", c, b, g, back=1)
                            project(0, FX[g], b, g, "q_proj")
                            w("qT_kept", c, b, g, back=1)
                            project(1, FY[g], b, g, "k_proj")

                    def project_v(c, b):
                        for g in range(NG):
                            w("q_silu", c, b, g)
                            project(2, FX[g], b, g, "v_proj")

                    def sum_decays(c, b, g):
                        w("spread_done", c, b, g)
                        w("v_silu", c, b, g)
                        nc.tensor.matmul(FX[g], ones[:], spread[:, g, :], start=True, stop=False)
                        nc.tensor.matmul(FX[g], identb[:], below_b[:].rearrange("p h c -> p (h c)"),
                                         start=False, stop=True).then_inc(s_["decay_sum"], 1)

                    def turn_k(c, b, g):
                        w("k_silu", c, b, g)
                        w("k_done", c, b, g)
                        turn(FY[g], kk[:, g, :], "kT_turned")

                    def couple(c, b, g):
                        w("kT_kept", c, b, g)
                        each_head(FY[g], lambda h: head(kT[:, b, g, :], h), lambda h: head(kT[:, b, g, :], h), "kk_done")

                    def turn_coupling(c, b, g):
                        w("decay_done", c, b, g)
                        w("raw_done", c, b, g)
                        turn(FX[g], raw[:, g, :], "coup_turned")

                    def turn_q(c, b, g):
                        w("raw_done", c, b, g)
                        w("q_done", c, b, g)
                        turn(FY[g], q[:, g, :], "qT_turned")

                    def turn_qg(c, b, g):
                        w("coup_done", c, b, g)
                        w("qg_done", c, b, g)
                        turn(FX[g], qg[:, g, :], "qgT_turned")

                    def both(part, ahead):
                        if ahead:
                            for g in range(NG):
                                part(*ahead, g)

                    def front(c, b):
                        project_qk(c, b)
                        project_v(c, b)
                        for part in (sum_decays, turn_k, couple, turn_coupling, turn_q, turn_qg):
                            both(part, (c, b))

                    def back(c, b, ahead):
                        if ahead:
                            project_qk(*ahead)
                        for g in range(NG):
                            w("qT_kept", c, b, g)
                            if g == 0:
                                wait_mixed(c, b)
                            each_head(BY[g], lambda h: head(kT[:, b, g, :], h), lambda h: head(qT[:, b, g, :], h), "kq_done")
                        if ahead:
                            project_v(*ahead)
                        for g in range(NG):
                            w("attend_done", c, b, g)
                            w("state_done", c, b, g, back=2)
                            each_head(BY[g], lambda h: head(kT[:, b, g, :], h), lambda h: head(state[:, b, g, :], h), "ks_done")
                        w("state_done", c, b, NG - 1, back=1)
                        pe.wait_ge(s_["solved"], SOLVE_STEPS * (B * c + b + 1))
                        nc.tensor.transpose(BX[0][:, 0:P], inverse[:].rearrange("p j i -> p (j i)"), k.ident[:]).then_inc(
                            s_["inverse_turned"], 1)
                        both(sum_decays, ahead)
                        w("base_done", c, b, NG - 1)
                        for g in range(NG):
                            turn(BX[g], solve_T[:, g, :], "solve_turned")
                        for lev, s in enumerate(LEVELS):
                            for g in range(NG):
                                if lev == 0:
                                    w("solve_kept", c, b, g)
                                else:
                                    w_level("n_read", c, b, g, lev - 1)
                                    w_level("t_kept", c, b, g, lev - 1, NLEV - 1)
                                merge(BX[g], coupling[:, g, :], lambda h: odd(head(solve[:, g, :], h), s), s, "m_done")
                            if lev == 1:
                                both(turn_k, ahead)
                            if lev == 2:
                                both(couple, ahead)
                            for g in range(NG):
                                w_level("m_read", c, b, g, lev)
                                if lev == 0:
                                    w("v_ready", c, b, g)
                                merge(BY[g], solve_T[:, g, :], lambda h: partial[:, g, h * HALF:(h + 1) * HALF], s, "n_done")
                            if lev < NLEV - 1:
                                for g in range(NG):
                                    w_level("n_read", c, b, g, lev)
                                    turn(BX[g], solve[:, g, :], "t_turned")
                        for g in range(NG):
                            w_level("n_read", c, b, g, NLEV - 1)
                            each_head(BX[g], lambda h: head(solve[:, g, :], h), lambda h: head(v[:, b, g, :], h), "u_done")
                        both(turn_coupling, ahead)
                        both(turn_q, ahead)
                        for g in range(NG):
                            w("qgT_kept", c, b, g)
                            w("u_kept", c, b, g)
                            for h in range(GROUP):
                                nc.tensor.matmul(head(BY[g], h), head(state[:, b, g, :], h), head(qgT[:, b, g, :], h), start=True, stop=False)
                                mm = nc.tensor.matmul(head(BY[g], h), head(update[:, g, :], h), head(attend[:, g, :], h), start=False, stop=True)
                            mm.then_inc(s_["o_done"], 1)
                        for g in range(NG):
                            each_head(BX[g], lambda h: head(kt[:, b, g, :], h), lambda h: head(update[:, g, :], h), "ds_done")
                        both(turn_qg, ahead)
                        for g in range(NG):
                            w("o_kept", c, b, g)
                            for h in range(GROUP):
                                mm = nc.tensor.matmul(BY[0][:, 0:D], head(out_T[:, g, :], h), w_o[:, g * GROUP + h, :],
                                                      start=(g == 0 and h == 0), stop=(g == NG - 1 and h == GROUP - 1))
                        mm.then_inc(s_["wo_done"], 1)

                    def wait_mixed(c, b):
                        n = B * c + b
                        if not (isinstance(n, int) and n == 0):
                            pe.wait_ge(s_["mixed_done"], n)

                    over_items(pe, front, back)

                @block.scalar
                def _(act):
                    w, w_level = waiter(act), level_waiter(act)

                    def keep(src, dst, ready, kept, c, b, g):
                        w(ready, c, b, g)
                        nc.scalar.copy(dst, src).then_inc(s_[kept], 1)

                    def silu_qk(c, b):
                        for g in range(NG):
                            w("q_proj", c, b, g)
                            w("qgT_turned", c, b, g, back=1)
                            w("v_done", c, b, g, back=1)
                            nc.scalar.activation(q[:, g, :], front_bank[:, 0, g, :], ACT.Silu).then_inc(s_["q_silu"], 1)
                            w("k_proj", c, b, g)
                            nc.scalar.activation(kk[:, g, :], front_bank[:, 1, g, :], ACT.Silu).then_inc(s_["k_silu"], 1)

                    def silu_v(c, b):
                        for g in range(NG):
                            w("v_proj", c, b, g)
                            w("u_done", c, b, g, back=2)
                            nc.scalar.activation(v[:, b, g, :], front_bank[:, 0, g, :], ACT.Silu).then_inc(s_["v_silu"], 1)

                    def exp_decay(c, b, g):
                        w("decay_sum", c, b, g)
                        act.wait_ge(s_["chunk_ready"], 2 * (B * c + b) + 2)
                        for h in range(GROUP):
                            last = nc.scalar.activation(head(decay[:, b, g, :], h), head(front_bank[:, 0, g, :], h), ACT.Exp,
                                                        bias=cols("neg_summed", b, g)[:, h:h + 1])
                        last.then_inc(s_["decay_done"], 1)

                    def keep_kT(c, b, g):
                        keep(front_bank[:, 1, g, :], kT[:, b, g, :], "kT_turned", "kT_kept", c, b, g)

                    def keep_qT(c, b, g):
                        keep(front_bank[:, 1, g, :], qT[:, b, g, :], "qT_turned", "qT_kept", c, b, g)

                    def keep_qgT(c, b, g):
                        keep(front_bank[:, 0, g, :], qgT[:, b, g, :], "qgT_turned", "qgT_kept", c, b, g)

                    def front(c, b):
                        silu_qk(c, b)
                        silu_v(c, b)
                        for part in (exp_decay, keep_kT, keep_qT, keep_qgT):
                            for g in range(NG):
                                part(c, b, g)

                    def both(part, ahead):
                        if ahead:
                            for g in range(NG):
                                part(*ahead, g)

                    def back(c, b, ahead):
                        if ahead:
                            silu_qk(*ahead)
                            silu_v(*ahead)
                        both(exp_decay, ahead)
                        for g in range(NG):
                            keep(back_bank[:, 0, g, :], solve[:, g, :], "solve_turned", "solve_kept", c, b, g)
                        for lev in range(NLEV - 1):
                            if lev == 1:
                                both(keep_kT, ahead)
                            for g in range(NG):
                                w_level("t_turned", c, b, g, lev, NLEV - 1)
                                nc.scalar.copy(solve_T[:, g, :], back_bank[:, 0, g, :]).then_inc(s_["t_kept"], 1)
                        for g in range(NG):
                            keep(back_bank[:, 0, g, :], update[:, g, :], "u_done", "u_kept", c, b, g)
                        both(keep_qT, ahead)
                        for g in range(NG):
                            keep(back_bank[:, 1, g, :], out_T[:, g, :], "o_done", "o_kept", c, b, g)
                        both(keep_qgT, ahead)

                    over_items(act, front, back)

                @block.vector
                def _(dve):
                    w, w_level = waiter(dve), level_waiter(dve)
                    k.link(dve, nc.vector.memset(state[:], 0.0))
                    dve.wait_ge(weights_in, WEIGHTS)

                    def take_chunk(c, b):
                        w("v_proj", c, b, NG - 1, back=2)
                        w("state_done", c, b, NG - 1, back=2)
                        w("v_done", c, b, NG - 1, back=2)
                        w("decay_done", c, b, NG - 1, back=2)
                        nc.vector.tensor_scalar(chunk_T[:, b, :], normT[:, bass.ds((b * CHUNKS + c) * P, P)], 0.0, None,
                                                ALU.add).then_inc(s_["chunk_ready"], 1)
                        nc.vector.tensor_scalar(chunk_gates[:, b], all_gates[:, b * CHUNKS + c], 0.0, None,
                                                ALU.add).then_inc(s_["chunk_ready"], 1)

                    def sum_squares(c, b, g):
                        w("squared", c, b, g)
                        nc.vector.tensor_reduce(squares[:, g, 0:GROUP], heads4(q_sq[:, g, :]), AX_X, ALU.add)
                        nc.vector.tensor_reduce(squares[:, g, GROUP:], heads4(k_sq[:, g, :]), AX_X, ALU.add).then_inc(s_["squares_done"], 1)
                        w("squares_done", c, b, g)
                        nc.vector.tensor_scalar(shifted[:, g, :], squares[:, g, :], 1e-6, None, ALU.add).then_inc(s_["shifted_done"], 1)

                    def weigh(c, b, g):
                        w("decay_done", c, b, g)
                        w("kk_done", c, b, g)
                        nc.vector.tensor_tensor(raw[:, g, :], front_bank[:, 1, g, :], decay[:, b, g, :], ALU.mult).then_inc(s_["raw_done"], 1)

                    def scale_coupling(c, b, g):
                        w("coup_turned", c, b, g)
                        nc.vector.tensor_tensor(heads4(coupling[:, g, :]), heads4(front_bank[:, 0, g, :]), wide(cols("neg_beta", b, g)),
                                                ALU.mult).then_inc(s_["coup_done"], 1)

                    def both(part, ahead):
                        if ahead:
                            for g in range(NG):
                                part(*ahead, g)

                    def front(c, b):
                        take_chunk(c, b)
                        for part in (sum_squares, weigh, scale_coupling):
                            both(part, (c, b))

                    def solve_rows(c, b, first, last):
                        done = SOLVE_STEPS * (B * c + b)
                        if first == 1:
                            dve.wait_ge(s_["blocks_in"], 16 * (B * c + b + 1))
                            nc.vector.tensor_copy(inverse[:], delta[:].unsqueeze(1).broadcast_to([P, NB, BASE])).then_inc(s_["solved"], 1)
                            nc.vector.memset(rows_of[:, :, ::BASE + 1], 1.0).then_inc(s_["solved"], 1)
                        for i in range(first, last):
                            dve.wait_ge(s_["solved"], done + 2 * i)
                            nc.vector.tensor_tensor(products[:, :, 0:i + 1], rows_of[:, :, i * BASE:i * BASE + i + 1],
                                                    inverse[:, :, 0:i + 1], ALU.mult).then_inc(s_["solved"], 1)
                            dve.wait_ge(s_["solved"], done + 2 * i + 1)
                            nc.vector.tensor_reduce(inverse[:, :, i], products[:, :, 0:i + 1], AX_X, ALU.add).then_inc(s_["solved"], 1)

                    def back(c, b, ahead):
                        if ahead:
                            take_chunk(*ahead)
                        solve_rows(c, b, 1, BASE // 2)
                        for g in range(NG):
                            w("kq_done", c, b, g)
                            nc.vector.tensor_tensor(attend[:, g, :], back_bank[:, 1, g, :], decay[:, b, g, :], ALU.mult).then_inc(s_["attend_done"], 1)
                        solve_rows(c, b, BASE // 2, BASE)
                        dve.wait_ge(s_["inverse_turned"], B * c + b + 1)
                        for g in range(NG):
                            nc.vector.tensor_tensor(
                                solve_T[:, g, :].rearrange("p (h j b) -> p h j b", h=GROUP, b=BASE),
                                back_bank[:, 0, 0, g * GROUP * BASE:(g + 1) * GROUP * BASE].rearrange("p (h b) -> p h b", b=BASE)
                                .unsqueeze(2).broadcast_to([P, GROUP, NB, BASE]),
                                block_of[:].unsqueeze(1).unsqueeze(3).broadcast_to([P, GROUP, NB, BASE]),
                                ALU.mult).then_inc(s_["base_done"], 1)
                        if ahead:
                            sum_squares(*ahead, 0)
                        for g in range(NG):
                            w("ks_done", c, b, g)
                            w("v_done", c, b, g)
                            for h in range(GROUP):
                                last = nc.vector.scalar_tensor_tensor(
                                    head(v[:, b, g, :], h), head(back_bank[:, 1, g, :], h), cols("neg_beta_grown", b, g)[:, h:h + 1],
                                    head(v[:, b, g, :], h), ALU.mult, ALU.add)
                            last.then_inc(s_["v_ready"], 1)
                        for lev, s in enumerate(LEVELS):
                            for g in range(NG):
                                w_level("m_done", c, b, g, lev)
                                nc.vector.tensor_tensor(
                                    partial[:, g, :].rearrange("p (h c) -> p h c", h=GROUP),
                                    back_bank[:, 0, g, 0:GROUP * HALF].rearrange("p (h c) -> p h c", h=GROUP),
                                    spread4(level_masks[:, lev, :]), ALU.mult).then_inc(s_["m_read"], 1)
                            if ahead and lev == 0:
                                sum_squares(*ahead, 1)
                            for g in range(NG):
                                w_level("n_done", c, b, g, lev)
                                for even in range(0, P, 2 * s) if s >= 32 else (0,):
                                    to = odd(solve[:, g, :], s).rearrange("p (h n) s -> p h n s", h=GROUP)
                                    of = back_bank[:, 1, g, 0:GROUP * HALF].rearrange("p (h n s) -> p h n s", h=GROUP, s=s)
                                    if s >= 32:
                                        to, of = (t[even:even + s, :, even // (2 * s), :] for t in (to, of))
                                    else:
                                        to, of = (t.rearrange("p h n s -> p (h n) s") for t in (to, of))
                                    last = nc.vector.tensor_tensor(to, of, to, ALU.add)
                                last.then_inc(s_["n_read"], 1)
                        both(weigh, ahead)
                        both(scale_coupling, ahead)
                        for g in range(NG):
                            w("ds_done", c, b, g)
                            for h in range(GROUP):
                                last = nc.vector.scalar_tensor_tensor(
                                    head(state[:, b, g, :], h), head(state[:, b, g, :], h), cols("last", b, g)[:, h:h + 1],
                                    head(back_bank[:, 0, g, :], h), ALU.mult, ALU.add)
                            last.then_inc(s_["state_done"], 1)
                        dve.wait_ge(s_["wo_done"], B * c + b + 1)
                        nc.vector.tensor_tensor(mixed[:, b * CHUNKS + c, :], back_bank[:, 1, 0, 0:D], k.n[:, b * CHUNKS + c, :],
                                                ALU.add).then_inc(s_["mixed_done"], 1)

                    over_items(dve, front, back)
                    dve.wait_ge(s_["mixed_done"], B * CHUNKS)

                @block.gpsimd
                def _(pool):
                    w = waiter(pool)
                    TT = nc.gpsimd.tensor_tensor
                    pool.wait_ge(weights_in, WEIGHTS)
                    for h in range(GROUP):
                        last = nc.gpsimd.tensor_copy(below_b[:, h, :], below[:])
                    last.then_inc(s_["consts_set"], 1)
                    nc.gpsimd.tensor_copy(identb[:], k.ident[:]).then_inc(s_["consts_set"], 1)
                    pool.wait_ge(s_["consts_set"], 2)

                    def front(c, b):
                        for g in range(NG):
                            w("q_silu", c, b, g)
                            TT(q_sq[:, g, :], q[:, g, :], q[:, g, :], ALU.mult)
                            w("k_silu", c, b, g)
                            TT(k_sq[:, g, :], kk[:, g, :], kk[:, g, :], ALU.mult).then_inc(s_["squared"], 1)
                        pool.wait_ge(s_["chunk_ready"], 2 * (B * c + b) + 2)
                        for g in range(NG):
                            w("decay_sum", c, b, g, back=1)
                            TT(heads4(spread[:, g, :]), spread4(upper[:]), wide(cols("log_a", b, g)), ALU.mult).then_inc(s_["spread_done"], 1)
                        for g in range(NG):
                            w("shifted_done", c, b, g)
                            TT(inv_norm[:, g, :], shifted[:, g, :], k.half[:, 0:2 * GROUP], ALU.pow).then_inc(s_["norm_done"], 1)
                            w("norm_done", c, b, g)
                            TT(heads4(kk[:, g, :]), heads4(kk[:, g, :]), wide(inv_norm[:, g, GROUP:]), ALU.mult).then_inc(s_["k_done"], 1)
                            TT(heads4(q[:, g, :]), heads4(q[:, g, :]), wide(inv_norm[:, g, 0:GROUP]), ALU.mult).then_inc(s_["q_done"], 1)
                        for g in range(NG):
                            w("q_done", c, b, g)
                            TT(heads4(qg[:, g, :]), heads4(q[:, g, :]), wide(cols("grown", b, g)), ALU.mult).then_inc(s_["qg_done"], 1)
                            w("ds_done", c, b, g, back=2)
                            TT(heads4(kt[:, b, g, :]), heads4(kk[:, g, :]), wide(cols("rest", b, g)), ALU.mult)
                            w("v_silu", c, b, g)
                            TT(heads4(v[:, b, g, :]), heads4(v[:, b, g, :]), wide(cols("beta", b, g)), ALU.mult).then_inc(s_["v_done"], 1)

                    def back(c, b, ahead):
                        if ahead:
                            front(*ahead)

                    over_items(pool, front, back)

        with ExitStack() as ctx:
            b2 = k.sb("f1_b2", [P, D], ctx=ctx)

            def loads(e, par, w1, w2, b1):
                return [(w1, a["L1_attn_W1"]), (w2, a["L1_attn_W2"].rearrange("(f p) d -> p f d", p=P)),
                        (b1, a["L1_attn_b1"].rearrange("(f p) -> p f", p=P)), (b2[:], a["L1_attn_b2"].partition_broadcast(P))]

            weights = HiddenWeights(k, "f1", ctx, loads, 4, 1)
            layer_norm(k, "ln4", mixed, 1e-5, k.n, k.nT, rows["ln2_w"], rows["ln2_b"], prefetch=weights.load_first)

            def finish(ctx, down, down_ready, down_read, weights_in):
                base_done, added = k.sem("f1_base_done"), k.sem("f1_added")

                def vector(dve):
                    weights_in(dve, 0, 0)
                    nc.vector.tensor_tensor(mixed[:], mixed[:], b2[:].unsqueeze(1).broadcast_to([P, TILES, D]), ALU.add).then_inc(base_done, 1)
                    dve.wait_ge(base_done, 1)
                    nc.vector.tensor_tensor(k.x[:], k.x[:], mixed[:], ALU.add).then_inc(base_done, 1)
                    dve.wait_ge(base_done, 2)
                    for blk in range(BLOCKS):
                        dve.wait_ge(down_ready, blk + 1)
                        nc.vector.tensor_tensor(k.x[:, 4 * blk:4 * blk + 4, :], down[:, blk % 2, :].rearrange("p (t d) -> p t d", t=4),
                                                k.x[:, 4 * blk:4 * blk + 4, :], ALU.add).then_inc(down_read, 1)
                    dve.wait_ge(down_read, BLOCKS)

                return {"vector": vector}

            feed_forward(k, "f1", weights, ACT.Gelu, True, finish)


def experts(k, a):
    nc = k.nc
    with ExitStack() as ctx:
        router = k.sb("moe_router", [D, EXPERTS], ctx=ctx)
        beta = k.sb("moe_beta", [EXPERTS, D], ctx=ctx)
        logits = k.sb("moe_logits", [P, TILES, EXPERTS], ctx=ctx)
        gate_of = k.sb("moe_gate_of", [P, EXPERTS, TILES], ctx=ctx)
        gates = k.sb("moe_gates", [P, TILES, EXPERTS], ctx=ctx)
        gates_T = k.sb("moe_gates_T", [EXPERTS, TILES, P], ctx=ctx)
        scaled = k.sb("moe_scaled", [P, TILES, EXPERTS], ctx=ctx)
        gap, expd, total, w_1, w_2 = (k.sb(f"moe_{s}", [P, TILES], ctx=ctx) for s in ("gap", "expd", "total", "w_1", "w_2"))
        w_in, logits_done, gap_done, expd_done, gates_done, turned_done, kept, beta_done = (
            k.sem(f"moe_{s}") for s in ("w_in", "logits_done", "gap_done", "expd_done", "gates_done", "turned_done",
                                        "kept", "beta_done"))
        hot, top, steps = top_two(k, "moe", ctx, logits)
        b2 = k.sb("moe_b2", [P, 2, D], ctx=ctx)
        gamma = k.sb("moe_gamma", [P, 2, D], ctx=ctx)

        def loads(e, par, w1, w2, b1):
            return [(w1, a["L1_ffn_w1"][e]), (w2, a["L1_ffn_w2"][e].rearrange("(f p) d -> p f d", p=P)),
                    (b1, a["L1_ffn_b1"][e].rearrange("(f p) -> p f", p=P)),
                    (b2[:, par], a["L1_ffn_b2"][e].partition_broadcast(P)),
                    (gamma[:, par], a["L1_ffn_gamma"][e].partition_broadcast(P))]

        weights = HiddenWeights(k, "moe", ctx, loads, 5, EXPERTS)

        def prefetch(sp):
            sp.dma_start(router[:], a["L1_ffn_router_w"]).then_inc(w_in, 16)
            sp.dma_start(beta[:], a["L1_ffn_beta"]).then_inc(w_in, 16)
            weights.load_first(sp)

        layer_norm(k, "ln5", k.x, 1e-5, k.n, k.nT, prefetch=prefetch)
        with ExitStack() as inner:
            route = k.ps("moe_route", [P, TILES, EXPERTS], ctx=inner)
            turned = k.ps("moe_turned", [EXPERTS, TILES, P], ctx=inner)
            offset = k.ps("moe_offset", [P, 2, BLK], ctx=inner)
            block = inner.enter_context(nc.Block())

            @block.tensor
            def _(pe):
                pe.wait_ge(w_in, 32)
                for t in range(TILES):
                    mm = nc.tensor.matmul(route[:, t, :], k.nT[:, t * P:(t + 1) * P], router[:], start=True, stop=True)
                mm.then_inc(logits_done, 1)
                pe.wait_ge(gates_done, 1)
                for t in range(TILES):
                    mm = nc.tensor.transpose(turned[:, t, :], gates[:, t, :], k.ident[:])
                mm.then_inc(turned_done, 1)
                pe.wait_ge(kept, 1)
                for t in range(TILES):
                    if t % 4 == 0 and t >= 8:
                        pe.wait_ge(beta_done, t // 4 - 1)
                    mm = nc.tensor.matmul(offset[:, (t // 4) % 2, (t % 4) * D:(t % 4 + 1) * D], gates_T[:, t, :], beta[:],
                                          start=True, stop=True)
                    if t % 4 == 3:
                        mm.then_inc(turned_done, 1)

            @block.scalar
            def _(act):
                act.wait_ge(gap_done, 1)
                nc.scalar.activation(expd[:], gap[:], ACT.Exp).then_inc(expd_done, 1)
                act.wait_ge(turned_done, 1)
                nc.scalar.copy(gates_T[:], turned[:]).then_inc(kept, 1)

            @block.vector
            def _(dve):
                dve.wait_ge(logits_done, 1)
                k.link(dve, nc.vector.tensor_copy(logits[:], route[:]))
                steps(dve)
                nc.vector.tensor_tensor(gap[:], top["top2"][:], top["top1"][:], ALU.subtract).then_inc(gap_done, 1)
                dve.wait_ge(expd_done, 1)

                W = [P, TILES, EXPERTS]
                k.link(dve, nc.vector.tensor_scalar(total[:], expd[:], 1.0, None, ALU.add))
                k.link(dve, nc.vector.reciprocal(w_1[:], total[:]))
                k.link(dve, nc.vector.tensor_tensor(w_2[:], w_1[:], expd[:], ALU.mult))
                k.link(dve, nc.vector.tensor_tensor(scaled[:], hot["hot1"][:], w_1[:].unsqueeze(2).broadcast_to(W), ALU.mult))
                k.link(dve, nc.vector.tensor_tensor(gates[:], hot["hot2"][:], w_2[:].unsqueeze(2).broadcast_to(W), ALU.mult))
                k.link(dve, nc.vector.tensor_tensor(gates[:], gates[:], scaled[:], ALU.add))
                nc.vector.tensor_copy(gate_of[:], gates[:].rearrange("p t e -> p e t")).then_inc(gates_done, 1)
                for g in range(BLOCKS):
                    dve.wait_ge(turned_done, g + 2)
                    nc.vector.tensor_tensor(k.x[:, 4 * g:4 * g + 4, :], offset[:, g % 2, :].rearrange("p (t d) -> p t d", t=4),
                                            k.x[:, 4 * g:4 * g + 4, :], ALU.add).then_inc(beta_done, 1)
                dve.wait_ge(beta_done, BLOCKS)
                dve.wait_ge(gates_done, 1)

        def finish(ctx, down, down_ready, down_read, weights_in):
            res = k.sb("moe_res", [P, 2, 4, D], ctx=ctx)
            stats = k.sb("moe_stats", [P, 2, 4, 6], ctx=ctx)
            moments = k.sb("moe_moments", [P, 2, 4, 2], ctx=ctx)
            shifted = k.sb("moe_shifted", [P, 2, 4], ctx=ctx)
            rstd = k.sb("moe_rstd", [P, 2, 4], ctx=ctx)
            gated = k.sb("moe_gated", [P, 2, 4], ctx=ctx)
            res_done, stats_done, moments_done, shifted_done, rstd_done, gated_done, normed, weighted, added = (
                k.sem(f"moe_{s}") for s in ("res_done", "stats_done", "moments_done", "shifted_done", "rstd_done",
                                            "gated_done", "normed", "weighted", "added"))
            ALL = EXPERTS * BLOCKS

            def over(eng, body):
                for par in range(2):
                    body(0, par)
                with eng.Fori(1, EXPERTS // 2) as r:
                    for par in range(2):
                        body(r, par)

            def vector(dve):
                def scale(e, m, blk, s):
                    dve.wait_ge(rstd_done, m + 1)
                    nc.vector.tensor_tensor(gated[:, s, :], rstd[:, s, :], gate_of[:, e, 4 * blk:4 * blk + 4],
                                            ALU.mult).then_inc(gated_done, 1)
                    dve.wait_ge(gated_done, m + 1)
                    for t in range(4):
                        last = nc.vector.tensor_scalar(res[:, s, t, :], res[:, s, t, :], moments[:, s, t, 0:1],
                                                       gated[:, s, t:t + 1], ALU.subtract, ALU.mult)
                    last.then_inc(normed, 1)

                def body(r, par):
                    e = 2 * r + par
                    weights_in(dve, r, par)
                    for blk in range(BLOCKS):
                        m, s = e * BLOCKS + blk, blk % 2
                        dve.wait_ge(down_ready, m + 1)
                        if not (isinstance(m, int) and m < 2):
                            dve.wait_ge(added, m - 1)
                        nc.vector.tensor_tensor(res[:, s], down[:, s, :].rearrange("p (t d) -> p t d", t=4),
                                                k.n[:, 4 * blk:4 * blk + 4, :], ALU.add).then_inc(down_read, 1)
                        dve.wait_ge(down_read, m + 1)
                        nc.vector.tensor_tensor(res[:, s], res[:, s], b2[:, par].unsqueeze(1).broadcast_to([P, 4, D]),
                                                ALU.add).then_inc(res_done, 1)
                        dve.wait_ge(res_done, m + 1)
                        for t in range(4):
                            last = nc.vector.bn_stats(stats[:, s, t, :], res[:, s, t, :])
                        last.then_inc(stats_done, 1)
                        dve.wait_ge(stats_done, m + 1)
                        if not (isinstance(m, int) and m == 0):
                            scale(e if blk else e - 1, m - 1, (blk - 1) % BLOCKS, 1 - s)
                        for t in range(4):
                            last = nc.vector.bn_aggr(moments[:, s, t, :], stats[:, s, t, :])
                        last.then_inc(moments_done, 1)
                        dve.wait_ge(moments_done, m + 1)
                        nc.vector.tensor_scalar(shifted[:, s, :], moments[:, s, :, 1], 1e-6, None, ALU.add).then_inc(shifted_done, 1)

                over(dve, body)
                scale(EXPERTS - 1, ALL - 1, BLOCKS - 1, 1)
                dve.wait_ge(normed, ALL)

            def gpsimd(pool):
                def add(par, m, blk, s):
                    pool.wait_ge(normed, m + 1)
                    nc.gpsimd.tensor_tensor(res[:, s], res[:, s], gamma[:, par].unsqueeze(1).broadcast_to([P, 4, D]),
                                            ALU.mult).then_inc(weighted, 1)
                    pool.wait_ge(weighted, m + 1)
                    nc.gpsimd.tensor_tensor(k.x[:, 4 * blk:4 * blk + 4, :], k.x[:, 4 * blk:4 * blk + 4, :], res[:, s],
                                            ALU.add).then_inc(added, 1)

                def body(r, par):
                    weights_in(pool, r, par)
                    for blk in range(BLOCKS):
                        m, s = (2 * r + par) * BLOCKS + blk, blk % 2
                        pool.wait_ge(shifted_done, m + 1)
                        nc.gpsimd.tensor_tensor(rstd[:, s, :], shifted[:, s, :], k.half[:, 0:4], ALU.pow).then_inc(rstd_done, 1)
                        if not (isinstance(m, int) and m == 0):
                            add(par if blk else 1 - par, m - 1, (blk - 1) % BLOCKS, 1 - s)

                over(pool, body)
                add(1, ALL - 1, BLOCKS - 1, 1)
                pool.wait_ge(added, ALL)

            def used(sp, e):
                sp.wait_ge(added, BLOCKS * (e + 1))

            return {"vector": vector, "gpsimd": gpsimd, "used": used}

        feed_forward(k, "moe", weights, ACT.Gelu, True, finish)


def store(k, out):
    with k.nc.Block() as block:
        @block.sync
        def _(sp):
            sp.dma_start(out.rearrange("b (t p) d -> p (b t) d", p=P), k.x[:]).then_inc(k.moved, 16)
            sp.wait_ge(k.moved, 64)


def build_program(nc, a, out):
    with ExitStack() as ctx:
        k = Core(nc, ctx)
        start(k, a)
        attention(k, a)
        feed_forward0(k, a)
        delta_layer(k, a)
        experts(k, a)
        store(k, out)


_INPUTS = [
    "L0_attn_X", "L0_attn_W_qkv", "L0_attn_b_qkv", "L0_attn_W_proj", "L0_attn_b_proj", "L0_ffn_Wg", "L0_ffn_w1",
    "L0_ffn_w2", "L1_attn_Wq", "L1_attn_Wk", "L1_attn_Wv", "L1_attn_Wb", "L1_attn_Wa", "L1_attn_Wo", "L1_attn_ln1_w",
    "L1_attn_ln1_b", "L1_attn_ln2_w", "L1_attn_ln2_b", "L1_attn_W1", "L1_attn_b1", "L1_attn_W2", "L1_attn_b2",
    "L1_ffn_router_w", "L1_ffn_w1", "L1_ffn_b1", "L1_ffn_w2", "L1_ffn_b2", "L1_ffn_gamma", "L1_ffn_beta",
]


def kernel(**inputs):
    from concourse import bacc
    from concourse.bass_utils import run_bass_kernel_spmd

    nc = bacc.Bacc("TRN2", target_bir_lowering=False, num_devices=1)
    arrays = {name: np.ascontiguousarray(inputs[name]) for name in _INPUTS}
    arrays.update(shape_constants())
    a = {name: nc.dram_tensor(f"in_{name}", v.shape, mybir.dt.from_np(v.dtype), kind="ExternalInput").ap()
         for name, v in arrays.items()}
    out = nc.dram_tensor("out", arrays["L0_attn_X"].shape, F32, kind="ExternalOutput").ap()
    build_program(nc, a, out)
    result = run_bass_kernel_spmd(nc, [{f"in_{name}": v for name, v in arrays.items()}], core_ids=[0])
    return result.results[0]["out"]
```

```python
from contextlib import ExitStack

import numpy as np

import concourse.bass as bass
from concourse import mybir

F32 = mybir.dt.float32
BF16 = mybir.dt.bfloat16
ALU = mybir.AluOpType
ACT = mybir.ActivationFunctionType
AX_X = mybir.AxisListType.X

P = 128
D = 128
BATCH, SEQ = 2, 1024
TILES = BATCH * SEQ // P
SEQ_TILES = SEQ // P
BLOCKS = 4
BLK = 512
FFN = 512
EXPERTS = 8

HEADS0, HDIM0 = 16, 8
SCALE0 = float(HDIM0) ** -0.5
PARTS = 3
PAIRS = [(a, b) for a in range(PARTS) for b in range(PARTS)]
MAX_ROW = len(PAIRS) * HDIM0
PAIR_OF_ONES = float(np.array(0x3F803F80, dtype=np.uint32).view(np.float32))
STACK = 96

HEADS1 = 8
GROUP = 4
BASE = 16
LEVELS = [16, 32, 64]
NEG = -1.0e30


def shape_constants():
    i = np.arange(P)
    ident = np.eye(P, dtype=np.float32)
    upper = (i[:, None] <= i[None, :]).astype(np.float32)
    below = np.where(i[:, None] <= i[None, :], 0.0, NEG).astype(np.float32)
    block_of = (i[:, None] // BASE == np.arange(P // BASE)[None, :]).astype(np.float32)
    delta = (i[:, None] % BASE == np.arange(BASE)[None, :]).astype(np.float32)
    masks = []
    for s in LEVELS:
        odd = (i.reshape(-1, 2, s)[:, 1, :]).reshape(-1)
        masks.append(((i[:, None] // s + 1) == (odd[None, :] // s)).astype(np.float32))
    iota = np.tile(np.arange(EXPERTS, dtype=np.float32), (P, 1))
    return {
        "ident": ident, "upper": upper, "below": below, "block_of": block_of, "delta": delta,
        "levels": np.concatenate(masks, axis=1), "iota": iota,
    }


class Core:

    def __init__(self, nc, ctx):
        self.nc, self.ctx = nc, ctx
        self.x = self.sb("x", [P, TILES, D])
        self.n = self.sb("n", [P, TILES, D])
        self.nT = self.sb("nT", [D, TILES * P])
        self.ident = self.sb("ident", [P, P])
        self.iota = self.sb("iota", [P, EXPERTS])
        self.norm_sems = [self.sem(f"norm_{s}") for s in (
            "stats_done", "moments_done", "shifted_done", "rstd_done", "normed", "turned_done", "kept")]
        self.norms = self.turned_norms = 0
        self.half = self.sb("half", [P, TILES])
        self.moved = self.sem("moved")
        self.chain, self.linked = self.sem("chain"), 0

    def link(self, dve, ins):
        self.linked += 1
        ins.then_inc(self.chain, 1)
        dve.wait_ge(self.chain, self.linked)

    def sb(self, name, shape, dt=F32, ctx=None):
        return (ctx or self.ctx).enter_context(self.nc.sbuf_tensor(name, shape, dt))

    def ps(self, name, shape, dt=F32, ctx=None):
        return (ctx or self.ctx).enter_context(self.nc.psum_tensor(name, shape, dt))

    def sem(self, name):
        return self.ctx.enter_context(self.nc.semaphore(name))


def layer_norm(k, tag, src, eps, tokens_out, turned_out=None, weight=None, bias=None, prefetch=None):
    nc = k.nc
    with ExitStack() as ctx:
        stats = k.sb(f"{tag}_stats", [P, TILES, 6], ctx=ctx)
        moments = k.sb(f"{tag}_moments", [P, TILES, 2], ctx=ctx)
        shifted = k.sb(f"{tag}_shifted", [P, TILES], ctx=ctx)
        rstd = k.sb(f"{tag}_rstd", [P, TILES], ctx=ctx)
        turned = k.ps(f"{tag}_turned", [P, BLOCKS, BLK], ctx=ctx)
        stats_done, moments_done, shifted_done, rstd_done, normed, turned_done, kept = k.norm_sems
        n, m = k.norms, k.turned_norms
        k.norms, k.turned_norms = n + 1, m + (turned_out is not None)
        BT = TILES // BLOCKS
        block = ctx.enter_context(nc.Block())

        if prefetch:
            @block.sync
            def _(sp):
                prefetch(sp)

        @block.vector
        def _(dve):
            def measure(blk):
                for i in range(BT * blk, BT * (blk + 1)):
                    last = nc.vector.bn_stats(stats[:, i, :], src[:, i, :])
                last.then_inc(stats_done, 1)

            def gather(blk):
                dve.wait_ge(stats_done, n * BLOCKS + blk + 1)
                for i in range(BT * blk, BT * (blk + 1)):
                    last = nc.vector.bn_aggr(moments[:, i, :], stats[:, i, :])
                last.then_inc(moments_done, 1)
                dve.wait_ge(moments_done, n * BLOCKS + blk + 1)
                nc.vector.tensor_scalar(shifted[:, BT * blk:BT * (blk + 1)], moments[:, BT * blk:BT * (blk + 1), 1], eps, None,
                                        ALU.add).then_inc(shifted_done, 1)

            def normalise(blk):
                dve.wait_ge(rstd_done, n * BLOCKS + blk + 1)
                for i in range(BT * blk, BT * (blk + 1)):
                    last = nc.vector.tensor_scalar(tokens_out[:, i, :], src[:, i, :], moments[:, i, 0:1], rstd[:, i:i + 1],
                                                   ALU.subtract, ALU.mult)
                last.then_inc(normed, 1)

            measure(0)
            for blk in range(BLOCKS):
                gather(blk)
                if blk < BLOCKS - 1:
                    measure(blk + 1)
                if blk > 0:
                    normalise(blk - 1)
            normalise(BLOCKS - 1)
            dve.wait_ge(normed, (n + 1) * BLOCKS)

        @block.gpsimd
        def _(pool):
            for blk in range(BLOCKS):
                pool.wait_ge(shifted_done, n * BLOCKS + blk + 1)
                nc.gpsimd.tensor_tensor(rstd[:, BT * blk:BT * (blk + 1)], shifted[:, BT * blk:BT * (blk + 1)],
                                        k.half[:, 0:BT], ALU.pow).then_inc(rstd_done, 1)

        if turned_out is None:
            return

        @block.tensor
        def _(pe):
            for blk in range(BLOCKS):
                pe.wait_ge(normed, n * BLOCKS + blk + 1)
                for t in range(BT):
                    mm = nc.tensor.transpose(turned[:, blk, t * P:(t + 1) * P], tokens_out[:, BT * blk + t, :], k.ident[:])
                mm.then_inc(turned_done, 1)

        @block.scalar
        def _(act):
            for blk in range(BLOCKS):
                act.wait_ge(turned_done, m * BLOCKS + blk + 1)
                nc.scalar.activation(
                    turned_out[:, blk * BLK:(blk + 1) * BLK], turned[:, blk, :], ACT.Identity,
                    bias=0.0 if bias is None else bias[:], scale=1.0 if weight is None else weight[:],
                ).then_inc(kept, 1)
            act.wait_ge(kept, (m + 1) * BLOCKS)


def start(k, a):
    nc = k.nc
    loaded, half_set = k.moved, k.sem("start_half_set")
    with nc.Block() as block:
        @block.sync
        def _(sp):
            sp.dma_start(k.x[:], a["L0_attn_X"].rearrange("b (t p) d -> p (b t) d", p=P)).then_inc(loaded, 16)
            sp.dma_start(k.ident[:], a["ident"]).then_inc(loaded, 16)
            sp.dma_start(k.iota[:], a["iota"]).then_inc(loaded, 16)
            sp.wait_ge(loaded, 48)

        @block.gpsimd
        def _(pool):
            nc.gpsimd.memset(k.half[:], -0.5).then_inc(half_set, 1)
            pool.wait_ge(half_set, 1)


def attention(k, a):
    nc = k.nc
    KB = SEQ_TILES
    PAIRS_BH = BATCH * HEADS0
    VW = 32
    parts_dram = nc.dram_tensor("parts_dram", [2, PARTS, D, BATCH * SEQ], BF16)
    max_dram = nc.dram_tensor("max_dram", [PAIRS_BH, PARTS * KB, P], BF16)

    with ExitStack() as outer:
        stack = {w: k.sb(f"{w}_stack", [STACK, PAIRS_BH, SEQ], BF16, outer) for w in "qk"}
        v_all = k.sb("v_all", [P, PAIRS_BH, KB, HDIM0], ctx=outer)
        identb = k.sb("identb", [P, P], BF16, outer)
        rows_set = k.sem("rows_set")
        stacked = [k.sem(f"stacked{b}") for b in range(BATCH)]

        def fill_stacks(sp, b):
            for s, (pq, pk) in enumerate(PAIRS):
                for w, part in (("q", pq), ("k", pk)):
                    if (s + 1) * HDIM0 > 64:
                        sp.wait_ge(rows_set, 2 * (b + 1))
                    sp.dma_start(
                        stack[w][s * HDIM0:(s + 1) * HDIM0, b * HEADS0:(b + 1) * HEADS0, :],
                        parts_dram["qk".index(w), part, :, b * SEQ:(b + 1) * SEQ].rearrange(
                            "(h d) t -> d h t", d=HDIM0)).then_inc(stacked[b], 16)

        with ExitStack() as ctx:
            w_qkv = k.sb("w_qkv", [D, 3 * D], ctx=ctx)
            b_col = k.sb("b_col", [D, 2], ctx=ctx)
            b_v = k.sb("b_v", [P, D], ctx=ctx)
            w_in = k.sem("qkv_w_in")

            def prefetch(sp):
                sp.dma_start(w_qkv[:], a["L0_attn_W_qkv"]).then_inc(w_in, 16)
                sp.dma_start(b_col[:], a["L0_attn_b_qkv"].rearrange("(w d) -> d w", d=D)[:, 0:2],
                             allow_slow_non_contiguous=True).then_inc(w_in, 16)
                sp.dma_start(b_v[:], a["L0_attn_b_qkv"][2 * D:3 * D].partition_broadcast(P)).then_inc(w_in, 16)

            layer_norm(k, "ln0", k.x, 1e-5, k.n, k.nT, prefetch=prefetch)
            full = k.sb("full", [D, 2, BLK], ctx=ctx)
            rest = k.sb("rest", [D, 2, BLK], ctx=ctx)
            CUTS = 4
            cut = k.sb("cut", [D, CUTS, PARTS, BLK], BF16, ctx)
            by_feature = k.ps("by_feature", [D, 2, BLK], ctx=ctx)
            v_psum = k.ps("v_psum", [P, 2, BLK], ctx=ctx)
            projected, biased = (k.sem(f"qkv_{s}") for s in ("projected", "biased"))
            cut1, rest1, cut2, rest2 = (k.sem(f"qkv_{s}") for s in ("cut1", "rest1", "cut2", "rest2"))
            saved = [k.sem(f"qkv_saved{i}") for i in range(CUTS)]
            STEPS = [(w, n) for b in range(BATCH) for w in range(2) for n in range(2 * b, 2 * b + 2)]
            v_done, v_kept, identb_set = (k.sem(f"qkv_{s}") for s in ("v_done", "v_kept", "identb_set"))
            block = ctx.enter_context(nc.Block())

            @block.sync
            def _(sp):
                def save(steps):
                    for step in steps:
                        w, n = STEPS[step]
                        sp.wait_ge(rest2, step + 1)
                        sp.dma_start(parts_dram[w, :, :, n * BLK:(n + 1) * BLK].rearrange("s d t -> d s t"),
                                     cut[:, step % CUTS, :, :]).then_inc(saved[step % CUTS], 16)
                    for buf in range(CUTS):
                        sp.wait_ge(saved[buf], 16 * (steps[-1] // CUTS + 1))

                save(range(CUTS))
                fill_stacks(sp, 0)
                save(range(CUTS, 2 * CUTS))
                sp.wait_ge(stacked[0], 16 * 2 * len(PAIRS))

            @block.gpsimd
            def _(pool):
                for b in range(BATCH):
                    for w, value in (("q", 0.0), ("k", PAIR_OF_ONES)):
                        nc.gpsimd.memset(stack[w][64:STACK, b * HEADS0:(b + 1) * HEADS0].rearrange("p h t -> p (h t)")
                                         .bitcast(F32), value).then_inc(rows_set, 1)
                pool.wait_ge(rows_set, 2 * BATCH)
                nc.gpsimd.tensor_copy(identb[:], k.ident[:]).then_inc(identb_set, 1)
                pool.wait_ge(identb_set, 1)

            @block.tensor
            def _(pe):
                pe.wait_ge(w_in, 48)
                for step, (w, n) in enumerate(STEPS):
                    if step >= 2:
                        pe.wait_ge(biased, step - 1)
                    nc.tensor.matmul(by_feature[:, step % 2, :], w_qkv[:, w * D:(w + 1) * D],
                                     k.nT[:, n * BLK:(n + 1) * BLK], start=True, stop=True).then_inc(projected, 1)
                for t in range(TILES):
                    if t % 4 == 0 and t >= 8:
                        pe.wait_ge(v_kept, t // 4 - 1)
                    mm = nc.tensor.matmul(v_psum[:, (t // 4) % 2, (t % 4) * D:(t % 4 + 1) * D],
                                          k.nT[:, t * P:(t + 1) * P], w_qkv[:, 2 * D:3 * D], start=True, stop=True)
                    if t % 4 == 3:
                        mm.then_inc(v_done, 1)

            @block.scalar
            def _(act):
                act.wait_ge(w_in, 48)
                for step, (w, _) in enumerate(STEPS):
                    act.wait_ge(projected, step + 1)
                    if step >= 2:
                        act.wait_ge(rest1, step - 1)
                    nc.scalar.activation(full[:, step % 2, :], by_feature[:, step % 2, :], ACT.Identity,
                                         bias=b_col[:, w:w + 1]).then_inc(biased, 1)

            @block.vector
            def _(dve):
                for step in range(len(STEPS)):
                    par, buf = step % 2, step % CUTS
                    dve.wait_ge(biased, step + 1)
                    if step >= CUTS:
                        dve.wait_ge(saved[buf], 16 * (step // CUTS))
                    nc.vector.tensor_copy(cut[:, buf, 0, :], full[:, par, :]).then_inc(cut1, 1)
                    dve.wait_ge(cut1, step + 1)
                    nc.vector.tensor_tensor(rest[:, par, :], full[:, par, :], cut[:, buf, 0, :], ALU.subtract).then_inc(rest1, 1)
                    dve.wait_ge(rest1, step + 1)
                    nc.vector.tensor_copy(cut[:, buf, 1, :], rest[:, par, :]).then_inc(cut2, 1)
                    dve.wait_ge(cut2, step + 1)
                    nc.vector.tensor_tensor(cut[:, buf, 2, :], rest[:, par, :], cut[:, buf, 1, :], ALU.subtract).then_inc(rest2, 1)
                for n in range(BLOCKS):
                    dve.wait_ge(v_done, n + 1)
                    dve.wait_ge(w_in, 48)
                    b, kb = n // 2, 4 * (n % 2)
                    for t in range(4):
                        last = nc.vector.tensor_tensor(
                            v_all[:, b * HEADS0:(b + 1) * HEADS0, kb + t, :],
                            v_psum[:, n % 2, t * D:(t + 1) * D].rearrange("p (h d) -> p h d", h=HEADS0),
                            b_v[:].rearrange("p (h d) -> p h d", h=HEADS0), ALU.add)
                    last.then_inc(v_kept, 1)
                dve.wait_ge(v_kept, BLOCKS)

        heads = k.sb("heads", [P, KB, PAIRS_BH, HDIM0], ctx=outer)
        with ExitStack() as ctx:
            v_head = k.sb("v_head", [P, 2, KB, VW], ctx=ctx)
            row_min = k.sb("row_min", [P, 2, KB, 2], ctx=ctx)
            neg_max = k.sb("neg_max", [P, 2, KB], ctx=ctx)
            zeros = k.sb("zeros", [P, KB * HDIM0], ctx=ctx)
            max_rest = k.sb("max_rest", [P, 2, KB], ctx=ctx)
            max_cut = k.sb("max_cut", [P, 2, PARTS, KB], BF16, ctx)
            max_rows = k.sb("max_rows", [PARTS * KB, 2, P], BF16, ctx)
            probs = k.sb("probs", [P, 2, SEQ], ctx=ctx)
            sums = k.sb("sums", [P, 2, 2 * P], ctx=ctx)
            recip = k.sb("recip", [P, 2, 2, 4], ctx=ctx)
            first = k.ps("first", [P, 2, BLK], ctx=ctx)
            scores = k.ps("scores", [P, 2, SEQ], ctx=ctx)
            summed = k.ps("summed", [P, BLK], ctx=ctx)
            turn = k.ps("turn", [P, BLK], ctx=ctx)
            turn_b = turn[:].bitcast(BF16)
            turn_q = turn[:, 0:2 * P].rearrange("p (half c w) -> p half c w", half=2, c=4)
            (first_ready, first_read, joined, m1, r1, m2, r2, m3, rows_turned, rows_kept, rows_out, rows_in, v_zeroed, v_ready,
             scores_ready, probs_ready, probs_used, sums_kept, sums_turned, recip_done, head_done) = (
                k.sem(f"att_{s}") for s in (
                    "first_ready", "first_read", "joined", "m1", "r1", "m2", "r2", "m3", "rows_turned", "rows_kept",
                    "rows_out", "rows_in", "v_zeroed", "v_ready", "scores_ready", "probs_ready", "probs_used",
                    "sums_kept", "sums_turned", "recip_done", "head_done"))
            block = ctx.enter_context(nc.Block())
            LOOPS = PAIRS_BH // 2

            @block.sync
            def _(sp):
                fill_stacks(sp, 1)

            def over_heads(eng, step, between=None):
                step(0, True)
                if between:
                    with eng.Fori(1, HEADS0 // 2 - 1) as r:
                        step(r, True)
                    between()
                with eng.Fori(HEADS0 // 2 - 1 if between else 1, LOOPS - 1) as r:
                    step(r, True)
                step(LOOPS - 1, False)

            @block.tensor
            def _(pe):
                def find_max(j, t):
                    for half in range(2):
                        n = 2 * (KB * j + t) + half
                        if not (isinstance(n, int) and n < 2):
                            pe.wait_ge(first_read, n - 1)
                        nc.tensor.matmul(first[:, half, :], stack["q"][:, j, t * P:(t + 1) * P],
                                         stack["k"][:, j, half * BLK:(half + 1) * BLK],
                                         start=True, stop=True).then_inc(first_ready, 1)

                def turn_max(j, par):
                    pe.wait_ge(m3, j + 1)
                    if not (isinstance(j, int) and j < 3):
                        pe.wait_ge(head_done, j - 2)
                    if not (isinstance(j, int) and j < 1):
                        pe.wait_ge(rows_kept, j)
                    nc.tensor.transpose(turn_b[0:PARTS * KB, 0:P], max_cut[:, par].rearrange("p s t -> p (s t)"),
                                        identb[:]).then_inc(rows_turned, 1)

                def scores_of(i, kb):
                    n = KB * i + kb
                    if not (isinstance(n, int) and n < 2):
                        pe.wait_ge(probs_ready, n - 1)
                    for half in range(2):
                        mm = nc.tensor.matmul(scores[:, kb % 2, half * BLK:(half + 1) * BLK],
                                              stack["k"][:, i, kb * P:(kb + 1) * P],
                                              stack["q"][:, i, half * BLK:(half + 1) * BLK], start=True, stop=True)
                    mm.then_inc(scores_ready, 1)

                def sum_values(i, par, kb):
                    if kb == 0:
                        pe.wait_ge(v_ready, i + 1)
                        if not (isinstance(i, int) and i < 1):
                            pe.wait_ge(sums_kept, i)
                    pe.wait_ge(probs_ready, KB * i + kb + 1)
                    for c in range(4):
                        mm = nc.tensor.matmul(summed[VW * c:VW * (c + 1), 0:2 * P], v_head[:, par, kb, :],
                                              probs[:, kb % 2, c * 2 * P:(c + 1) * 2 * P],
                                              start=(kb == 0), stop=(kb == KB - 1))
                    mm.then_inc(probs_used, 1)

                def turn_sums(i, par, rows):
                    pe.wait_ge(sums_kept, i + 1)
                    pe.wait_ge(rows_kept, rows)
                    if not (isinstance(i, int) and i < 1):
                        pe.wait_ge(head_done, i)
                    for half in range(2):
                        mm = nc.tensor.transpose(turn[:, half * P:(half + 1) * P], sums[:, par, half * P:(half + 1) * P],
                                                 k.ident[:])
                    mm.then_inc(sums_turned, 1)

                def step(r, ahead):
                    for par in range(2):
                        i = 2 * r + par
                        pe.wait_ge(rows_in, 16 * i + 16)
                        for kb in range(KB):
                            if ahead:
                                find_max(i + 2, kb)
                            scores_of(i, kb)
                            if kb >= 1:
                                sum_values(i, par, kb - 1)
                            elif not (isinstance(i, int) and i == 0):
                                sum_values(i - 1, 1 - par, KB - 1)
                            if kb == 1 and (ahead or par == 0):
                                turn_max(i + 1, 1 - par)
                            if kb == 3 and not (isinstance(i, int) and i == 0):
                                turn_sums(i - 1, 1 - par, i + 2 if (ahead or par == 0) else PAIRS_BH)

                for j in range(2):
                    for t in range(KB):
                        find_max(j, t)
                turn_max(0, 0)
                over_heads(pe, step, lambda: pe.wait_ge(stacked[1], 16 * 2 * len(PAIRS)))
                sum_values(PAIRS_BH - 1, 1, KB - 1)
                turn_sums(PAIRS_BH - 1, 1, PAIRS_BH)

            @block.vector
            def _(dve):
                def find_max(j, par, t):
                    if t == 0 and not (isinstance(j, int) and j < 2):
                        dve.wait_ge(joined, j - 1)
                    for half in range(2):
                        dve.wait_ge(first_ready, 2 * (KB * j + t) + half + 1)
                        nc.vector.tensor_reduce(row_min[:, par, t, half:half + 1], first[:, half, :], AX_X, ALU.max,
                                                negate=True).then_inc(first_read, 1)

                def join(j, par):
                    dve.wait_ge(first_read, 2 * KB * (j + 1))
                    if not (isinstance(j, int) and j < 2):
                        dve.wait_ge(m3, j - 1)
                    nc.vector.tensor_reduce(neg_max[:, par, :], row_min[:, par], AX_X, ALU.min).then_inc(joined, 1)

                def keep_rows(j, par):
                    dve.wait_ge(rows_turned, j + 1)
                    if not (isinstance(j, int) and j < 2):
                        dve.wait_ge(rows_out, 16 * j - 16)
                    nc.vector.tensor_copy(max_rows[:, par, :], turn_b[0:PARTS * KB, 0:P]).then_inc(rows_kept, 1)

                def divide(i, par):
                    dve.wait_ge(sums_turned, i + 1)
                    if not (isinstance(i, int) and i < 2):
                        dve.wait_ge(head_done, i - 1)
                    nc.vector.reciprocal(recip[:, par], turn_q[:, :, :, HDIM0]).then_inc(recip_done, 1)
                    dve.wait_ge(recip_done, i + 1)
                    nc.vector.tensor_tensor(
                        heads[:, :, i, :].rearrange("p (c half) d -> p half c d", half=2), turn_q[:, :, :, 0:HDIM0],
                        recip[:, par].unsqueeze(3).broadcast_to([P, 2, 4, HDIM0]), ALU.mult).then_inc(head_done, 1)

                def step(r, ahead):
                    for par in range(2):
                        i = 2 * r + par
                        for kb in range(KB):
                            if ahead:
                                find_max(i + 2, par, kb)
                            if kb == 2 and (ahead or par == 0):
                                keep_rows(i + 1, 1 - par)
                            if kb == 5 and not (isinstance(i, int) and i == 0):
                                divide(i - 1, 1 - par)
                        if ahead:
                            join(i + 2, par)

                for j in range(2):
                    for t in range(KB):
                        find_max(j, j, t)
                    join(j, j)
                keep_rows(0, 0)
                over_heads(dve, step)
                divide(PAIRS_BH - 1, 1)
                dve.wait_ge(head_done, PAIRS_BH)

            @block.scalar
            def _(act):
                def keep_sums(i, par):
                    act.wait_ge(probs_used, KB * (i + 1))
                    if not (isinstance(i, int) and i < 2):
                        act.wait_ge(sums_turned, i - 1)
                    nc.scalar.copy(sums[:, par, :], summed[:, 0:2 * P]).then_inc(sums_kept, 1)

                def rows_to_dram(j, par):
                    act.wait_ge(rows_kept, j + 1)
                    act.dma_start(max_dram[j], max_rows[:, par, :]).then_inc(rows_out, 16)

                def rows_to_stack(j):
                    act.wait_ge(rows_out, 16 * j + 16)
                    if not (isinstance(j, int) and j < 1):
                        act.wait_ge(rows_in, 16 * j)
                    act.dma_start(stack["q"][MAX_ROW:MAX_ROW + PARTS, j, :],
                                  max_dram[j].rearrange("(s t) q -> s (t q)", s=PARTS)).then_inc(rows_in, 16)

                def step(r, ahead):
                    for par in range(2):
                        i = 2 * r + par
                        for kb in range(KB):
                            if kb == 3 and (ahead or par == 0):
                                rows_to_dram(i + 1, 1 - par)
                            if kb == 5 and (ahead or par == 0):
                                rows_to_stack(i + 1)
                            n = KB * i + kb
                            act.wait_ge(scores_ready, n + 1)
                            if not (isinstance(n, int) and n < 2):
                                act.wait_ge(probs_used, n - 1)
                            nc.scalar.activation(probs[:, kb % 2, :], scores[:, kb % 2, :], ACT.Exp,
                                                 scale=SCALE0).then_inc(probs_ready, 1)
                            if kb == 0 and not (isinstance(i, int) and i == 0):
                                keep_sums(i - 1, 1 - par)

                rows_to_dram(0, 0)
                rows_to_stack(0)
                over_heads(act, step)
                keep_sums(PAIRS_BH - 1, 1)

            @block.gpsimd
            def _(pool):
                def cut_max(j, par):
                    pool.wait_ge(joined, j + 1)
                    if not (isinstance(j, int) and j < 2):
                        pool.wait_ge(rows_turned, j - 1)
                    nc.gpsimd.tensor_tensor(max_cut[:, par, 0, :], neg_max[:, par, :], zeros[:, 0:KB], ALU.add).then_inc(m1, 1)
                    pool.wait_ge(m1, j + 1)
                    nc.gpsimd.tensor_tensor(max_rest[:, par, :], neg_max[:, par, :], max_cut[:, par, 0, :],
                                            ALU.subtract).then_inc(r1, 1)
                    pool.wait_ge(r1, j + 1)
                    nc.gpsimd.tensor_tensor(max_cut[:, par, 1, :], max_rest[:, par, :], zeros[:, 0:KB], ALU.add).then_inc(m2, 1)
                    pool.wait_ge(m2, j + 1)
                    nc.gpsimd.tensor_tensor(max_cut[:, par, 2, :], max_rest[:, par, :], max_cut[:, par, 1, :],
                                            ALU.subtract).then_inc(m3, 1)

                def take_values(i, par):
                    if not (isinstance(i, int) and i < 2):
                        pool.wait_ge(probs_used, KB * (i - 1))
                    nc.gpsimd.tensor_tensor(v_head[:, par, :, 0:HDIM0], v_all[:, i],
                                            zeros[:].rearrange("p (t d) -> p t d", t=KB), ALU.add).then_inc(v_ready, 1)

                def step(r, ahead):
                    for par in range(2):
                        i = 2 * r + par
                        take_values(i, par)
                        if ahead:
                            cut_max(i + 2, par)

                nc.gpsimd.memset(v_head[:], 0.0).then_inc(v_zeroed, 1)
                pool.wait_ge(v_zeroed, 1)
                nc.gpsimd.memset(v_head[:, :, :, HDIM0:HDIM0 + 1], 1.0).then_inc(v_zeroed, 1)
                nc.gpsimd.memset(zeros[:], 0.0).then_inc(v_zeroed, 1)
                pool.wait_ge(v_zeroed, 3)
                for j in range(2):
                    cut_max(j, j)
                over_heads(pool, step)

        with ExitStack() as ctx:
            w_proj = k.sb("w_proj", [D, D], ctx=ctx)
            b_proj = k.sb("b_proj", [P, D], ctx=ctx)
            heads_T = k.sb("heads_T", [P, TILES, P], ctx=ctx)
            turned = k.ps("proj_turned", [P, 4, BLK], ctx=ctx)
            out = k.ps("proj_out", [P, 4, BLK], ctx=ctx)
            w_in, turned_done, kept, out_done, bias_added, done = (
                k.sem(f"proj_{s}") for s in ("w_in", "turned_done", "kept", "out_done", "bias_added", "done"))
            block = ctx.enter_context(nc.Block())

            @block.sync
            def _(sp):
                sp.dma_start(w_proj[:], a["L0_attn_W_proj"]).then_inc(w_in, 16)
                sp.dma_start(b_proj[:], a["L0_attn_b_proj"].partition_broadcast(P)).then_inc(w_in, 16)

            @block.tensor
            def _(pe):
                for t in range(TILES):
                    b, kb = t // KB, t % KB
                    mm = nc.tensor.transpose(turned[:, t // 4, (t % 4) * P:(t % 4 + 1) * P],
                                             heads[:, kb, b * HEADS0:(b + 1) * HEADS0, :], k.ident[:])
                    if t % 4 == 3:
                        mm.then_inc(turned_done, 1)
                pe.wait_ge(w_in, 32)
                for t in range(TILES):
                    pe.wait_ge(kept, t // 4 + 1)
                    mm = nc.tensor.matmul(out[:, t // 4, (t % 4) * P:(t % 4 + 1) * P], heads_T[:, t, :], w_proj[:],
                                          start=True, stop=True)
                    if t % 4 == 3:
                        mm.then_inc(out_done, 1)

            @block.scalar
            def _(act):
                for n in range(BLOCKS):
                    act.wait_ge(turned_done, n + 1)
                    nc.scalar.copy(heads_T[:, 4 * n:4 * n + 4, :], turned[:, n, :].rearrange("p (t q) -> p t q", t=4)).then_inc(kept, 1)

            @block.vector
            def _(dve):
                dve.wait_ge(w_in, 32)
                nc.vector.tensor_tensor(k.x[:], k.x[:], b_proj[:].unsqueeze(1).broadcast_to([P, TILES, D]),
                                        ALU.add).then_inc(bias_added, 1)
                dve.wait_ge(bias_added, 1)
                for n in range(BLOCKS):
                    dve.wait_ge(out_done, n + 1)
                    nc.vector.tensor_tensor(k.x[:, 4 * n:4 * n + 4, :], out[:, n, :].rearrange("p (t d) -> p t d", t=4),
                                            k.x[:, 4 * n:4 * n + 4, :], ALU.add).then_inc(done, 1)
                dve.wait_ge(done, BLOCKS)


class HiddenWeights:

    def __init__(self, k, tag, ctx, loads, loads_per, experts):
        self.loads, self.loads_per, self.experts = loads, loads_per, experts
        self.pars = min(experts, 2)
        self.w1 = k.sb(f"{tag}_w1", [D, self.pars, FFN], ctx=ctx)
        self.w2 = k.sb(f"{tag}_w2", [P, self.pars, FFN // P, D], ctx=ctx)
        self.b1 = k.sb(f"{tag}_b1", [P, self.pars, FFN // P], ctx=ctx)
        self.loaded = [k.sem(f"{tag}_loaded{i}") for i in range(self.pars)]

    def load(self, sp, e):
        par = e % 2
        for dst, src in self.loads(e, par, self.w1[:, par], self.w2[:, par], self.b1[:, par]):
            sp.dma_start(dst, src, allow_slow_non_contiguous=True).then_inc(self.loaded[par], 16)

    def load_first(self, sp):
        for par in range(self.pars):
            self.load(sp, par)


def feed_forward(k, tag, weights, func, has_bias, finish):
    nc = k.nc
    FC = FFN // P
    experts, pars, loads_per = weights.experts, weights.pars, weights.loads_per
    w1, w2, b1, loaded = weights.w1, weights.w2, weights.b1, weights.loaded
    with ExitStack() as ctx:
        hidden = k.sb(f"{tag}_hidden", [P, 2, FC, BLK], ctx=ctx)
        up = k.ps(f"{tag}_up", [P, FC, BLK], ctx=ctx)
        down = k.ps(f"{tag}_down", [P, 2, BLK], ctx=ctx)
        up_ready, hidden_ready, down_ready, down_read = (
            k.sem(f"{tag}_{s}") for s in ("up_ready", "hidden_ready", "down_ready", "down_read"))

        def weights_in(eng, r, par):
            eng.wait_ge(loaded[par], 16 * loads_per * (r + 1))

        parts = finish(ctx, down, down_ready, down_read, weights_in)
        block = ctx.enter_context(nc.Block())

        def over_experts(eng, body):
            for par in range(pars):
                body(0, par)
            if experts > 2:
                with eng.Fori(1, experts // 2) as r:
                    for par in range(2):
                        body(r, par)

        @block.sync
        def _(sp):
            for e in range(2, experts):
                sp.wait_ge(down_ready, BLOCKS * (e - 1))
                parts["used"](sp, e - 2)
                weights.load(sp, e)

        @block.tensor
        def _(pe):
            def body(r, par):
                weights_in(pe, r, par)
                for blk in range(BLOCKS):
                    m = (pars * r + par) * BLOCKS + blk
                    for f in range(FC):
                        if not (isinstance(m, int) and m == 0):
                            pe.wait_ge(hidden_ready, FC * (m - 1) + f + 1)
                        nc.tensor.matmul(up[:, f, :], w1[:, par, f * P:(f + 1) * P], k.nT[:, blk * BLK:(blk + 1) * BLK],
                                         start=True, stop=True).then_inc(up_ready, 1)
                    if isinstance(m, int) and m == 0 and "tensor_between" in parts:
                        parts["tensor_between"](pe)
                    if not (isinstance(m, int) and m < 2):
                        pe.wait_ge(down_read, m - 1)
                    for f in range(FC):
                        pe.wait_ge(hidden_ready, FC * m + f + 1)
                        for t in range(4):
                            mm = nc.tensor.matmul(down[:, blk % 2, t * D:(t + 1) * D], hidden[:, blk % 2, f, t * P:(t + 1) * P],
                                                  w2[:, par, f, :], start=(f == 0 and t == 0), stop=(f == FC - 1),
                                                  skip_group_check=True)
                    mm.then_inc(down_ready, 1)

            over_experts(pe, body)

        @block.scalar
        def _(act):
            def body(r, par):
                weights_in(act, r, par)
                for blk in range(BLOCKS):
                    m = (pars * r + par) * BLOCKS + blk
                    if not (isinstance(m, int) and m < 2):
                        act.wait_ge(down_ready, m - 1)
                    for f in range(FC):
                        act.wait_ge(up_ready, FC * m + f + 1)
                        nc.scalar.activation(hidden[:, blk % 2, f, :], up[:, f, :], func,
                                             bias=b1[:, par, f:f + 1] if has_bias else 0.0).then_inc(hidden_ready, 1)
                    if isinstance(m, int) and m == 0 and "scalar_after_first" in parts:
                        parts["scalar_after_first"](act)

            over_experts(act, body)

        @block.vector
        def _(dve):
            parts["vector"](dve)

        @block.gpsimd
        def _(pool):
            if "gpsimd" in parts:
                parts["gpsimd"](pool)


def top_two(k, tag, ctx, logits):
    nc = k.nc
    W = [P, TILES, EXPERTS]
    b = {s: k.sb(f"{tag}_{s}", W, ctx=ctx) for s in ("at_top", "index", "hot1", "hot2", "others")}
    v = {s: k.sb(f"{tag}_{s}", [P, TILES], ctx=ctx) for s in ("top1", "top2", "index1", "index2")}

    def wide(x):
        return x[:].unsqueeze(2).broadcast_to(W)

    def steps(dve):
        iota = k.iota[:].unsqueeze(1).broadcast_to(W)
        source = logits
        for top, index, hot in (("top1", "index1", "hot1"), ("top2", "index2", "hot2")):
            k.link(dve, nc.vector.tensor_reduce(v[top][:], source[:], AX_X, ALU.max))
            k.link(dve, nc.vector.tensor_tensor(b["at_top"][:], source[:], wide(v[top]), ALU.is_lt))
            k.link(dve, nc.vector.scalar_tensor_tensor(b["index"][:], b["at_top"][:], 2.0 * EXPERTS, iota, ALU.mult, ALU.add))
            k.link(dve, nc.vector.tensor_reduce(v[index][:], b["index"][:], AX_X, ALU.min))
            k.link(dve, nc.vector.tensor_tensor(b[hot][:], iota, wide(v[index]), ALU.is_equal))
            if source is logits:
                k.link(dve, nc.vector.scalar_tensor_tensor(b["others"][:], b[hot][:], -3.0e38, logits[:], ALU.mult, ALU.add))
                source = b["others"]

    return b, v, steps


def feed_forward0(k, a):
    nc = k.nc
    with ExitStack() as ctx:
        gate_w = k.sb("f0_gate_w", [D, EXPERTS], ctx=ctx)
        logits = k.sb("f0_logits", [P, TILES, EXPERTS], ctx=ctx)
        shifted = k.sb("f0_shifted", [P, TILES, EXPERTS], ctx=ctx)
        expd = k.sb("f0_expd", [P, TILES, EXPERTS], ctx=ctx)
        picked = k.sb("f0_picked", [P, TILES, EXPERTS], ctx=ctx)
        total, total_r, g1, g2, both, denom, denom_r, coef1, coef2, coef = (
            k.sb(f"f0_{s}", [P, TILES], ctx=ctx)
            for s in ("total", "total_r", "g1", "g2", "both", "denom", "denom_r", "coef1", "coef2", "coef"))
        w_in, logits_done, shifted_done, expd_done = (
            k.sem(f"f0_{s}") for s in ("w_in", "logits_done", "shifted_done", "expd_done"))
        hot, top, steps = top_two(k, "f0", ctx, logits)

        def loads(e, par, w1, w2, b1):
            return [(w1, a["L0_ffn_w1"]), (w2, a["L0_ffn_w2"].rearrange("(f p) d -> p f d", p=P))]

        weights = HiddenWeights(k, "f0", ctx, loads, 2, 1)

        def prefetch(sp):
            sp.dma_start(gate_w[:], a["L0_ffn_Wg"]).then_inc(w_in, 16)
            weights.load_first(sp)

        layer_norm(k, "ln1", k.x, 1e-5, k.n, k.nT, prefetch=prefetch)
        def finish(ctx, down, down_ready, down_read, weights_in):
            gates = k.ps("f0_gates", [P, TILES, EXPERTS], ctx=ctx)

            def route(pe):
                pe.wait_ge(w_in, 16)
                for t in range(TILES):
                    mm = nc.tensor.matmul(gates[:, t, :], k.nT[:, t * P:(t + 1) * P], gate_w[:], start=True, stop=True)
                mm.then_inc(logits_done, 1)

            def exponentials(act):
                act.wait_ge(shifted_done, 1)
                nc.scalar.activation(expd[:], shifted[:], ACT.Exp).then_inc(expd_done, 1)

            def find_coefficients(dve):
                W = [P, TILES, EXPERTS]
                dve.wait_ge(logits_done, 1)
                k.link(dve, nc.vector.tensor_copy(logits[:], gates[:]))
                steps(dve)
                nc.vector.tensor_tensor(shifted[:], logits[:], top["top1"][:].unsqueeze(2).broadcast_to(W),
                                        ALU.subtract).then_inc(shifted_done, 1)
                dve.wait_ge(expd_done, 1)

                k.link(dve, nc.vector.tensor_reduce(total[:], expd[:], AX_X, ALU.add))
                k.link(dve, nc.vector.reciprocal(total_r[:], total[:]))
                for h, g in (("hot1", g1), ("hot2", g2)):
                    k.link(dve, nc.vector.tensor_tensor(picked[:], expd[:], hot[h][:], ALU.mult))
                    k.link(dve, nc.vector.tensor_reduce(g[:], picked[:], AX_X, ALU.add))
                    k.link(dve, nc.vector.tensor_tensor(g[:], g[:], total_r[:], ALU.mult))
                k.link(dve, nc.vector.tensor_tensor(both[:], g1[:], g2[:], ALU.add))
                k.link(dve, nc.vector.tensor_scalar(denom[:], both[:], float(np.finfo(np.float32).eps), None, ALU.max))
                k.link(dve, nc.vector.reciprocal(denom_r[:], denom[:]))
                k.link(dve, nc.vector.tensor_tensor(coef1[:], g1[:], denom_r[:], ALU.mult))
                k.link(dve, nc.vector.tensor_tensor(coef2[:], g2[:], denom_r[:], ALU.mult))
                k.link(dve, nc.vector.tensor_tensor(coef[:], coef1[:], coef2[:], ALU.add))

            def vector(dve):
                find_coefficients(dve)
                for blk in range(BLOCKS):
                    dve.wait_ge(down_ready, blk + 1)
                    for t in range(4):
                        i = 4 * blk + t
                        last = nc.vector.scalar_tensor_tensor(k.x[:, i, :], down[:, blk % 2, t * D:(t + 1) * D], coef[:, i:i + 1],
                                                              k.x[:, i, :], ALU.mult, ALU.add)
                    last.then_inc(down_read, 1)
                dve.wait_ge(down_read, BLOCKS)

            return {"vector": vector, "tensor_between": route, "scalar_after_first": exponentials}

        feed_forward(k, "f0", weights, ACT.Relu, False, finish)


def delta_layer(k, a):
    nc = k.nc
    H, B = HEADS1, BATCH
    CHUNKS = SEQ_TILES
    GATES = TILES * H
    UNITS = [(b, g) for b in range(B) for g in range(H // GROUP)]
    NU = len(UNITS)
    W = GROUP * P
    NLEV = len(LEVELS)
    HALF = P // 2

    with ExitStack() as outer:
        mixed = k.sb("mixed", [P, TILES, D], ctx=outer)
        normT = k.nT
        rows = {s: k.sb(f"d_{s}", [D, 1], ctx=outer) for s in ("ln1_w", "ln1_b", "ln2_w", "ln2_b")}
        rows_in = k.sem("d_rows_in")
        with ExitStack() as gated:
            names = ("summed", "neg_summed", "beta", "neg_beta", "grown", "neg_beta_grown", "rest", "last")
            all_gates = k.sb("d_all_gates", [P, TILES, len(names), H], ctx=gated)
            gate = {s: all_gates[:, :, i, :] for i, s in enumerate(names)}
            upper = k.sb("d_upper", [P, P], ctx=gated)
            summed_dram = nc.dram_tensor("summed_dram", [TILES, H * P], F32)
            w_ab = k.sb("d_w_ab", [D, 2, H], ctx=gated)
            w_qkv = k.sb("g_w_qkv", [D, 3, H * P], ctx=gated)
            w_o = k.sb("g_w_o", [P, H, D], ctx=gated)
            level_masks = k.sb("g_level_masks", [P, NLEV, HALF], ctx=gated)
            block_of = k.sb("g_block_of", [P, P // BASE], ctx=gated)
            delta = k.sb("g_delta", [P, BASE], ctx=gated)
            below = k.sb("g_below", [P, P], ctx=gated)
            w_in, weights_in = k.sem("d_w_in"), k.sem("g_weights_in")

            def prefetch(sp):
                for s, t in rows.items():
                    sp.dma_start(t[:], a[f"L1_attn_{s}"].rearrange("(d o) -> d o", o=1)).then_inc(rows_in, 16)
                sp.dma_start(w_ab[:, 0, :], a["L1_attn_Wa"]).then_inc(w_in, 16)
                sp.dma_start(w_ab[:, 1, :], a["L1_attn_Wb"]).then_inc(w_in, 16)
                sp.dma_start(upper[:], a["upper"]).then_inc(w_in, 16)
                for i, w in enumerate(("Wq", "Wk", "Wv")):
                    sp.dma_start(w_qkv[:, i, :], a[f"L1_attn_{w}"]).then_inc(weights_in, 16)
                sp.dma_start(w_o[:], a["L1_attn_Wo"].rearrange("(h v) d -> v h d", v=P)).then_inc(weights_in, 16)
                sp.dma_start(level_masks[:], a["levels"].rearrange("p (l c) -> p l c", l=NLEV)).then_inc(weights_in, 16)
                sp.dma_start(block_of[:], a["block_of"]).then_inc(weights_in, 16)
                sp.dma_start(delta[:], a["delta"]).then_inc(weights_in, 16)
                sp.dma_start(below[:], a["below"]).then_inc(weights_in, 16)
                sp.wait_ge(rows_in, 64)

            layer_norm(k, "ln2", k.x, 1e-5, k.n, prefetch=prefetch)
            layer_norm(k, "ln3", k.n, 1e-5, mixed, normT, rows["ln1_w"], rows["ln1_b"])

            with ExitStack() as ctx:
                z = k.sb("d_z", [P, 2, TILES, H], ctx=ctx)
                size, soft, tmp = (k.sb(f"d_{s}", [P, 2, TILES, H], ctx=ctx) for s in ("size", "soft", "tmp"))
                ones = k.sb("d_ones", [P, P], ctx=ctx)
                log_a = k.sb("d_log_a", [P, TILES, H], ctx=ctx)
                summed_T = k.sb("d_summed_T", [P, P], ctx=ctx)
                logits = k.ps("d_logits", [P, TILES, 2 * H], ctx=ctx)
                sums = k.ps("d_sums", [P, 2, BLK], ctx=ctx)
                z_done, operands, taken, ones_set, log_a_done, sums_done, rows_ready, rows_saved, done = (
                    k.sem(f"d_{s}") for s in ("z_done", "operands", "taken", "ones_set", "log_a_done", "sums_done", "rows_ready",
                                              "rows_saved", "gates_done"))
                block = ctx.enter_context(nc.Block())

                @block.sync
                def _(sp):
                    sp.wait_ge(rows_ready, 1)
                    sp.dma_start(summed_dram.rearrange("t (h p) -> (t h) p", h=H), summed_T[:]).then_inc(rows_saved, 16)
                    sp.wait_ge(rows_saved, 16)

                @block.gpsimd
                def _(pool):
                    nc.gpsimd.memset(ones[:], 1.0).then_inc(ones_set, 1)
                    pool.wait_ge(ones_set, 1)

                @block.tensor
                def _(pe):
                    pe.wait_ge(w_in, 48)
                    for t in range(TILES):
                        mm = nc.tensor.matmul(logits[:, t, :], normT[:, t * P:(t + 1) * P], w_ab[:].rearrange("d w h -> d (w h)"),
                                              start=True, stop=True)
                    mm.then_inc(z_done, 1)
                    pe.wait_ge(log_a_done, 1)
                    pe.wait_ge(ones_set, 1)
                    columns = log_a[:].rearrange("p t h -> p (t h)")
                    nc.tensor.matmul(sums[:, 0, 0:GATES], upper[:], columns, start=True, stop=True)
                    nc.tensor.matmul(sums[:, 0, GATES:GATES + P], columns, upper[:], start=True, stop=True)
                    nc.tensor.matmul(sums[:, 1, 0:GATES], ones[:], columns, start=True, stop=True).then_inc(sums_done, 1)

                @block.scalar
                def _(act):
                    act.wait_ge(operands, 1)
                    nc.scalar.activation(soft[:], size[:], ACT.Exp, scale=-1.0).then_inc(taken, 1)
                    act.wait_ge(operands, 2)
                    nc.scalar.activation(tmp[:, 0], size[:, 0], ACT.Ln).then_inc(taken, 1)
                    act.wait_ge(operands, 3)
                    nc.scalar.activation(gate["grown"], gate["summed"], ACT.Exp).then_inc(taken, 1)
                    nc.scalar.activation(gate["rest"], z[:, 0], ACT.Exp).then_inc(taken, 1)
                    nc.scalar.activation(gate["last"], size[:, 1], ACT.Exp).then_inc(taken, 1)

                @block.vector
                def _(dve):
                    dve.wait_ge(z_done, 1)
                    k.link(dve, nc.vector.tensor_copy(z[:], logits[:].rearrange("p t (w h) -> p w t h", w=2)))
                    k.link(dve, nc.vector.tensor_scalar(tmp[:], z[:], -1.0, None, ALU.mult))
                    nc.vector.tensor_tensor(size[:], z[:], tmp[:], ALU.max).then_inc(operands, 1)
                    dve.wait_ge(taken, 1)
                    k.link(dve, nc.vector.tensor_scalar(size[:], soft[:], 1.0, None, ALU.add))
                    nc.vector.tensor_scalar(z[:, 0], z[:, 0], 0.0, None, ALU.min).then_inc(operands, 1)
                    k.link(dve, nc.vector.reciprocal(tmp[:, 1], size[:, 1]))
                    k.link(dve, nc.vector.tensor_scalar(z[:, 1], z[:, 1], 0.0, None, ALU.is_ge))
                    k.link(dve, nc.vector.tensor_tensor(soft[:, 1], soft[:, 1], z[:, 1], ALU.max))
                    k.link(dve, nc.vector.tensor_tensor(gate["beta"], soft[:, 1], tmp[:, 1], ALU.mult))
                    k.link(dve, nc.vector.tensor_scalar(gate["neg_beta"], gate["beta"], -1.0, None, ALU.mult))
                    dve.wait_ge(taken, 2)
                    nc.vector.tensor_tensor(log_a[:], z[:, 0], tmp[:, 0], ALU.subtract).then_inc(log_a_done, 1)
                    dve.wait_ge(sums_done, 1)
                    dve.wait_ge(log_a_done, 1)
                    nc.vector.tensor_copy(summed_T[:], sums[:, 0, GATES:GATES + P]).then_inc(rows_ready, 1)
                    k.link(dve, nc.vector.tensor_copy(gate["summed"], sums[:, 0, 0:GATES].rearrange("p (t h) -> p t h", h=H)))
                    k.link(dve, nc.vector.tensor_copy(size[:, 1].rearrange("p t h -> p (t h)"), sums[:, 1, 0:GATES]))
                    k.link(dve, nc.vector.tensor_scalar(gate["neg_summed"], gate["summed"], -1.0, None, ALU.mult))
                    nc.vector.tensor_tensor(z[:, 0], size[:, 1], gate["summed"], ALU.subtract).then_inc(operands, 1)
                    dve.wait_ge(taken, 5)
                    nc.vector.tensor_tensor(gate["neg_beta_grown"], gate["neg_beta"], gate["grown"], ALU.mult).then_inc(done, 1)
                    dve.wait_ge(done, 1)

            with ExitStack() as ctx:
                NG = H // GROUP
                NB = P // BASE
                blocks_dram = nc.dram_tensor("blocks_dram", [B, H, NB, BASE, BASE], F32)
                inverse = k.sb("g_inverse", [P, NB, BASE], ctx=ctx)
                rows_of = k.sb("g_rows_of", [P, NB, BASE * BASE], ctx=ctx)
                products = k.sb("g_products", [P, NB, BASE], ctx=ctx)
                chunk_T = k.sb("g_chunk_T", [D, B, P], ctx=ctx)
                chunk_gates = k.sb("g_chunk_gates", [P, B, len(names), H], ctx=ctx)
                state, kt, v, kT, qT, qgT, decay, coupling = (k.sb(f"g_{s}", [P, B, NG, W], ctx=ctx)
                                                    for s in ("state", "kt", "v", "kT", "qT", "qgT", "decay", "coupling"))
                q, qg, kk, sum_rows, masked = (k.sb(f"g_{s}", [P, NG, W], ctx=ctx)
                                                 for s in ("q", "qg", "k", "sum_rows", "masked"))
                square = k.sb("g_square", [P, NG, 2, W], ctx=ctx)
                eps = k.sb("g_eps", [P, 2 * GROUP], ctx=ctx)
                squares, shifted, inv_norm = (k.sb(f"g_{s}", [P, NG, 2 * GROUP], ctx=ctx) for s in ("squares", "shifted", "inv_norm"))
                raw, attend, solve_T, solve, update, out_T = (
                    k.sb(f"g_{s}", [P, NG, W], ctx=ctx)
                    for s in ("raw", "attend", "solve_T", "solve", "update", "out_T"))
                partial = k.sb("g_partial", [P, NG, GROUP * HALF], ctx=ctx)
                front_bank = k.ps("g_front_bank", [P, 2, NG, W], ctx=ctx)
                back_bank = k.ps("g_back_bank", [P, 2, NG, W], ctx=ctx)

                sem_names = (
                    
                    "chunk_ready", "q_proj", "k_proj", "v_proj", "q_silu", "k_silu", "v_silu",
                    "squares_done", "shifted_done", "norm_done", "k_done", "q_done", "qg_done", "v_done",
                    "eps_set", "rows_in", "masked", "kT_turned", "kT_kept", "qT_turned", "qT_kept", "qgT_turned", "qgT_kept", "decay_done",
                    "kk_done", "raw_done", "kq_done", "attend_done", "coup_turned", "coup_done", "blocks_out", "blocks_in",
                    "solved", "inverse_turned", "base_done",
                    "solve_turned", "solve_kept", "m_done", "m_read", "n_done", "n_read", "t_turned", "t_kept",
                    "ks_done", "v_ready", "u_done", "u_kept", "o_done", "o_kept", "ds_done", "state_done", "wo_done", "mixed_done")
                s_ = {n: k.sem(f"g_{n}") for n in sem_names}
                block = ctx.enter_context(nc.Block())
                WEIGHTS = 16 * 8

                SOLVE_STEPS = 2 * BASE
                EARLY, MIDDLE = 4, 8

                def heads4(t):
                    return t.rearrange("p (h c) -> p h c", h=GROUP)

                def wide(col):
                    return col.unsqueeze(2).broadcast_to([P, GROUP, P])

                def spread4(mask):
                    return mask.unsqueeze(1).broadcast_to([P, GROUP, mask.shape[-1]])

                def odd(t, s):
                    return t.rearrange("p (n two s) -> p n two s", two=2, s=s)[:, :, 1, :]

                def columns(t, col, s):
                    return t[:, col:col + s] if len(t.shape) == 2 else t[:, col // s, :]

                def head(t, h):
                    return t[:, h * P:(h + 1) * P]

                def cols(name, b, g):
                    return chunk_gates[:, b, names.index(name), g * GROUP:(g + 1) * GROUP]

                def first_item(c, b):
                    return isinstance(c, int) and c == 0 and b == 0

                def before(c, b):
                    return (c, 0) if b else (c - 1, 1)

                def waiter(eng):
                    def w(name, c, b, g, back=0):
                        n = NG * (B * c + b - back) + g + 1
                        if not (isinstance(n, int) and n <= 0):
                            eng.wait_ge(s_[name], n)
                    return w

                def level_waiter(eng):
                    def w(name, c, b, g, lev, levels=NLEV):
                        eng.wait_ge(s_[name], NG * (levels * (B * c + b) + lev) + g + 1)
                    return w

                def over_items(eng, front, back):
                    front(0, 0)
                    back(0, 0, (0, 1))
                    back(0, 1, (1, 0))
                    with eng.Fori(1, CHUNKS - 1) as c:
                        back(c, 0, (c, 1))
                        back(c, 1, (c + 1, 0))
                    back(CHUNKS - 1, 0, (CHUNKS - 1, 1))
                    back(CHUNKS - 1, 1, None)

                @block.sync
                def _(sp):
                    def move_item(c, b):
                        n = B * c + b + 1
                        waiter(sp)("masked", c, b, NG - 1, back=1)
                        sp.dma_start(sum_rows[:].rearrange("p g w -> p (g w)"),
                                     summed_dram[b * CHUNKS + c].partition_broadcast(P)).then_inc(s_["rows_in"], 16)
                        waiter(sp)("coup_done", c, b, NG - 1)
                        for j in range(NB):
                            sp.dma_start(
                                blocks_dram[b, :, j].rearrange("h i k -> i h k"),
                                coupling[j * BASE:(j + 1) * BASE, b].rearrange("p g (h c) -> p (g h) c", h=GROUP)[:, :, j * BASE:(j + 1) * BASE],
                            ).then_inc(s_["blocks_out"], 16)
                        sp.wait_ge(s_["blocks_out"], 16 * NB * n)
                        sp.dma_start(rows_of[:].rearrange("p j x -> p (j x)"),
                                     blocks_dram[b].rearrange("h j i k -> h (j i k)").unsqueeze(1)
                                     .broadcast_to([H, BASE, NB * BASE * BASE])).then_inc(s_["blocks_in"], 16)

                    def back(c, b, ahead):
                        if ahead:
                            move_item(*ahead)

                    over_items(sp, move_item, back)

                @block.tensor
                def _(pe):
                    w, w_level = waiter(pe), level_waiter(pe)
                    pe.wait_ge(weights_in, WEIGHTS)

                    def each_head(out, lhs, rhs, done, width=P):
                        for h in range(GROUP):
                            mm = nc.tensor.matmul(out[:, h * width:(h + 1) * width], lhs(h), rhs(h), start=True, stop=True)
                        mm.then_inc(s_[done], 1)

                    def merge(out, lhs, rhs, s, done):
                        for h in range(GROUP):
                            if s < 32:
                                mm = nc.tensor.matmul(out[:, h * HALF:(h + 1) * HALF], head(lhs, h), rhs(h), start=True, stop=True)
                            else:
                                for even in range(0, P, 2 * s):
                                    col = even // 2
                                    mm = nc.tensor.matmul(
                                        out[even:even + s, h * HALF + col:h * HALF + col + s],
                                        lhs[:, h * P + even:h * P + even + s], columns(rhs(h), col, s),
                                        start=True, stop=True, tile_position=(0, even))
                        mm.then_inc(s_[done], 1)

                    def turn(out, src, done):
                        for h in range(GROUP):
                            mm = nc.tensor.transpose(head(out, h), head(src, h), k.ident[:])
                        mm.then_inc(s_[done], 1)

                    FX, FY = ([front_bank[:, i, g, :] for g in range(NG)] for i in range(2))
                    BX, BY = ([back_bank[:, i, g, :] for g in range(NG)] for i in range(2))

                    def project(i, bank, b, g, done):
                        nc.tensor.matmul(bank, chunk_T[:, b, :], w_qkv[:, i, g * W:(g + 1) * W],
                                         start=True, stop=True).then_inc(s_[done], 1)

                    def project_qk(c, b, g):
                        if g == 0:
                            pe.wait_ge(s_["chunk_ready"], 2 * (B * c + b) + 1)
                        w("qgT_kept", c, b, g, back=1)
                        project(0, FX[g], b, g, "q_proj")
                        w("qT_kept", c, b, g, back=1)
                        project(1, FY[g], b, g, "k_proj")

                    def project_v(c, b):
                        for g in range(NG):
                            w("q_silu", c, b, g)
                            project(2, FX[g], b, g, "v_proj")

                    def turn_k(c, b, g):
                        w("k_silu", c, b, g)
                        w("k_done", c, b, g)
                        turn(FY[g], kk[:, g, :], "kT_turned")

                    def couple(c, b, g):
                        w("kT_kept", c, b, g)
                        each_head(FY[g], lambda h: head(kT[:, b, g, :], h), lambda h: head(kT[:, b, g, :], h), "kk_done")

                    def turn_coupling(c, b, g):
                        w("v_silu", c, b, g)
                        w("raw_done", c, b, g)
                        turn(FX[g], raw[:, g, :], "coup_turned")

                    def turn_q(c, b, g):
                        w("raw_done", c, b, g)
                        w("q_done", c, b, g)
                        turn(FY[g], q[:, g, :], "qT_turned")

                    def turn_qg(c, b, g):
                        w("coup_done", c, b, g)
                        w("qg_done", c, b, g)
                        turn(FX[g], qg[:, g, :], "qgT_turned")

                    def project_out(c, b):
                        w("state_done", c, b, 1)
                        for g in range(NG):
                            w("o_kept", c, b, g)
                            for h in range(GROUP):
                                mm = nc.tensor.matmul(BX[1][:, 0:D], head(out_T[:, g, :], h), w_o[:, g * GROUP + h, :],
                                                      start=(g == 0 and h == 0), stop=(g == NG - 1 and h == GROUP - 1))
                        mm.then_inc(s_["wo_done"], 1)

                    def both(part, ahead):
                        if ahead:
                            for g in range(NG):
                                part(*ahead, g)

                    def front(c, b):
                        both(project_qk, (c, b))
                        project_v(c, b)
                        for part in (turn_k, couple, turn_coupling, turn_q, turn_qg):
                            both(part, (c, b))

                    def back(c, b, ahead):
                        if ahead:
                            project_qk(*ahead, 0)
                        for g in range(NG):
                            w("qT_kept", c, b, g)
                            w("o_kept", c, b, g, back=1)
                            each_head(BY[g], lambda h: head(kT[:, b, g, :], h), lambda h: head(qT[:, b, g, :], h), "kq_done")
                        if ahead:
                            project_qk(*ahead, 1)
                            project_v(*ahead)
                        if not first_item(c, b):
                            project_out(*before(c, b))
                        w("state_done", c, b, 0, back=1)
                        pe.wait_ge(s_["solved"], SOLVE_STEPS * (B * c + b + 1))
                        nc.tensor.transpose(BX[0][:, 0:P], inverse[:].rearrange("p j i -> p (j i)"), k.ident[:]).then_inc(
                            s_["inverse_turned"], 1)
                        for g in range(NG):
                            w("attend_done", c, b, g)
                            w("state_done", c, b, g, back=2)
                            each_head(BY[g], lambda h: head(kT[:, b, g, :], h), lambda h: head(state[:, b, g, :], h), "ks_done")
                        w("base_done", c, b, NG - 1)
                        for g in range(NG):
                            if g == 1 and not first_item(c, b):
                                pe.wait_ge(s_["mixed_done"], B * c + b)
                            turn(BX[g], solve_T[:, g, :], "solve_turned")
                        for lev, s in enumerate(LEVELS):
                            for g in range(NG):
                                if lev == 0:
                                    w("solve_kept", c, b, g)
                                else:
                                    w_level("n_read", c, b, g, lev - 1)
                                    w_level("t_kept", c, b, g, lev - 1, NLEV - 1)
                                merge(BX[g], coupling[:, b, g, :], lambda h: odd(head(solve[:, g, :], h), s), s, "m_done")
                            if lev < 2:
                                both((turn_k, turn_coupling)[lev], ahead)
                            for g in range(NG):
                                w_level("m_read", c, b, g, lev)
                                if lev == 0:
                                    w("v_ready", c, b, g)
                                merge(BY[g], solve_T[:, g, :], lambda h: partial[:, g, h * HALF:(h + 1) * HALF], s, "n_done")
                            if lev == 0:
                                both(couple, ahead)
                            if lev < NLEV - 1:
                                for g in range(NG):
                                    w_level("n_read", c, b, g, lev)
                                    turn(BX[g], solve[:, g, :], "t_turned")
                        for g in range(NG):
                            w_level("n_read", c, b, g, NLEV - 1)
                            each_head(BX[g], lambda h: head(solve[:, g, :], h), lambda h: head(v[:, b, g, :], h), "u_done")
                        both(turn_q, ahead)
                        for g in range(NG):
                            w("qgT_kept", c, b, g)
                            w("u_kept", c, b, g)
                            for h in range(GROUP):
                                nc.tensor.matmul(head(BY[g], h), head(state[:, b, g, :], h), head(qgT[:, b, g, :], h), start=True, stop=False)
                                mm = nc.tensor.matmul(head(BY[g], h), head(update[:, g, :], h), head(attend[:, g, :], h), start=False, stop=True)
                            mm.then_inc(s_["o_done"], 1)
                        for g in range(NG):
                            each_head(BX[g], lambda h: head(kt[:, b, g, :], h), lambda h: head(update[:, g, :], h), "ds_done")
                        both(turn_qg, ahead)

                    over_items(pe, front, back)
                    project_out(CHUNKS - 1, B - 1)

                @block.scalar
                def _(act):
                    w, w_level = waiter(act), level_waiter(act)

                    def keep(src, dst, ready, kept, c, b, g):
                        w(ready, c, b, g)
                        nc.scalar.copy(dst, src).then_inc(s_[kept], 1)

                    def sum_squares(c, b, g):
                        w("q_silu", c, b, g)
                        w("k_silu", c, b, g)
                        w("shifted_done", c, b, g, back=1)
                        for i, t in enumerate((q, kk)):
                            for h in range(GROUP):
                                last = nc.scalar.activation(head(square[:, g, i, :], h), head(t[:, g, :], h), ACT.Square,
                                                            accum_out=squares[:, g, i * GROUP + h:i * GROUP + h + 1])
                        last.then_inc(s_["squares_done"], 1)

                    def silu_qk(c, b):
                        for g in range(NG):
                            w("q_proj", c, b, g)
                            w("qgT_turned", c, b, g, back=1)
                            w("v_done", c, b, g, back=1)
                            nc.scalar.activation(q[:, g, :], front_bank[:, 0, g, :], ACT.Silu).then_inc(s_["q_silu"], 1)
                            w("k_proj", c, b, g)
                            nc.scalar.activation(kk[:, g, :], front_bank[:, 1, g, :], ACT.Silu).then_inc(s_["k_silu"], 1)
                            sum_squares(c, b, g)

                    def silu_v(c, b):
                        for g in range(NG):
                            w("v_proj", c, b, g)
                            w("u_done", c, b, g, back=2)
                            nc.scalar.activation(v[:, b, g, :], front_bank[:, 0, g, :], ACT.Silu).then_inc(s_["v_silu"], 1)

                    def exp_decay(c, b, g):
                        w("masked", c, b, g)
                        w("attend_done", c, b, g, back=2)
                        act.wait_ge(s_["chunk_ready"], 2 * (B * c + b) + 2)
                        for h in range(GROUP):
                            last = nc.scalar.activation(head(decay[:, b, g, :], h), head(masked[:, g, :], h), ACT.Exp,
                                                        bias=cols("neg_summed", b, g)[:, h:h + 1])
                        last.then_inc(s_["decay_done"], 1)

                    def keep_kT(c, b, g):
                        keep(front_bank[:, 1, g, :], kT[:, b, g, :], "kT_turned", "kT_kept", c, b, g)

                    def keep_qT(c, b, g):
                        keep(front_bank[:, 1, g, :], qT[:, b, g, :], "qT_turned", "qT_kept", c, b, g)

                    def keep_qgT(c, b, g):
                        keep(front_bank[:, 0, g, :], qgT[:, b, g, :], "qgT_turned", "qgT_kept", c, b, g)

                    def front(c, b):
                        silu_qk(c, b)
                        silu_v(c, b)
                        for part in (exp_decay, keep_kT, keep_qT, keep_qgT):
                            for g in range(NG):
                                part(c, b, g)

                    def both(part, ahead):
                        if ahead:
                            for g in range(NG):
                                part(*ahead, g)

                    def back(c, b, ahead):
                        if ahead:
                            silu_qk(*ahead)
                            silu_v(*ahead)
                        if ahead:
                            exp_decay(*ahead, 0)
                        for g in range(NG):
                            keep(back_bank[:, 0, g, :], solve[:, g, :], "solve_turned", "solve_kept", c, b, g)
                        if ahead:
                            exp_decay(*ahead, 1)
                        for lev in range(NLEV - 1):
                            if lev == 0:
                                both(keep_kT, ahead)
                            for g in range(NG):
                                w_level("t_turned", c, b, g, lev, NLEV - 1)
                                nc.scalar.copy(solve_T[:, g, :], back_bank[:, 0, g, :]).then_inc(s_["t_kept"], 1)
                        for g in range(NG):
                            keep(back_bank[:, 0, g, :], update[:, g, :], "u_done", "u_kept", c, b, g)
                        both(keep_qT, ahead)
                        for g in range(NG):
                            keep(back_bank[:, 1, g, :], out_T[:, g, :], "o_done", "o_kept", c, b, g)
                        both(keep_qgT, ahead)

                    over_items(act, front, back)

                @block.vector
                def _(dve):
                    w, w_level = waiter(dve), level_waiter(dve)
                    k.link(dve, nc.vector.memset(state[:], 0.0))
                    dve.wait_ge(weights_in, WEIGHTS)

                    def take_tokens(c, b):
                        w("v_proj", c, b, NG - 1, back=2)
                        nc.vector.tensor_scalar(chunk_T[:, b, :], normT[:, bass.ds((b * CHUNKS + c) * P, P)], 0.0, None,
                                                ALU.add).then_inc(s_["chunk_ready"], 1)

                    def take_gates(c, b):
                        w("state_done", c, b, NG - 1, back=2)
                        w("v_done", c, b, NG - 1, back=2)
                        w("decay_done", c, b, NG - 1, back=2)
                        nc.vector.tensor_scalar(chunk_gates[:, b], all_gates[:, b * CHUNKS + c], 0.0, None,
                                                ALU.add).then_inc(s_["chunk_ready"], 1)

                    def weigh(c, b, g):
                        w("decay_done", c, b, g)
                        w("kk_done", c, b, g)
                        nc.vector.tensor_tensor(raw[:, g, :], front_bank[:, 1, g, :], decay[:, b, g, :], ALU.mult).then_inc(s_["raw_done"], 1)

                    def scale_coupling(c, b, g):
                        w("coup_turned", c, b, g)
                        nc.vector.tensor_tensor(heads4(coupling[:, b, g, :]), heads4(front_bank[:, 0, g, :]), wide(cols("neg_beta", b, g)),
                                                ALU.mult).then_inc(s_["coup_done"], 1)

                    def both(part, ahead):
                        if ahead:
                            for g in range(NG):
                                part(*ahead, g)

                    def front(c, b):
                        take_tokens(c, b)
                        take_gates(c, b)
                        for part in (weigh, scale_coupling):
                            both(part, (c, b))
                        take_tokens(c, b + 1)

                    def add_output(c, b):
                        dve.wait_ge(s_["wo_done"], B * c + b + 1)
                        nc.vector.tensor_tensor(mixed[:, b * CHUNKS + c, :], back_bank[:, 0, 1, 0:D], k.n[:, b * CHUNKS + c, :],
                                                ALU.add).then_inc(s_["mixed_done"], 1)

                    def solve_rows(c, b, first, last):
                        done = SOLVE_STEPS * (B * c + b)
                        if first == 1:
                            dve.wait_ge(s_["blocks_in"], 16 * (B * c + b + 1))
                            nc.vector.tensor_copy(inverse[:], delta[:].unsqueeze(1).broadcast_to([P, NB, BASE])).then_inc(s_["solved"], 1)
                            nc.vector.memset(rows_of[:, :, ::BASE + 1], 1.0).then_inc(s_["solved"], 1)
                        for i in range(first, last):
                            dve.wait_ge(s_["solved"], done + 2 * i)
                            nc.vector.tensor_tensor(products[:, :, 0:i + 1], rows_of[:, :, i * BASE:i * BASE + i + 1],
                                                    inverse[:, :, 0:i + 1], ALU.mult).then_inc(s_["solved"], 1)
                            dve.wait_ge(s_["solved"], done + 2 * i + 1)
                            nc.vector.tensor_reduce(inverse[:, :, i], products[:, :, 0:i + 1], AX_X, ALU.add).then_inc(s_["solved"], 1)

                    def back(c, b, ahead):
                        if ahead:
                            take_gates(*ahead)
                        solve_rows(c, b, 1 if first_item(c, b) else EARLY, MIDDLE)
                        for g in range(NG):
                            w("kq_done", c, b, g)
                            nc.vector.tensor_tensor(attend[:, g, :], back_bank[:, 1, g, :], decay[:, b, g, :], ALU.mult).then_inc(s_["attend_done"], 1)
                        solve_rows(c, b, MIDDLE, BASE)
                        if not first_item(c, b):
                            add_output(*before(c, b))
                        dve.wait_ge(s_["inverse_turned"], B * c + b + 1)
                        for g in range(NG):
                            nc.vector.tensor_tensor(
                                solve_T[:, g, :].rearrange("p (h j b) -> p h j b", h=GROUP, b=BASE),
                                back_bank[:, 0, 0, g * GROUP * BASE:(g + 1) * GROUP * BASE].rearrange("p (h b) -> p h b", b=BASE)
                                .unsqueeze(2).broadcast_to([P, GROUP, NB, BASE]),
                                block_of[:].unsqueeze(1).unsqueeze(3).broadcast_to([P, GROUP, NB, BASE]),
                                ALU.mult).then_inc(s_["base_done"], 1)
                        for g in range(NG):
                            w("ks_done", c, b, g)
                            w("v_done", c, b, g)
                            for h in range(GROUP):
                                last = nc.vector.scalar_tensor_tensor(
                                    head(v[:, b, g, :], h), head(back_bank[:, 1, g, :], h), cols("neg_beta_grown", b, g)[:, h:h + 1],
                                    head(v[:, b, g, :], h), ALU.mult, ALU.add)
                            last.then_inc(s_["v_ready"], 1)
                        for lev, s in enumerate(LEVELS):
                            for g in range(NG):
                                w_level("m_done", c, b, g, lev)
                                nc.vector.tensor_tensor(
                                    partial[:, g, :].rearrange("p (h c) -> p h c", h=GROUP),
                                    back_bank[:, 0, g, 0:GROUP * HALF].rearrange("p (h c) -> p h c", h=GROUP),
                                    spread4(level_masks[:, lev, :]), ALU.mult).then_inc(s_["m_read"], 1)
                            for g in range(NG):
                                w_level("n_done", c, b, g, lev)
                                for even in range(0, P, 2 * s) if s >= 32 else (0,):
                                    to = odd(solve[:, g, :], s).rearrange("p (h n) s -> p h n s", h=GROUP)
                                    of = back_bank[:, 1, g, 0:GROUP * HALF].rearrange("p (h n s) -> p h n s", h=GROUP, s=s)
                                    if s >= 32:
                                        to, of = (t[even:even + s, :, even // (2 * s), :] for t in (to, of))
                                    else:
                                        to, of = (t.rearrange("p h n s -> p (h n) s") for t in (to, of))
                                    last = nc.vector.tensor_tensor(to, of, to, ALU.add)
                                last.then_inc(s_["n_read"], 1)
                            if lev < 2:
                                both((weigh, scale_coupling)[lev], ahead)
                        if not (isinstance(c, int) and c == CHUNKS - 1):
                            take_tokens(c + 1, b)
                        for g in range(NG):
                            w("ds_done", c, b, g)
                            for h in range(GROUP):
                                last = nc.vector.scalar_tensor_tensor(
                                    head(state[:, b, g, :], h), head(state[:, b, g, :], h), cols("last", b, g)[:, h:h + 1],
                                    head(back_bank[:, 0, g, :], h), ALU.mult, ALU.add)
                            last.then_inc(s_["state_done"], 1)
                        if ahead:
                            solve_rows(*ahead, 1, EARLY)

                    over_items(dve, front, back)
                    add_output(CHUNKS - 1, B - 1)
                    dve.wait_ge(s_["mixed_done"], B * CHUNKS)

                @block.gpsimd
                def _(pool):
                    w = waiter(pool)
                    TT = nc.gpsimd.tensor_tensor
                    pool.wait_ge(weights_in, WEIGHTS)
                    nc.gpsimd.memset(eps[:], 1e-6).then_inc(s_["eps_set"], 1)
                    pool.wait_ge(s_["eps_set"], 1)
                    def front(c, b):
                        pool.wait_ge(s_["chunk_ready"], 2 * (B * c + b) + 2)
                        pool.wait_ge(s_["rows_in"], 16 * (B * c + b + 1))
                        for g in range(NG):
                            w("decay_done", c, b, g, back=1)
                            TT(heads4(masked[:, g, :]), heads4(sum_rows[:, g, :]), spread4(below[:]), ALU.add).then_inc(s_["masked"], 1)
                        for g in range(NG):
                            w("squares_done", c, b, g)
                            TT(shifted[:, g, :], squares[:, g, :], eps[:], ALU.add).then_inc(s_["shifted_done"], 1)
                            w("shifted_done", c, b, g)
                            TT(inv_norm[:, g, :], shifted[:, g, :], k.half[:, 0:2 * GROUP], ALU.pow).then_inc(s_["norm_done"], 1)
                            w("norm_done", c, b, g)
                            TT(heads4(kk[:, g, :]), heads4(kk[:, g, :]), wide(inv_norm[:, g, GROUP:]), ALU.mult).then_inc(s_["k_done"], 1)
                            TT(heads4(q[:, g, :]), heads4(q[:, g, :]), wide(inv_norm[:, g, 0:GROUP]), ALU.mult).then_inc(s_["q_done"], 1)
                        for g in range(NG):
                            w("q_done", c, b, g)
                            TT(heads4(qg[:, g, :]), heads4(q[:, g, :]), wide(cols("grown", b, g)), ALU.mult).then_inc(s_["qg_done"], 1)
                            w("ds_done", c, b, g, back=2)
                            TT(heads4(kt[:, b, g, :]), heads4(kk[:, g, :]), wide(cols("rest", b, g)), ALU.mult)
                            w("v_silu", c, b, g)
                            TT(heads4(v[:, b, g, :]), heads4(v[:, b, g, :]), wide(cols("beta", b, g)), ALU.mult).then_inc(s_["v_done"], 1)

                    def back(c, b, ahead):
                        if ahead:
                            front(*ahead)

                    over_items(pool, front, back)

        with ExitStack() as ctx:
            b2 = k.sb("f1_b2", [P, D], ctx=ctx)

            def loads(e, par, w1, w2, b1):
                return [(w1, a["L1_attn_W1"]), (w2, a["L1_attn_W2"].rearrange("(f p) d -> p f d", p=P)),
                        (b1, a["L1_attn_b1"].rearrange("(f p) -> p f", p=P)), (b2[:], a["L1_attn_b2"].partition_broadcast(P))]

            weights = HiddenWeights(k, "f1", ctx, loads, 4, 1)
            layer_norm(k, "ln4", mixed, 1e-5, k.n, k.nT, rows["ln2_w"], rows["ln2_b"], prefetch=weights.load_first)

            def finish(ctx, down, down_ready, down_read, weights_in):
                base_done = k.sem("f1_base_done")

                def vector(dve):
                    weights_in(dve, 0, 0)
                    nc.vector.tensor_tensor(mixed[:], mixed[:], b2[:].unsqueeze(1).broadcast_to([P, TILES, D]), ALU.add).then_inc(base_done, 1)
                    dve.wait_ge(base_done, 1)
                    nc.vector.tensor_tensor(k.x[:], k.x[:], mixed[:], ALU.add).then_inc(base_done, 1)
                    dve.wait_ge(base_done, 2)
                    for blk in range(BLOCKS):
                        dve.wait_ge(down_ready, blk + 1)
                        nc.vector.tensor_tensor(k.x[:, 4 * blk:4 * blk + 4, :], down[:, blk % 2, :].rearrange("p (t d) -> p t d", t=4),
                                                k.x[:, 4 * blk:4 * blk + 4, :], ALU.add).then_inc(down_read, 1)
                    dve.wait_ge(down_read, BLOCKS)

                return {"vector": vector}

            feed_forward(k, "f1", weights, ACT.Gelu, True, finish)


def experts(k, a):
    nc = k.nc
    with ExitStack() as ctx:
        router = k.sb("moe_router", [D, EXPERTS], ctx=ctx)
        logits = k.sb("moe_logits", [P, TILES, EXPERTS], ctx=ctx)
        picked = k.sb("moe_picked", [P, TILES, EXPERTS], ctx=ctx)
        gates = k.sb("moe_gates", [P, EXPERTS, TILES], ctx=ctx)
        scaled = k.sb("moe_scaled", [P, TILES, EXPERTS], ctx=ctx)
        gap, expd, total, w_1, w_2 = (k.sb(f"moe_{s}", [P, TILES], ctx=ctx) for s in ("gap", "expd", "total", "w_1", "w_2"))
        w_in, logits_done, gap_done, expd_done = (
            k.sem(f"moe_{s}") for s in ("w_in", "logits_done", "gap_done", "expd_done"))
        hot, top, steps = top_two(k, "moe", ctx, logits)
        b2 = k.sb("moe_b2", [P, 2, D], ctx=ctx)
        gamma = k.sb("moe_gamma", [P, 2, D], ctx=ctx)
        beta = k.sb("moe_beta", [P, 2, D], ctx=ctx)

        def loads(e, par, w1, w2, b1):
            return [(w1, a["L1_ffn_w1"][e]), (w2, a["L1_ffn_w2"][e].rearrange("(f p) d -> p f d", p=P)),
                    (b1, a["L1_ffn_b1"][e].rearrange("(f p) -> p f", p=P)),
                    (b2[:, par], a["L1_ffn_b2"][e].partition_broadcast(P)),
                    (gamma[:, par], a["L1_ffn_gamma"][e].partition_broadcast(P)),
                    (beta[:, par], a["L1_ffn_beta"][e].partition_broadcast(P))]

        weights = HiddenWeights(k, "moe", ctx, loads, 6, EXPERTS)

        def prefetch(sp):
            sp.dma_start(router[:], a["L1_ffn_router_w"]).then_inc(w_in, 16)
            weights.load_first(sp)

        layer_norm(k, "ln5", k.x, 1e-5, k.n, k.nT, prefetch=prefetch)
        def finish(ctx, down, down_ready, down_read, weights_in):
            routed = k.ps("moe_routed", [P, TILES, EXPERTS], ctx=ctx)

            def route(pe):
                pe.wait_ge(w_in, 16)
                for t in range(TILES):
                    mm = nc.tensor.matmul(routed[:, t, :], k.nT[:, t * P:(t + 1) * P], router[:], start=True, stop=True)
                mm.then_inc(logits_done, 1)

            def exponentials(act):
                act.wait_ge(gap_done, 1)
                nc.scalar.activation(expd[:], gap[:], ACT.Exp).then_inc(expd_done, 1)

            def find_gates(dve):
                dve.wait_ge(logits_done, 1)
                k.link(dve, nc.vector.tensor_copy(logits[:], routed[:]))
                steps(dve)
                nc.vector.tensor_tensor(gap[:], top["top2"][:], top["top1"][:], ALU.subtract).then_inc(gap_done, 1)
                dve.wait_ge(expd_done, 1)

                W = [P, TILES, EXPERTS]
                k.link(dve, nc.vector.tensor_scalar(total[:], expd[:], 1.0, None, ALU.add))
                k.link(dve, nc.vector.reciprocal(w_1[:], total[:]))
                k.link(dve, nc.vector.tensor_tensor(w_2[:], w_1[:], expd[:], ALU.mult))
                k.link(dve, nc.vector.tensor_tensor(scaled[:], hot["hot1"][:], w_1[:].unsqueeze(2).broadcast_to(W), ALU.mult))
                k.link(dve, nc.vector.tensor_tensor(picked[:], hot["hot2"][:], w_2[:].unsqueeze(2).broadcast_to(W), ALU.mult))
                k.link(dve, nc.vector.tensor_tensor(gates[:], picked[:].rearrange("p t e -> p e t"),
                                                    scaled[:].rearrange("p t e -> p e t"), ALU.add))

            res = k.sb("moe_res", [P, BLOCKS, 4, D], ctx=ctx)
            stats = k.sb("moe_stats", [P, BLOCKS, 4, 6], ctx=ctx)
            moments = k.sb("moe_moments", [P, BLOCKS, 4, 2], ctx=ctx)
            shifted = k.sb("moe_shifted", [P, BLOCKS, 4], ctx=ctx)
            rstd = k.sb("moe_rstd", [P, BLOCKS, 4], ctx=ctx)
            gate = k.sb("moe_gate", [P, 2, TILES], ctx=ctx)
            res_done, stats_done, moments_done, shifted_done, rstd_done, normed, weighted, offset, gate_done, added = (
                k.sem(f"moe_{s}") for s in ("res_done", "stats_done", "moments_done", "shifted_done", "rstd_done",
                                            "normed", "weighted", "offset", "gate_done", "added"))
            ALL = EXPERTS * BLOCKS

            def over(eng, body):
                for par in range(2):
                    body(0, par)
                with eng.Fori(1, EXPERTS // 2) as r:
                    for par in range(2):
                        body(r, par)

            def vector(dve):
                def normalise(m, blk):
                    dve.wait_ge(rstd_done, m + 1)
                    for t in range(4):
                        last = nc.vector.tensor_scalar(res[:, blk, t, :], res[:, blk, t, :], moments[:, blk, t, 0:1],
                                                       rstd[:, blk, t:t + 1], ALU.subtract, ALU.mult)
                    last.then_inc(normed, 1)

                def add(m, par, blk):
                    dve.wait_ge(offset, m + 1)
                    for t in range(4):
                        i = 4 * blk + t
                        last = nc.vector.scalar_tensor_tensor(k.x[:, i, :], res[:, blk, t, :], gate[:, par, i:i + 1],
                                                              k.x[:, i, :], ALU.mult, ALU.add)
                    last.then_inc(added, 1)

                def take_gate(e, par):
                    nc.vector.tensor_scalar(gate[:, par, :], gates[:, e, :], 0.0, None, ALU.add).then_inc(gate_done, 1)
                    dve.wait_ge(gate_done, e + 1)

                def body(r, par):
                    e = 2 * r + par
                    weights_in(dve, r, par)
                    for blk in range(BLOCKS):
                        m = e * BLOCKS + blk
                        if blk == 0:
                            take_gate(e, par)
                        if not (isinstance(m, int) and m < BLOCKS):
                            dve.wait_ge(added, m - 3)
                        dve.wait_ge(down_ready, m + 1)
                        nc.vector.tensor_tensor(res[:, blk], down[:, blk % 2, :].rearrange("p (t d) -> p t d", t=4),
                                                k.n[:, 4 * blk:4 * blk + 4, :], ALU.add).then_inc(down_read, 1)
                        dve.wait_ge(down_read, m + 1)
                        nc.vector.tensor_tensor(res[:, blk], res[:, blk], b2[:, par].unsqueeze(1).broadcast_to([P, 4, D]),
                                                ALU.add).then_inc(res_done, 1)
                        dve.wait_ge(res_done, m + 1)
                        for t in range(4):
                            last = nc.vector.bn_stats(stats[:, blk, t, :], res[:, blk, t, :])
                        last.then_inc(stats_done, 1)
                        dve.wait_ge(stats_done, m + 1)
                        if not (isinstance(m, int) and m == 0):
                            normalise(m - 1, (blk - 1) % BLOCKS)
                        for t in range(4):
                            last = nc.vector.bn_aggr(moments[:, blk, t, :], stats[:, blk, t, :])
                        last.then_inc(moments_done, 1)
                        dve.wait_ge(moments_done, m + 1)
                        nc.vector.tensor_scalar(shifted[:, blk, :], moments[:, blk, :, 1], 1e-6, None, ALU.add).then_inc(shifted_done, 1)
                        if not (isinstance(m, int) and m < 2):
                            add(m - 2, par if blk >= 2 else 1 - par, (blk - 2) % BLOCKS)

                find_gates(dve)
                over(dve, body)
                normalise(ALL - 1, BLOCKS - 1)
                add(ALL - 2, 1, BLOCKS - 2)
                add(ALL - 1, 1, BLOCKS - 1)
                dve.wait_ge(added, ALL)

            def gpsimd(pool):
                def weigh(m, par, blk):
                    pool.wait_ge(normed, m + 1)
                    nc.gpsimd.tensor_tensor(res[:, blk], res[:, blk], gamma[:, par].unsqueeze(1).broadcast_to([P, 4, D]),
                                            ALU.mult).then_inc(weighted, 1)
                    pool.wait_ge(weighted, m + 1)
                    nc.gpsimd.tensor_tensor(res[:, blk], res[:, blk], beta[:, par].unsqueeze(1).broadcast_to([P, 4, D]),
                                            ALU.add).then_inc(offset, 1)

                def body(r, par):
                    weights_in(pool, r, par)
                    for blk in range(BLOCKS):
                        m = (2 * r + par) * BLOCKS + blk
                        pool.wait_ge(shifted_done, m + 1)
                        nc.gpsimd.tensor_tensor(rstd[:, blk, :], shifted[:, blk, :], k.half[:, 0:4], ALU.pow).then_inc(rstd_done, 1)
                        if not (isinstance(m, int) and m == 0):
                            weigh(m - 1, par if blk else 1 - par, (blk - 1) % BLOCKS)

                over(pool, body)
                weigh(ALL - 1, 1, BLOCKS - 1)

            def used(sp, e):
                sp.wait_ge(added, BLOCKS * (e + 1))

            return {"vector": vector, "gpsimd": gpsimd, "used": used, "tensor_between": route,
                    "scalar_after_first": exponentials}

        feed_forward(k, "moe", weights, ACT.Gelu, True, finish)


def store(k, out):
    with k.nc.Block() as block:
        @block.sync
        def _(sp):
            sp.dma_start(out.rearrange("b (t p) d -> p (b t) d", p=P), k.x[:]).then_inc(k.moved, 16)
            sp.wait_ge(k.moved, 64)


def build_program(nc, a, out):
    with ExitStack() as ctx:
        k = Core(nc, ctx)
        start(k, a)
        attention(k, a)
        feed_forward0(k, a)
        delta_layer(k, a)
        experts(k, a)
        store(k, out)


_INPUTS = [
    "L0_attn_X", "L0_attn_W_qkv", "L0_attn_b_qkv", "L0_attn_W_proj", "L0_attn_b_proj", "L0_ffn_Wg", "L0_ffn_w1",
    "L0_ffn_w2", "L1_attn_Wq", "L1_attn_Wk", "L1_attn_Wv", "L1_attn_Wb", "L1_attn_Wa", "L1_attn_Wo", "L1_attn_ln1_w",
    "L1_attn_ln1_b", "L1_attn_ln2_w", "L1_attn_ln2_b", "L1_attn_W1", "L1_attn_b1", "L1_attn_W2", "L1_attn_b2",
    "L1_ffn_router_w", "L1_ffn_w1", "L1_ffn_b1", "L1_ffn_w2", "L1_ffn_b2", "L1_ffn_gamma", "L1_ffn_beta",
]


def kernel(**inputs):
    from concourse import bacc
    from concourse.bass_utils import run_bass_kernel_spmd

    nc = bacc.Bacc("TRN2", target_bir_lowering=False, num_devices=1)
    arrays = {name: np.ascontiguousarray(inputs[name]) for name in _INPUTS}
    arrays.update(shape_constants())
    a = {name: nc.dram_tensor(f"in_{name}", v.shape, mybir.dt.from_np(v.dtype), kind="ExternalInput").ap()
         for name, v in arrays.items()}
    out = nc.dram_tensor("out", arrays["L0_attn_X"].shape, F32, kind="ExternalOutput").ap()
    build_program(nc, a, out)
    result = run_bass_kernel_spmd(nc, [{f"in_{name}": v for name, v in arrays.items()}], core_ids=[0])
    return result.results[0]["out"]
```
